# Optimizing a Trainium2 kernel written in Bass

```python
import numpy as np
import jax
import jax.numpy as jnp

def _softmax(x, axis=-1):
    return jax.nn.softmax(x, axis=axis)

def _gelu(x):
    return jax.nn.gelu(x, approximate=True)

def _silu(x):
    return jax.nn.silu(x)

def _sigmoid(x):
    return jax.nn.sigmoid(x)

def _layernorm(x, axis=-1, eps=1e-05):
    m = jnp.mean(x, axis=axis, keepdims=True)
    v = jnp.var(x, axis=axis, keepdims=True)
    return (x - m) / jnp.sqrt(v + eps)

def _scatter_add(tgt, idx, src, axis=0):
    return tgt.at[idx].add(src)

def _segment_sum(src, seg, n):
    return jax.ops.segment_sum(src, seg, n)
kernel_name = 'mk_decoder_postln_d2_seqx_r8_4d0361'

def setup_inputs(seed: int=0):
    np.random.seed(seed)
    _w = jnp.asarray

    def _rec_inputs():
        import jax
        import jax.numpy as jnp
        _rk = jax.random.key(seed)
        x = -0.0003929 + 0.9999 * jax.random.normal(jax.random.fold_in(_rk, 1), (4, 256, 128), jnp.float32)
        _lenS = 256 - jax.random.randint(jax.random.fold_in(_rk, 7), (4,), 0, max(1, 256 // 4) + 1, jnp.int32)
        _lenS2 = 256 - jax.random.randint(jax.random.fold_in(_rk, 8), (4,), 0, max(1, 256 // 4) + 1, jnp.int32)
        _ctx_1024P = jax.random.normal(jax.random.fold_in(_rk, 11), (4, 16, 128), jnp.float32)
        _ctx_1024c = jax.random.dirichlet(jax.random.fold_in(_rk, 511), 0.3 * jnp.ones((16,), jnp.float32), (4, 256))
        _ctx_1024t = jnp.einsum('bsk,bkd->bsd', _ctx_1024c, _ctx_1024P)
        _ctx_1024t = _ctx_1024t * jax.lax.rsqrt(jnp.mean(jnp.square(_ctx_1024t)) + 1e-12) * 0.953939
        ctx_1024 = 0.000227908 + 0.99994 * (_ctx_1024t + 0.3 * jax.random.normal(jax.random.fold_in(_rk, 611), (4, 256, 128), jnp.float32))
        return (x, ctx_1024)
    x, ctx_1024 = _rec_inputs()

    def _L0_attn_setup():
        import jax, jax.numpy as jnp
        import numpy as np
        B, S, D = (2, 256, 128)
        H, A = (16, 64)
        key = jax.random.key(seed)
        ks = jax.random.split(key, 9)
        sd = D ** (-0.5)
        so = (H * A) ** (-0.5)
        return {'x': jax.random.normal(ks[0], (B, S, D), dtype=jnp.float32), 'Wq': jax.random.normal(ks[1], (D, H * A), dtype=jnp.float32) * sd, 'bq': jnp.zeros((H * A,), dtype=jnp.float32), 'Wk': jax.random.normal(ks[2], (D, H * A), dtype=jnp.float32) * sd, 'bk': jnp.zeros((H * A,), dtype=jnp.float32), 'Wv': jax.random.normal(ks[3], (D, H * A), dtype=jnp.float32) * sd, 'bv': jnp.zeros((H * A,), dtype=jnp.float32), 'Wo': jax.random.normal(ks[4], (H * A, D), dtype=jnp.float32) * so, 'bo': jnp.zeros((D,), dtype=jnp.float32)}
    _L0_attn_all = _L0_attn_setup()
    _L0_attn_in = {k: v for k, v in _L0_attn_all.items() if k in ('Wq', 'bq', 'Wk', 'bk', 'Wv', 'bv', 'Wo', 'bo')}
    del _L0_attn_all

    def _L0_xattn_setup():
        import jax, jax.numpy as jnp
        import numpy as np
        DIM = 128
        HEADS = 16
        HEAD_DIM = 64
        INNER = HEADS * HEAD_DIM
        SCALE = 8.0
        LN_EPS = 1e-05
        NORM_EPS = 1e-12

        def layer_norm(x, g, b):
            m = jnp.mean(x, axis=-1, keepdims=True)
            v = jnp.mean((x - m) ** 2, axis=-1, keepdims=True)
            return (x - m) * jax.lax.rsqrt(v + LN_EPS) * g + b

        def l2_normalize(x):
            n = jnp.sqrt(jnp.sum(x * x, axis=-1, keepdims=True))
            return x / jnp.maximum(n, NORM_EPS)
        key = jax.random.key(seed)
        ks = jax.random.split(key, 8)
        B, N, T = (4, 512, 32)
        s = 0.02
        return {'x': jax.random.normal(ks[0], (B, N, DIM), jnp.float32), 'context': jax.random.normal(ks[1], (B, T, DIM), jnp.float32), 'Wq': jax.random.normal(ks[2], (DIM, INNER), jnp.float32) * s, 'Wkv': jax.random.normal(ks[3], (DIM, 2 * INNER), jnp.float32) * s, 'Wo': jax.random.normal(ks[4], (INNER, DIM), jnp.float32) * s, 'null_kv': jax.random.normal(ks[5], (2, HEAD_DIM), jnp.float32), 'q_scale': jnp.ones((HEAD_DIM,), jnp.float32), 'k_scale': jnp.ones((HEAD_DIM,), jnp.float32), 'ln_in_g': jnp.ones((DIM,), jnp.float32), 'ln_in_b': jnp.zeros((DIM,), jnp.float32), 'ln_ctx_g': jnp.ones((DIM,), jnp.float32), 'ln_ctx_b': jnp.zeros((DIM,), jnp.float32), 'ln_out_g': jnp.ones((DIM,), jnp.float32), 'ln_out_b': jnp.zeros((DIM,), jnp.float32)}
    _L0_xattn_all = _L0_xattn_setup()
    _L0_xattn_in = {k: v for k, v in _L0_xattn_all.items() if k in ('Wq', 'Wkv', 'Wo', 'null_kv', 'q_scale', 'k_scale', 'ln_in_g', 'ln_in_b', 'ln_ctx_g', 'ln_ctx_b', 'ln_out_g', 'ln_out_b')}
    del _L0_xattn_all

    def _L0_ffn_setup():
        import jax, jax.numpy as jnp
        import numpy as np
        N_HEAD = 16
        NUM_EXPERTS = 8
        TOP_K = 2
        LN_EPS = 1e-05

        def _layernorm(x, g, b):
            mu = jnp.mean(x, axis=-1, keepdims=True)
            var = jnp.mean(jnp.square(x - mu), axis=-1, keepdims=True)
            return (x - mu) * jax.lax.rsqrt(var + LN_EPS) * g + b

        def _attention(h, Wq, bq, Wk, bk, Wv, bv, Wp, bp):
            B, T, D = h.shape
            hd = D // N_HEAD

            def split(z):
                return z.reshape(B, T, N_HEAD, hd).transpose(0, 2, 1, 3)
            q = split(h @ Wq + bq)
            k = split(h @ Wk + bk)
            v = split(h @ Wv + bv)
            att = jnp.einsum('bhqd,bhkd->bhqk', q, k) / jnp.sqrt(jnp.float32(hd))
            causal = jnp.tril(jnp.ones((T, T), bool))
            att = jnp.where(causal, att, -jnp.inf)
            att = jax.nn.softmax(att, axis=-1)
            y = jnp.einsum('bhqk,bhkd->bhqd', att, v)
            y = y.transpose(0, 2, 1, 3).reshape(B, T, D)
            return y @ Wp + bp

        def _token_moe(h, gate_W, gate_b, exp_W1, exp_b1, exp_W2, exp_b2):
            B, T, D = h.shape
            flat = h.reshape(-1, D)
            N = flat.shape[0]
            logits = flat @ gate_W + gate_b
            top_v, top_i = jax.lax.top_k(logits, TOP_K)
            w = jax.nn.softmax(top_v, axis=-1)
            w_full = jnp.zeros((N, NUM_EXPERTS), flat.dtype)
            w_full = w_full.at[jnp.arange(N)[:, None], top_i].add(w)
            out = jnp.zeros_like(flat)
            for e in range(NUM_EXPERTS):
                mid = jax.nn.gelu(flat @ exp_W1[e] + exp_b1[e], approximate=False)
                y_e = mid @ exp_W2[e] + exp_b2[e]
                out = out + w_full[:, e:e + 1] * y_e
            return out.reshape(B, T, D)
        key = jax.random.key(seed)
        B, T, D = (8, 128, 128)
        H = 4 * D
        E = NUM_EXPERTS
        ks = jax.random.split(key, 24)
        s = 0.02
        inp = {'x': jax.random.normal(ks[0], (B, T, D), jnp.float32), 'ln1_g': jnp.ones((D,), jnp.float32), 'ln1_b': jnp.zeros((D,), jnp.float32), 'ln2_g': jnp.ones((D,), jnp.float32), 'ln2_b': jnp.zeros((D,), jnp.float32), 'Wq': jax.random.normal(ks[1], (D, D), jnp.float32) * s, 'bq': jnp.zeros((D,), jnp.float32), 'Wk': jax.random.normal(ks[2], (D, D), jnp.float32) * s, 'bk': jnp.zeros((D,), jnp.float32), 'Wv': jax.random.normal(ks[3], (D, D), jnp.float32) * s, 'bv': jnp.zeros((D,), jnp.float32), 'Wp': jax.random.normal(ks[4], (D, D), jnp.float32) * s, 'bp': jnp.zeros((D,), jnp.float32), 'gate_W': jax.random.normal(ks[5], (D, E), jnp.float32) * s, 'gate_b': jnp.zeros((E,), jnp.float32), 'exp_W1': jax.random.normal(ks[6], (E, D, H), jnp.float32) * s, 'exp_b1': jnp.zeros((E, H), jnp.float32), 'exp_W2': jax.random.normal(ks[7], (E, H, D), jnp.float32) * s, 'exp_b2': jnp.zeros((E, D), jnp.float32)}
        return inp
    _L0_ffn_all = _L0_ffn_setup()
    _L0_ffn_in = {k: v for k, v in _L0_ffn_all.items() if k in ('ln1_g', 'ln1_b', 'ln2_g', 'ln2_b', 'Wq', 'bq', 'Wk', 'bk', 'Wv', 'bv', 'Wp', 'bp', 'gate_W', 'gate_b', 'exp_W1', 'exp_b1', 'exp_W2', 'exp_b2')}
    del _L0_ffn_all

    def _L1_attn_setup():
        import jax, jax.numpy as jnp
        import numpy as np
        HEADS = 16
        D_MODEL = 128
        D_K = D_MODEL // HEADS
        SEQ = 256
        BSZ = 2

        def softmax_one(x, axis):
            x = x - jnp.max(x, axis=axis, keepdims=True)
            ex = jnp.exp(x)
            return ex / (1.0 + jnp.sum(ex, axis=axis, keepdims=True))
        key = jax.random.key(seed)
        ks = jax.random.split(key, 7)
        s = 1.0 / np.sqrt(D_MODEL)
        return {'x': jax.random.normal(ks[0], (SEQ, BSZ, D_MODEL), dtype=jnp.float32), 'Wq': jax.random.normal(ks[1], (D_MODEL, D_MODEL), dtype=jnp.float32) * s, 'bq': jnp.zeros((D_MODEL,), dtype=jnp.float32), 'Wk': jax.random.normal(ks[2], (D_MODEL, D_MODEL), dtype=jnp.float32) * s, 'bk': jnp.zeros((D_MODEL,), dtype=jnp.float32), 'Wv': jax.random.normal(ks[3], (D_MODEL, D_MODEL), dtype=jnp.float32) * s, 'bv': jnp.zeros((D_MODEL,), dtype=jnp.float32)}
    _L1_attn_all = _L1_attn_setup()
    _L1_attn_in = {k: v for k, v in _L1_attn_all.items() if k in ('Wq', 'bq', 'Wk', 'bk', 'Wv', 'bv')}
    del _L1_attn_all

    def _L1_xattn_setup():
        import jax, jax.numpy as jnp
        import numpy as np
        E, T, H, F = (16, 256, 128, 512)
        key = jax.random.key(seed)
        kx, k1, k2, k3 = jax.random.split(key, 4)
        s = 1.0 / np.sqrt(H)
        return {'x': jax.random.normal(kx, (E, T, H), dtype=jnp.float32), 'w1': jax.random.normal(k1, (E, F, H), dtype=jnp.float32) * s, 'v1': jax.random.normal(k2, (E, F, H), dtype=jnp.float32) * s, 'w2': jax.random.normal(k3, (E, F, H), dtype=jnp.float32) * s}
    _L1_xattn_all = _L1_xattn_setup()
    _L1_xattn_in = {k: v for k, v in _L1_xattn_all.items() if k in ()}
    del _L1_xattn_all

    def _L1_ffn_setup():
        import jax, jax.numpy as jnp
        import numpy as np
        D_IN, D_HID = (128, 512)

        def _ternary(key, shape):
            return jax.random.randint(key, shape, -1, 2).astype(jnp.float32)

        def _tlin(x, w, s):
            return jnp.einsum('bsi,oi->bso', x, w) * s
        key = jax.random.key(seed)
        ks = jax.random.split(key, 12)
        inv = lambda fan: 1.0 / np.sqrt(fan).astype(np.float32)
        return {'x': jax.random.normal(ks[0], (4, 256, D_IN), dtype=jnp.float32), 'w1_w': _ternary(ks[1], (D_HID, D_IN)), 'w1_s': jax.random.uniform(ks[2], (D_HID,), dtype=jnp.float32) * inv(D_IN), 'w2_w': _ternary(ks[3], (D_HID, D_IN)), 'w2_s': jax.random.uniform(ks[4], (D_HID,), dtype=jnp.float32) * inv(D_IN), 'h1_w': _ternary(ks[5], (D_HID, D_HID)), 'h1_s': jax.random.uniform(ks[6], (D_HID,), dtype=jnp.float32) * inv(D_HID), 'h2_w': _ternary(ks[7], (D_HID, D_HID)), 'h2_s': jax.random.uniform(ks[8], (D_HID,), dtype=jnp.float32) * inv(D_HID), 'w3_w': _ternary(ks[9], (D_IN, D_HID)), 'w3_s': jax.random.uniform(ks[10], (D_IN,), dtype=jnp.float32) * inv(D_HID)}
    _L1_ffn_all = _L1_ffn_setup()
    _L1_ffn_in = {k: v for k, v in _L1_ffn_all.items() if k in ('w1_w', 'w1_s', 'w2_w', 'w2_s', 'h1_w', 'h1_s', 'h2_w', 'h2_s', 'w3_w', 'w3_s')}
    del _L1_ffn_all
    return {'x': x, 'ctx_1024': ctx_1024, 'L0_attn_Wq': _L0_attn_in['Wq'], 'L0_attn_bq': _L0_attn_in['bq'], 'L0_attn_Wk': _L0_attn_in['Wk'], 'L0_attn_bk': _L0_attn_in['bk'], 'L0_attn_Wv': _L0_attn_in['Wv'], 'L0_attn_bv': _L0_attn_in['bv'], 'L0_attn_Wo': _L0_attn_in['Wo'], 'L0_attn_bo': _L0_attn_in['bo'], 'L0_xattn_Wq': _L0_xattn_in['Wq'], 'L0_xattn_Wkv': _L0_xattn_in['Wkv'], 'L0_xattn_Wo': _L0_xattn_in['Wo'], 'L0_xattn_null_kv': _L0_xattn_in['null_kv'], 'L0_xattn_q_scale': _L0_xattn_in['q_scale'], 'L0_xattn_k_scale': _L0_xattn_in['k_scale'], 'L0_xattn_ln_in_g': _L0_xattn_in['ln_in_g'], 'L0_xattn_ln_in_b': _L0_xattn_in['ln_in_b'], 'L0_xattn_ln_ctx_g': _L0_xattn_in['ln_ctx_g'], 'L0_xattn_ln_ctx_b': _L0_xattn_in['ln_ctx_b'], 'L0_xattn_ln_out_g': _L0_xattn_in['ln_out_g'], 'L0_xattn_ln_out_b': _L0_xattn_in['ln_out_b'], 'L0_ffn_ln1_g': _L0_ffn_in['ln1_g'], 'L0_ffn_ln1_b': _L0_ffn_in['ln1_b'], 'L0_ffn_ln2_g': _L0_ffn_in['ln2_g'], 'L0_ffn_ln2_b': _L0_ffn_in['ln2_b'], 'L0_ffn_Wq': _L0_ffn_in['Wq'], 'L0_ffn_bq': _L0_ffn_in['bq'], 'L0_ffn_Wk': _L0_ffn_in['Wk'], 'L0_ffn_bk': _L0_ffn_in['bk'], 'L0_ffn_Wv': _L0_ffn_in['Wv'], 'L0_ffn_bv': _L0_ffn_in['bv'], 'L0_ffn_Wp': _L0_ffn_in['Wp'], 'L0_ffn_bp': _L0_ffn_in['bp'], 'L0_ffn_gate_W': _L0_ffn_in['gate_W'], 'L0_ffn_gate_b': _L0_ffn_in['gate_b'], 'L0_ffn_exp_W1': _L0_ffn_in['exp_W1'], 'L0_ffn_exp_b1': _L0_ffn_in['exp_b1'], 'L0_ffn_exp_W2': _L0_ffn_in['exp_W2'], 'L0_ffn_exp_b2': _L0_ffn_in['exp_b2'], 'L1_attn_Wq': _L1_attn_in['Wq'], 'L1_attn_bq': _L1_attn_in['bq'], 'L1_attn_Wk': _L1_attn_in['Wk'], 'L1_attn_bk': _L1_attn_in['bk'], 'L1_attn_Wv': _L1_attn_in['Wv'], 'L1_attn_bv': _L1_attn_in['bv'], 'L1_ffn_w1_w': _L1_ffn_in['w1_w'], 'L1_ffn_w1_s': _L1_ffn_in['w1_s'], 'L1_ffn_w2_w': _L1_ffn_in['w2_w'], 'L1_ffn_w2_s': _L1_ffn_in['w2_s'], 'L1_ffn_h1_w': _L1_ffn_in['h1_w'], 'L1_ffn_h1_s': _L1_ffn_in['h1_s'], 'L1_ffn_h2_w': _L1_ffn_in['h2_w'], 'L1_ffn_h2_s': _L1_ffn_in['h2_s'], 'L1_ffn_w3_w': _L1_ffn_in['w3_w'], 'L1_ffn_w3_s': _L1_ffn_in['w3_s']}

def reference(x, ctx_1024, L0_attn_Wq, L0_attn_bq, L0_attn_Wk, L0_attn_bk, L0_attn_Wv, L0_attn_bv, L0_attn_Wo, L0_attn_bo, L0_xattn_Wq, L0_xattn_Wkv, L0_xattn_Wo, L0_xattn_null_kv, L0_xattn_q_scale, L0_xattn_k_scale, L0_xattn_ln_in_g, L0_xattn_ln_in_b, L0_xattn_ln_ctx_g, L0_xattn_ln_ctx_b, L0_xattn_ln_out_g, L0_xattn_ln_out_b, L0_ffn_ln1_g, L0_ffn_ln1_b, L0_ffn_ln2_g, L0_ffn_ln2_b, L0_ffn_Wq, L0_ffn_bq, L0_ffn_Wk, L0_ffn_bk, L0_ffn_Wv, L0_ffn_bv, L0_ffn_Wp, L0_ffn_bp, L0_ffn_gate_W, L0_ffn_gate_b, L0_ffn_exp_W1, L0_ffn_exp_b1, L0_ffn_exp_W2, L0_ffn_exp_b2, L1_attn_Wq, L1_attn_bq, L1_attn_Wk, L1_attn_bk, L1_attn_Wv, L1_attn_bv, L1_ffn_w1_w, L1_ffn_w1_s, L1_ffn_w2_w, L1_ffn_w2_s, L1_ffn_h1_w, L1_ffn_h1_s, L1_ffn_h2_w, L1_ffn_h2_s, L1_ffn_w3_w, L1_ffn_w3_s):
    import jax
    import jax.numpy as jnp

    def _L0_attn_ref(x, Wq, bq, Wk, bk, Wv, bv, Wo, bo):
        import jax, jax.numpy as jnp
        import numpy as np
        B, S, D = (2, 256, 128)
        H, A = (16, 64)
        b, s, _ = x.shape
        q = (x @ Wq + bq).reshape(b, s, H, A)
        k = (x @ Wk + bk).reshape(b, s, H, A)
        v = (x @ Wv + bv).reshape(b, s, H, A)
        scores = jnp.einsum('bqhd,bkhd->bhqk', q, k) / jnp.sqrt(jnp.float32(A))
        weights = jax.nn.softmax(scores, axis=-1)
        attended = jnp.einsum('bhqk,bkhd->bqhd', weights, v).reshape(b, s, H * A)
        return attended @ Wo + bo

    def _L0_xattn_ref(x, context, Wq, Wkv, Wo, null_kv, q_scale, k_scale, ln_in_g, ln_in_b, ln_ctx_g, ln_ctx_b, ln_out_g, ln_out_b):
        import jax, jax.numpy as jnp
        import numpy as np
        DIM = 128
        HEADS = 16
        HEAD_DIM = 64
        INNER = HEADS * HEAD_DIM
        SCALE = 8.0
        LN_EPS = 1e-05
        NORM_EPS = 1e-12

        def layer_norm(x, g, b):
            m = jnp.mean(x, axis=-1, keepdims=True)
            v = jnp.mean((x - m) ** 2, axis=-1, keepdims=True)
            return (x - m) * jax.lax.rsqrt(v + LN_EPS) * g + b

        def l2_normalize(x):
            n = jnp.sqrt(jnp.sum(x * x, axis=-1, keepdims=True))
            return x / jnp.maximum(n, NORM_EPS)
        B, N, _ = x.shape
        T = context.shape[1]
        xn = layer_norm(x, ln_in_g, ln_in_b)
        cn = layer_norm(context, ln_ctx_g, ln_ctx_b)
        q = xn @ Wq
        kv = cn @ Wkv
        k, v = jnp.split(kv, 2, axis=-1)

        def split_heads(t):
            b, s, _ = t.shape
            return t.reshape(b, s, HEADS, HEAD_DIM).transpose(0, 2, 1, 3)
        q, k, v = (split_heads(q), split_heads(k), split_heads(v))
        nk = jnp.broadcast_to(null_kv[0], (B, HEADS, 1, HEAD_DIM))
        nv = jnp.broadcast_to(null_kv[1], (B, HEADS, 1, HEAD_DIM))
        k = jnp.concatenate([k, nk], axis=2)
        v = jnp.concatenate([v, nv], axis=2)
        q = l2_normalize(q) * q_scale
        k = l2_normalize(k) * k_scale
        scores = jnp.einsum('bhid,bhkd->bhik', q, k) * SCALE
        attn = jax.nn.softmax(scores, axis=-1)
        out = jnp.einsum('bhik,bhkd->bhid', attn, v)
        out = out.transpose(0, 2, 1, 3).reshape(B, N, INNER)
        out = out @ Wo
        return layer_norm(out, ln_out_g, ln_out_b)

    def _L0_ffn_ref(x, ln1_g, ln1_b, ln2_g, ln2_b, Wq, bq, Wk, bk, Wv, bv, Wp, bp, gate_W, gate_b, exp_W1, exp_b1, exp_W2, exp_b2):
        import jax, jax.numpy as jnp
        import numpy as np
        N_HEAD = 16
        NUM_EXPERTS = 8
        TOP_K = 2
        LN_EPS = 1e-05

        def _layernorm(x, g, b):
            mu = jnp.mean(x, axis=-1, keepdims=True)
            var = jnp.mean(jnp.square(x - mu), axis=-1, keepdims=True)
            return (x - mu) * jax.lax.rsqrt(var + LN_EPS) * g + b

        def _attention(h, Wq, bq, Wk, bk, Wv, bv, Wp, bp):
            B, T, D = h.shape
            hd = D // N_HEAD

            def split(z):
                return z.reshape(B, T, N_HEAD, hd).transpose(0, 2, 1, 3)
            q = split(h @ Wq + bq)
            k = split(h @ Wk + bk)
            v = split(h @ Wv + bv)
            att = jnp.einsum('bhqd,bhkd->bhqk', q, k) / jnp.sqrt(jnp.float32(hd))
            causal = jnp.tril(jnp.ones((T, T), bool))
            att = jnp.where(causal, att, -jnp.inf)
            att = jax.nn.softmax(att, axis=-1)
            y = jnp.einsum('bhqk,bhkd->bhqd', att, v)
            y = y.transpose(0, 2, 1, 3).reshape(B, T, D)
            return y @ Wp + bp

        def _token_moe(h, gate_W, gate_b, exp_W1, exp_b1, exp_W2, exp_b2):
            B, T, D = h.shape
            flat = h.reshape(-1, D)
            N = flat.shape[0]
            logits = flat @ gate_W + gate_b
            top_v, top_i = jax.lax.top_k(logits, TOP_K)
            w = jax.nn.softmax(top_v, axis=-1)
            w_full = jnp.zeros((N, NUM_EXPERTS), flat.dtype)
            w_full = w_full.at[jnp.arange(N)[:, None], top_i].add(w)
            out = jnp.zeros_like(flat)
            for e in range(NUM_EXPERTS):
                mid = jax.nn.gelu(flat @ exp_W1[e] + exp_b1[e], approximate=False)
                y_e = mid @ exp_W2[e] + exp_b2[e]
                out = out + w_full[:, e:e + 1] * y_e
            return out.reshape(B, T, D)
        x = x + _attention(_layernorm(x, ln1_g, ln1_b), Wq, bq, Wk, bk, Wv, bv, Wp, bp)
        x = x + _token_moe(_layernorm(x, ln2_g, ln2_b), gate_W, gate_b, exp_W1, exp_b1, exp_W2, exp_b2)
        return x

    def _L1_attn_ref(x, Wq, bq, Wk, bk, Wv, bv):
        import jax, jax.numpy as jnp
        import numpy as np
        HEADS = 16
        D_MODEL = 128
        D_K = D_MODEL // HEADS
        SEQ = 256
        BSZ = 2

        def softmax_one(x, axis):
            x = x - jnp.max(x, axis=axis, keepdims=True)
            ex = jnp.exp(x)
            return ex / (1.0 + jnp.sum(ex, axis=axis, keepdims=True))
        S, B, D = x.shape
        q = (x @ Wq.T + bq).reshape(S, B, HEADS, D_K)
        k = (x @ Wk.T + bk).reshape(S, B, HEADS, D_K)
        v = (x @ Wv.T + bv).reshape(S, B, HEADS, D_K)
        scores = jnp.einsum('ibhd,jbhd->ijbh', q, k) / np.sqrt(D_K).astype(np.float32)
        causal = jnp.tril(jnp.ones((S, S), dtype=bool))[:, :, None, None]
        scores = jnp.where(causal, scores, -jnp.inf)
        attn = softmax_one(scores, axis=1)
        out = jnp.einsum('ijbh,jbhd->ibhd', attn, v)
        return out.reshape(S, B, D)

    def _L1_xattn_ref(x, w1, v1, w2):
        import jax, jax.numpy as jnp
        import numpy as np
        E, T, H, F = (16, 256, 128, 512)
        x1 = jnp.einsum('eth,efh->etf', x, w1)
        x2 = jnp.einsum('eth,efh->etf', x, v1)
        h = jax.nn.gelu(x1, approximate=True) * x2
        return jnp.einsum('etf,efh->eth', h, w2)

    def _L1_ffn_ref(x, w1_w, w1_s, w2_w, w2_s, h1_w, h1_s, h2_w, h2_s, w3_w, w3_s):
        import jax, jax.numpy as jnp
        import numpy as np
        D_IN, D_HID = (128, 512)

        def _ternary(key, shape):
            return jax.random.randint(key, shape, -1, 2).astype(jnp.float32)

        def _tlin(x, w, s):
            return jnp.einsum('bsi,oi->bso', x, w) * s
        h = jax.nn.silu(_tlin(x, w1_w, w1_s)) * _tlin(x, w2_w, w2_s)
        h = jax.nn.gelu(_tlin(h, h1_w, h1_s), approximate=False)
        h = jax.nn.gelu(_tlin(h, h2_w, h2_s), approximate=False)
        return _tlin(h, w3_w, w3_s)
    x = _layernorm(x + _L0_attn_ref(x, L0_attn_Wq, L0_attn_bq, L0_attn_Wk, L0_attn_bk, L0_attn_Wv, L0_attn_bv, L0_attn_Wo, L0_attn_bo), axis=-1)
    x = _layernorm(x + _L0_xattn_ref(x, ctx_1024, L0_xattn_Wq, L0_xattn_Wkv, L0_xattn_Wo, L0_xattn_null_kv, L0_xattn_q_scale, L0_xattn_k_scale, L0_xattn_ln_in_g, L0_xattn_ln_in_b, L0_xattn_ln_ctx_g, L0_xattn_ln_ctx_b, L0_xattn_ln_out_g, L0_xattn_ln_out_b), axis=-1)
    x = _layernorm(x + _L0_ffn_ref(x, L0_ffn_ln1_g, L0_ffn_ln1_b, L0_ffn_ln2_g, L0_ffn_ln2_b, L0_ffn_Wq, L0_ffn_bq, L0_ffn_Wk, L0_ffn_bk, L0_ffn_Wv, L0_ffn_bv, L0_ffn_Wp, L0_ffn_bp, L0_ffn_gate_W, L0_ffn_gate_b, L0_ffn_exp_W1, L0_ffn_exp_b1, L0_ffn_exp_W2, L0_ffn_exp_b2), axis=-1)
    x = _layernorm(x + _L1_attn_ref(x, L1_attn_Wq, L1_attn_bq, L1_attn_Wk, L1_attn_bk, L1_attn_Wv, L1_attn_bv), axis=-1)
    x = _layernorm(x + _L1_xattn_ref(x, ctx_1024, ctx_1024, ctx_1024), axis=-1)
    x = _layernorm(x + _L1_ffn_ref(x, L1_ffn_w1_w, L1_ffn_w1_s, L1_ffn_w2_w, L1_ffn_w2_s, L1_ffn_h1_w, L1_ffn_h1_s, L1_ffn_h2_w, L1_ffn_h2_s, L1_ffn_w3_w, L1_ffn_w3_s), axis=-1)
    return x

_drawn_inputs = setup_inputs


def setup_inputs(seed=0):
    import zlib

    import numpy as np

    out = dict(_drawn_inputs(seed))
    spreads = {'L0_attn_bq': (0.0, 0.8),
     'L0_attn_bk': (0.0, 0.8),
     'L0_attn_bv': (0.0, 0.1),
     'L0_attn_bo': (0.0, 0.1),
     'L0_xattn_q_scale': (1.0, 0.2),
     'L0_xattn_k_scale': (1.0, 0.2),
     'L0_xattn_ln_in_g': (1.0, 0.2),
     'L0_xattn_ln_in_b': (0.0, 0.364),
     'L0_xattn_ln_ctx_g': (1.0, 0.2),
     'L0_xattn_ln_ctx_b': (0.0, 0.1),
     'L0_xattn_ln_out_g': (1.0, 0.2),
     'L0_xattn_ln_out_b': (0.0, 0.1),
     'L0_ffn_ln1_g': (1.0, 0.6),
     'L0_ffn_ln1_b': (0.0, 0.8),
     'L0_ffn_ln2_g': (1.0, 0.6),
     'L0_ffn_ln2_b': (0.0, 0.8),
     'L0_ffn_bq': (0.0, 0.8),
     'L0_ffn_bk': (0.0, 0.8),
     'L0_ffn_bv': (0.0, 0.643),
     'L0_ffn_bp': (0.0, 0.1),
     'L0_ffn_gate_b': (0.0, 0.315),
     'L0_ffn_exp_b1': (0.0, 0.8),
     'L0_ffn_exp_b2': (0.0, 0.1),
     'L1_attn_bq': (0.0, 0.501),
     'L1_attn_bk': (0.0, 0.8),
     'L1_attn_bv': (0.0, 0.1)}
    factors = {'L0_ffn_Wq': 8.0,
     'L0_ffn_Wk': 8.0,
     'L0_ffn_Wv': 2.695,
     'L0_ffn_exp_W1': 3.321,
     'L0_ffn_exp_W2': 2.725,
     'L1_ffn_w1_w': 8.0,
     'L1_ffn_w1_s': 8.0,
     'L1_ffn_w2_w': 8.0,
     'L1_ffn_w2_s': 8.0,
     'L1_ffn_h1_w': 8.0,
     'L1_ffn_h1_s': 8.0,
     'L1_ffn_h2_w': 8.0,
     'L1_ffn_h2_s': 8.0,
     'L1_ffn_w3_w': 8.0,
     'L1_ffn_w3_s': 8.0}
    for name, (base, spread) in spreads.items():
        noise = np.random.default_rng([zlib.crc32(name.encode()), seed]).standard_normal(out[name].shape)
        drawn = base * np.exp(spread * noise) if base else spread * noise
        out[name] = jnp.asarray(drawn.astype(out[name].dtype))
    for name, factor in factors.items():
        out[name] = (out[name] * factor).astype(out[name].dtype)
    return out
```

```python
from contextlib import ExitStack

import concourse.bass as bass
from concourse import mybir

F32 = mybir.dt.float32
BF16 = mybir.dt.bfloat16
I32 = mybir.dt.int32
U32 = mybir.dt.uint32
ALU = mybir.AluOpType
ACT = mybir.ActivationFunctionType
AX = mybir.AxisListType

B, S, D = 4, 256, 128
P = 128
NC = B * S // P
CB = S // P
H, A = 16, 64
PAIRS = H // 2
HD = D // H
E, FF = 8, 4 * D
FC = FF // P
LN_EPS = 1e-5
NORM_EPS = 1e-12
MASKED = 1e30

COLS = {}
for _n, _w in [("A_bq", PAIRS), ("A_bk", PAIRS), ("A_bv", PAIRS), ("B_qs", 1), ("B_ks", 1), ("B_nv", 1),
               ("B_in_g", 1), ("B_in_b", 1), ("B_ctx_g", 1), ("B_ctx_b", 1), ("C_ln1_g", 1), ("C_ln1_b", 1),
               ("C_ln2_g", 1), ("C_ln2_b", 1), ("C_bq", 1), ("C_bk", 1), ("C_bv", 4),
               ("F_s1", FC), ("F_s2", FC), ("F_h1", FC), ("F_h2", FC)]:
    COLS[_n] = (sum(w for _, w in COLS.values()), _w)
NCOLS = sum(w for _, w in COLS.values())
ROWS = {}
for _n, _w in [("A_bo", D), ("B_out_g", D), ("B_out_b", D), ("B_nk", A), ("B_qsr", A), ("B_ksr", A), ("C_bp", D), ("M_gb", E), ("D_b", 3 * D),
               ("F_s3", D)]:
    ROWS[_n] = (sum(w for _, w in ROWS.values()), _w)
NROWS = sum(w for _, w in ROWS.values())


class Chain:

    def __init__(self, eng, sem, base=0):
        self.eng, self.sem, self.base, self.n = eng, sem, base, 0

    def done(self, ins):
        self.n += 1
        ins.then_inc(self.sem, 1)

    def step(self, ins):
        self.done(ins)
        self.eng.wait_ge(self.sem, self.base + self.n)


def decoder(nc, t, upto=99):
    ctx = ExitStack()
    with ctx:
        wide = ctx.enter_context(ExitStack())
        scope = [ctx]

        def sb(name, shape, dt=F32):
            return scope[0].enter_context(nc.sbuf_tensor(name, shape, dt))

        def sem(name):
            return ctx.enter_context(nc.semaphore(name))

        x_res = sb("x_res", [P, NC, D])
        ctx_tok = sb("ctx_tok", [P, NC, D])
        cols = sb("cols", [P, NCOLS])
        rows = sb("rows", [P, NROWS])
        ident = sb("ident", [P, P])
        ones = sb("ones", [P, P])
        CONSTS = [-0.5, LN_EPS, float(A) ** 0.5, -float(A) ** 0.5]
        const = sb("const", [P, len(CONSTS), 64])
        half = const[:, 0, :]

        def col(name, i=0, lo=0, hi=P):
            o = COLS[name][0] + i
            return cols[lo:hi, o:o + 1]

        def row(name):
            o, w = ROWS[name]
            return rows[:, o:o + w]

        st = sb("st", [P, NC, 6])
        mv = sb("mv", [P, NC, 2])
        scrap = sb("scrap", [P, 1])
        veps = sb("veps", [P, NC])
        rstd = sb("rstd", [P, NC])
        xn_all, cn_all = sb("xn_all", [P, NC * P]), sb("cn_all", [P, NC * P])
        hat = sb("hat", [P, NC, D])
        y = sb("y", [P, CB, D])
        y2 = sb("y2", [P, CB, D])

        scope[0] = wide
        A_wq = sb("A_wq", [P, H * A])
        A_wk = sb("A_wk", [P, H * A])
        A_wv = sb("A_wv", [P, H * A])
        A_wo = sb("A_wo", [P, PAIRS, D])
        B_wq = sb("B_wq", [P, H * A])
        B_wkv = sb("B_wkv", [P, 2 * H * A])
        B_wo = sb("B_wo", [P, PAIRS, D])

        xT = sb("xT", [P, S])
        vtok = sb("vtok", [P, CB, H * A])
        qT = [sb(f"qT{i}", [P, S]) for i in range(2)]
        kz = [sb(f"kz{i}", [P, 2, S]) for i in range(2)]
        probs = [sb(f"probs{i}", [P, CB, 2, S]) for i in range(4)]
        probsT = [sb(f"probsT{i}", [P, 2, CB, S]) for i in range(2)]
        oT = sb("oT", [P, PAIRS, S])
        negmax = sb("negmax", [P, PAIRS, CB, 2])
        sums = sb("sums", [P, PAIRS, CB, 2])
        rsum = sb("rsum", [P, PAIRS, CB, 2])

        loadA, loadAw = sem("loadA"), sem("loadAw")
        loadB, loadC = sem("loadB"), sem("loadC")

        def ln_stats(ch, src, n):
            for i in range(n):
                ins = nc.vector.bn_stats(st[:, i, :], src(i))
            ch.step(ins)
            nc.vector.memset(scrap[:, :], 0.0)
            for i in range(n):
                ins = nc.vector.bn_aggr(mv[:, i, :], st[:, i, :])
            return ins

        def ln_power(ch, n):
            ch.step(nc.gpsimd.tensor_tensor(veps[:, 0:n], mv[:, 0:n, 1], const[:, 1, 0:n], ALU.add))
            return nc.gpsimd.tensor_tensor(rstd[:, 0:n], veps[:, 0:n], half[:, 0:n], ALU.pow)

        cst = sem("cst")
        pch = sem("pch")
        dch0 = sem("dch0")
        with nc.Block() as block:
            @block.sync
            def _(sp):
                sp.dma_start(cols[:, :], t["cols"]).then_inc(loadA, 16)
                sp.dma_start(A_wv[:, :], t["A_wv"]).then_inc(loadAw, 16)
                sp.dma_start(A_wk[:, :], t["A_wk"]).then_inc(loadAw, 16)
                sp.dma_start(x_res[:, :, :], t["x"].rearrange("(j p) d -> p j d", p=P)).then_inc(loadA, 16)
                sp.dma_start(B_wkv[:, :], t["B_wkv"]).then_inc(loadB, 16)
                sp.dma_start(B_wo[:, :, :], t["B_wo"].rearrange("(a p) d -> p a d", p=P)).then_inc(loadB, 16)

            @block.scalar
            def _(act):
                act.dma_start(A_wq[:, :], t["A_wq"]).then_inc(loadAw, 16)
                act.dma_start(A_wo[:, :, :], t["A_wo"].rearrange("(a p) d -> p a d", p=P)).then_inc(loadAw, 16)
                act.dma_start(rows[:, :], t["rows"].partition_broadcast(P)).then_inc(loadA, 16)
                act.dma_start(ctx_tok[:, :, :], t["ctx"].rearrange("(j p) d -> p j d", p=P)).then_inc(loadB, 16)
                act.dma_start(B_wq[:, :], t["B_wq"]).then_inc(loadB, 16)

            @block.gpsimd
            def _(pool):
                nc.gpsimd.memset(ident[:, :], 0.0).then_inc(cst, 1)
                pool.wait_ge(cst, 1)
                nc.gpsimd.affine_select(out=ident[:, :], in_=ident[:, :], compare_op=ALU.not_equal, fill=1.0,
                                        base=0, pattern=[[-1, P]], channel_multiplier=1).then_inc(cst, 1)
                nc.gpsimd.memset(ones[:, :], 1.0).then_inc(cst, 1)
                for k, value in enumerate(CONSTS):
                    nc.gpsimd.memset(const[:, k, :], value).then_inc(cst, 1)

            @block.vector
            def _(dve):
                for i in range(2):
                    nc.vector.memset(kz[i][:, :, :], 0.0)
                ch = Chain(dve, dch0)
                dve.wait_ge(loadA, 48)
                ch.done(nc.vector.tensor_scalar(cols[:, 0:PAIRS], cols[:, 0:PAIRS], -float(A) ** -0.5, None, ALU.mult))
                bo = row("A_bo").unsqueeze(1).broadcast_to([P, NC, D])
                ch.done(nc.vector.tensor_tensor(x_res[:, :, :], x_res[:, :, :], bo, ALU.add))

        U = CB * PAIRS
        TL = 3
        RING = 4
        ring = ctx.enter_context(nc.psum_tensor("ring", [P, RING, 512], F32))
        ptb = ctx.enter_context(nc.psum_tensor("ptb", [P, CB, 512], F32))
        obank = ctx.enter_context(nc.psum_tensor("obank", [P, 512], F32))
        misc = ctx.enter_context(nc.psum_tensor("misc", [P, 512], F32))

        def wide_attention(name, cross):
            xT_ready = sem(name + "_xT_ready")
            ring_done = sem(name + "_ring_done")
            ring_free = sem(name + "_ring_free")
            misc_done, misc_free = sem(name + "_misc_done"), sem(name + "_misc_free")
            max_ready, exp_done = sem(name + "_max_ready"), sem(name + "_exp_done")
            norm_done = sem(name + "_norm_done")
            pt_done, pt_free = sem(name + "_pt_done"), sem(name + "_pt_free")
            o_done, o_free = sem(name + "_o_done"), sem(name + "_o_free")
            stat, rstd_ready = sem(name + "_stat"), sem(name + "_rstd")
            dve_steps, pool_steps = sem(name + "_dve_steps"), sem(name + "_pool_steps")
            khat_ready, rq_ready, pnt_ready = sem(name + "_khat_ready"), sem(name + "_rq_ready"), sem(name + "_pnt_ready")
            qsum_ready, ksum_ready, krn_ready = sem(name + "_qsum"), sem(name + "_ksum"), sem(name + "_krn")
            PRE = 3 * RING if cross else RING
            NR = PRE + U
            M0 = 1 if cross else 0
            NM = M0 + PAIRS + (2 if cross else 1)
            DSTEPS = 5 * PAIRS + 9 if cross else PAIRS + 2
            PSTEPS = 4 if cross else 1
            lnum = 2 if cross else 1
            wq, wo = (B_wq, B_wo) if cross else (A_wq, A_wo)

            with nc.Block() as block:
                @block.sync
                def _(sp):
                    if not cross:
                        with sp.Fori(0, B) as b:
                            sp.wait_ge(misc_done, NM * b + 1)
                            sp.dma_start(xT[:, :], t["xT"][b]).then_inc(xT_ready, 16)

                @block.tensor
                def _(pe):
                    pe.sem_inc(pt_done, 4)
                    pe.sem_inc(o_done, 2)
                    pe.sem_inc(misc_done, 1)
                    pe.wait_ge(loadB if cross else loadAw, 64)
                    with pe.Fori(0, B) as b:
                        def ring_bank(r):
                            pe.wait_ge(ring_free, NR * b + r + 1)
                            return ring[:, r % RING, :]

                        def misc_bank(m):
                            pe.wait_ge(misc_free, NM * b + m + 1)
                            return misc

                        pe.wait_ge(xT_ready, 2 * b + 2 if cross else 16 * b + 16)
                        for r in range(2 * RING if cross else RING):
                            c, hf = r % RING // 2, r % 2
                            src = cT if cross else xT
                            w = (B_wkv[:, r // 4 * H * A + hf * 512:][:, 0:512]) if cross else A_wv[:, hf * 512:(hf + 1) * 512]
                            nc.tensor.matmul(ring_bank(r), src[:, c * P:(c + 1) * P], w, start=True, stop=True).then_inc(ring_done, 1)
                        if cross:
                            for r in range(2 * RING, PRE):
                                bank = ring_bank(r)
                                for k in range(2):
                                    p = 2 * (r - 2 * RING) + k
                                    ins = nc.tensor.matmul(bank[:, k * S:(k + 1) * S], wq[:, p * P:(p + 1) * P], xT[:, :],
                                                           start=True, stop=True)
                                ins.then_inc(ring_done, 1)
                            misc_bank(0)
                            pe.wait_ge(ring_free, NR * b + PRE + RING)
                            for p in range(PAIRS):
                                for c in range(CB):
                                    nc.tensor.matmul(misc[:, 4 * p + 2 * c:4 * p + 2 * c + 2], qsq[:, p, c * P:(c + 1) * P], blk[:, :],
                                                     start=True, stop=True)
                            for c in range(CB):
                                nullc = misc[:, 4 * PAIRS:8 * PAIRS].rearrange("p (a c h) -> p a c h", c=CB, h=2)[:, :, c, :]
                                ins = nc.tensor.matmul(nullc, xT[:, c * P:(c + 1) * P], wnull[:, :].rearrange("p (a h) -> p a h", h=2),
                                                       start=True, stop=True)
                            ins.then_inc(misc_done, 1)
                        for p in range(PAIRS + TL + 1):
                            if p < PAIRS:
                                misc_bank(M0 + p)
                                if cross:
                                    if p == 0:
                                        pe.wait_ge(khat_ready, b + 1)
                                    for c in range(CB):
                                        ins = nc.tensor.transpose(misc[:, c * P:(c + 1) * P], ktok[:, c, p * P:(p + 1) * P], ident[:, :])
                                else:
                                    nc.tensor.matmul(misc[:, 0:S], wq[:, p * P:(p + 1) * P], xT[:, :], start=True, stop=True)
                                    ins = nc.tensor.matmul(misc[:, S:2 * S], A_wk[:, p * P:(p + 1) * P], xT[:, :], start=True, stop=True)
                                ins.then_inc(misc_done, 1)
                            if 1 <= p <= PAIRS:
                                pe.wait_ge(misc_free, NM * b + M0 + p + 1)
                                q = qT_all[:, p - 1, :] if cross else qT[(p - 1) % 2][:, :]
                                for c in range(CB):
                                    bank = ring_bank(PRE + CB * (p - 1) + c)
                                    nc.tensor.matmul(bank, q[:, c * P:(c + 1) * P], kz[(p - 1) % 2][:, :, :], start=True,
                                                     stop=True).then_inc(ring_done, 1)
                            if TL <= p < PAIRS + TL:
                                q = p - TL
                                pe.wait_ge(norm_done, PAIRS * b + q + 1)
                                pe.wait_ge(pt_free, PAIRS * b + q + 1)
                                for c in range(CB):
                                    for k in range(4):
                                        ins = nc.tensor.transpose(ptb[:, c, k * P:(k + 1) * P],
                                                                  probs[q % 4][:, c, k // 2, (k % 2) * P:(k % 2 + 1) * P], ident[:, :])
                                ins.then_inc(pt_done, 1)
                            if TL < p:
                                q = p - TL - 1
                                pe.wait_ge(pt_free, PAIRS * b + q + 2)
                                pe.wait_ge(o_free, PAIRS * b + q + 1)
                                for kc in range(CB):
                                    for h in range(2):
                                        ins = nc.tensor.matmul(obank[h * A:(h + 1) * A, 0:S],
                                                               vtok[:, kc, (2 * q + h) * A:(2 * q + h + 1) * A],
                                                               probsT[q % 2][:, h, kc, :], start=kc == 0, stop=kc == CB - 1)
                                ins.then_inc(o_done, 1)
                        if cross:
                            misc_bank(M0 + PAIRS)
                            pe.wait_ge(pnt_ready, b + 1)
                            for c in range(CB):
                                ins = nc.tensor.transpose(misc[0:H, c * P:(c + 1) * P], pnt[:, c, :], ident[:, :])
                            ins.then_inc(misc_done, 1)
                        pe.wait_ge(o_free, PAIRS * b + PAIRS + 1)
                        misc_bank(NM - 1)
                        for c in range(CB):
                            for q in range(PAIRS):
                                ins = nc.tensor.matmul(misc[:, c * D:(c + 1) * D], oT[:, q, c * P:(c + 1) * P], wo[:, q, :],
                                                       start=q == 0, stop=q == PAIRS - 1 and not cross)
                            if cross:
                                ins = nc.tensor.matmul(misc[:, c * D:(c + 1) * D], pnT[:, c * P:(c + 1) * P], nvwo[:, :],
                                                       start=False, stop=True)
                        ins.then_inc(misc_done, 1)

                @block.scalar
                def _(act):
                    act.sem_inc(ring_free, RING)
                    act.sem_inc(misc_free, 1)
                    with act.Fori(0, B) as b:
                        act.wait_ge(o_done, PAIRS * b + 2)
                        for r in range(2 * RING if cross else RING):
                            c, hf = r % RING // 2, r % 2
                            dst = ktok if cross and r < RING else vtok
                            act.wait_ge(ring_done, NR * b + r + 1)
                            nc.scalar.copy(dst[:, c, hf * 512:(hf + 1) * 512], ring[:, r % RING, :]).then_inc(ring_free, 1)
                        if cross:
                            for r in range(2 * RING, PRE):
                                p = 2 * (r - 2 * RING)
                                act.wait_ge(ring_done, NR * b + r + 1)
                                src = ring[:, r % RING, :].rearrange("p (a s) -> p a s", a=2)
                                nc.scalar.activation(qsq[:, p:p + 2, :], src, ACT.Square)
                                nc.scalar.activation(qT_all[:, p:p + 2, :], src, ACT.Copy, scale=nqk[:, 0:1]).then_inc(ring_free, 1)
                            act.wait_ge(misc_done, NM * b + 2)
                            nc.scalar.copy(ssn[:, :], misc[:, 0:8 * PAIRS]).then_inc(misc_free, 1)
                        for p in range(PAIRS + 1):
                            if p < PAIRS:
                                act.wait_ge(misc_done, NM * b + M0 + p + 2)
                                if p >= 2:
                                    act.wait_ge(ring_done, NR * b + PRE + CB * (p - 1))
                                lo, hi = slice(0, A), slice(A, P)
                                if cross:
                                    nc.scalar.copy(kz[p % 2][lo, 0, :], misc[lo, 0:S])
                                    ins = nc.scalar.copy(kz[p % 2][hi, 1, :], misc[hi, 0:S])
                                else:
                                    nc.scalar.activation(qT[p % 2][:, :], misc[:, 0:S], ACT.Identity, bias=col("A_bq", p), scale=-float(A) ** -0.5)
                                    nc.scalar.activation(kz[p % 2][lo, 0, :], misc[lo, S:2 * S], ACT.Identity, bias=col("A_bk", p, 0, A))
                                    ins = nc.scalar.activation(kz[p % 2][hi, 1, :], misc[hi, S:2 * S], ACT.Identity, bias=col("A_bk", p, A, P))
                                ins.then_inc(misc_free, 1)
                            if 1 <= p:
                                q = p - 1
                                act.wait_ge(max_ready, PAIRS * b + q + 1)
                                act.wait_ge(pt_done, PAIRS * b + q + 1)
                                for c in range(CB):
                                    for h in range(2):
                                        if cross and c + h == 0:
                                            nc.scalar.activation(pn[:, q, :, :], pnarg[:, q, :, :], ACT.Exp)
                                        ins = nc.scalar.activation(
                                            probs[q % 4][:, c, h, :], ring[:, (PRE + CB * q + c) % RING, h * S:(h + 1) * S], ACT.Exp,
                                            bias=negmax[:, q, c, h:h + 1], scale=nrq[:, q, c, h:h + 1] if cross else -1.0,
                                            accum_out=sums[:, q, c, h:h + 1])
                                    ins.then_inc(ring_free, 1)
                        if cross:
                            act.wait_ge(misc_done, NM * b + M0 + PAIRS + 2)
                            nc.scalar.copy(pnT[:, :], misc[0:H, 0:S]).then_inc(misc_free, 1)

                @block.vector
                def _(dve):
                    dve.sem_inc(pt_free, 1)
                    dve.sem_inc(o_free, 1)
                    with dve.Fori(0, B) as b:
                        ch = Chain(dve, dve_steps, DSTEPS * b)
                        if cross:
                            k3 = ktok[:, :, :].rearrange("p c (h a) -> p (c h) a", a=A)
                            dve.wait_ge(ring_free, NR * b + RING + RING)
                            ch.step(nc.vector.tensor_tensor(ksq[:, :, :], k3, k3, ALU.mult))
                            ch.step(nc.vector.tensor_reduce(kss[:, :], ksq[:, :, :], AX.X, ALU.add))
                            nc.vector.tensor_scalar(kss[:, :], kss[:, :], NORM_EPS ** 2, None, ALU.max).then_inc(ksum_ready, 1)
                            dve.wait_ge(krn_ready, b + 1)
                            nc.vector.tensor_tensor(k3, k3, krn[:, :].unsqueeze(2).broadcast_to([P, CB * H, A]), ALU.mult).then_inc(khat_ready, 1)
                            dve.wait_ge(misc_free, NM * b + 2)
                            nc.vector.tensor_scalar(rqt[:, :], ssn[:, 0:4 * PAIRS], NORM_EPS ** 2, None, ALU.max).then_inc(qsum_ready, 1)
                            dve.wait_ge(rq_ready, b + 1)
                        for p in range(1, PAIRS + TL + 2):
                            if TL < p <= PAIRS + TL:
                                q = p - TL - 1
                                dve.wait_ge(o_done, PAIRS * b + q + 1)
                                dve.wait_ge(pt_done, PAIRS * b + q + 1 + 4)
                                nc.vector.tensor_copy(probsT[q % 2][:, :, :, :].rearrange("p h k (c q) -> p c (h k) q", c=CB),
                                                      ptb[:, :, :].rearrange("p c (k q) -> p c k q", q=P)).then_inc(pt_free, 1)
                            if TL + 2 <= p:
                                q = p - TL - 2
                                dve.wait_ge(o_done, PAIRS * b + q + 1 + 2)
                                if q == 0:
                                    dve.wait_ge(misc_done, NM * b + 1)
                                if cross:
                                    nc.vector.tensor_copy(oT[:, q, :], obank[:, 0:S]).then_inc(o_free, 1)
                                else:
                                    nc.vector.tensor_scalar(oT[:, q, :], obank[:, 0:S], col("A_bv", q), None, ALU.add).then_inc(o_free, 1)
                            if 2 <= p <= PAIRS + 1:
                                q = p - 2
                                dve.wait_ge(ring_free, NR * b + PRE + CB * (q + 1) + RING)
                                if cross:
                                    ch.step(nc.vector.tensor_tensor(sums[:, q, :, :], sums[:, q, :, :], pn[:, q, :, :], ALU.add))
                                ch.step(nc.vector.reciprocal(rsum[:, q, :, :], sums[:, q, :, :]))
                                for c in range(CB):
                                    for h in range(2):
                                        pr = probs[q % 4][:, c, h, :]
                                        ins = nc.vector.tensor_scalar(pr, pr, rsum[:, q, c, h:h + 1], None, ALU.mult)
                                ins.then_inc(norm_done, 1)
                            if p <= PAIRS:
                                q = p - 1
                                dve.wait_ge(ring_done, NR * b + PRE + CB * (q + 1))
                                r = (PRE + CB * q) % RING
                                ins = nc.vector.tensor_reduce((mins if cross else negmax)[:, q, :, :],
                                                              ring[:, r:r + CB, :].rearrange("p c (h k) -> p c h k", h=2), AX.X, ALU.min)
                                if cross:
                                    ch.step(ins)
                                    ch.step(nc.vector.tensor_tensor(mins[:, q, :, :], mins[:, q, :, :], nulls(q), ALU.min))
                                    ch.step(nc.vector.tensor_tensor(negmax[:, q, :, :], mins[:, q, :, :], prq[:, q, :, :], ALU.mult))
                                    ins = nc.vector.tensor_tensor(pnarg[:, q, :, :], negmax[:, q, :, :], snr[:, q, :, :], ALU.add)
                                ins.then_inc(max_ready, 1)
                        if cross:
                            ins = nc.vector.tensor_tensor(pnt[:, :, :].rearrange("p c (a h) -> p a c h", h=2), pn[:, :, :, :], rsum[:, :, :, :], ALU.mult)
                            ins.then_inc(pnt_ready, 1)
                        dve.wait_ge(misc_done, NM * b + NM + 1)
                        out = misc[:, 0:CB * D].rearrange("p (c d) -> p c d", c=CB)
                        xb = x_res[:, bass.ds(CB * b, CB), :]
                        if cross:
                            nc.vector.tensor_copy(y[:, :, :], out).then_inc(misc_free, 1)
                            dve.wait_ge(misc_free, NM * b + NM + 1)
                            ln_stats(ch, lambda i: y[:, i, :], CB).then_inc(stat, 1)
                            dve.wait_ge(rstd_ready, lnum * b + 1)
                            for c in range(CB):
                                ins = nc.vector.tensor_scalar(y2[:, c, :], y[:, c, :], mv[:, c, 0:1], rstd[:, c:c + 1], ALU.subtract, ALU.mult)
                            ch.step(ins)
                            ch.step(nc.vector.tensor_tensor(y2[:, :, :], y2[:, :, :], row("B_out_g").unsqueeze(1).broadcast_to([P, CB, D]), ALU.mult))
                            ch.step(nc.vector.tensor_tensor(y2[:, :, :], y2[:, :, :], row("B_out_b").unsqueeze(1).broadcast_to([P, CB, D]), ALU.add))
                            ch.step(nc.vector.tensor_tensor(y[:, :, :], y2[:, :, :], xb, ALU.add))
                        else:
                            nc.vector.tensor_tensor(y[:, :, :], out, xb, ALU.add).then_inc(misc_free, 1)
                            dve.wait_ge(misc_free, NM * b + NM + 1)
                        ln_stats(ch, lambda i: y[:, i, :], CB).then_inc(stat, 1)
                        dve.wait_ge(rstd_ready, lnum * b + lnum)
                        for c in range(CB):
                            ins = nc.vector.tensor_scalar(x_res[:, bass.ds(CB * b + c, 1), :], y[:, c:c + 1, :], mv[:, c, 0:1], rstd[:, c:c + 1],
                                                          ALU.subtract, ALU.mult)
                        ch.step(ins)
                        assert ch.n == DSTEPS

                @block.gpsimd
                def _(pool):
                    with pool.Fori(0, B) as b:
                        ch = Chain(pool, pool_steps, PSTEPS * b)
                        if cross:
                            pool.wait_ge(misc_done, NM * b + 1)
                            nc.gpsimd.tensor_copy(cT[:, :], cn_all[:, bass.ds(S * b, S)]).then_inc(xT_ready, 1)
                            nc.gpsimd.tensor_copy(xT[:, :], xn_all[:, bass.ds(S * b, S)]).then_inc(xT_ready, 1)
                            pool.wait_ge(ksum_ready, b + 1)
                            nc.gpsimd.tensor_tensor(krn[:, :], kss[:, :], half[:, 0:CB * H], ALU.pow).then_inc(krn_ready, 1)
                            pool.wait_ge(qsum_ready, b + 1)
                            rq4 = lambda x: x[:, :, :, :].rearrange("p a c h -> p (a c h)")
                            ch.step(nc.gpsimd.tensor_tensor(rqt[:, :], rqt[:, :], half[:, 0:4 * PAIRS], ALU.pow))
                            nc.gpsimd.tensor_tensor(rq4(prq), rqt[:, :], const[:, 2, 0:4 * PAIRS], ALU.mult)
                            ch.step(nc.gpsimd.tensor_tensor(rq4(nrq), rqt[:, :], const[:, 3, 0:4 * PAIRS], ALU.mult))
                            nc.gpsimd.tensor_tensor(rq4(snr), rq4(nrq), ssn[:, 4 * PAIRS:], ALU.mult).then_inc(rq_ready, 1)
                        for i in range(lnum):
                            pool.wait_ge(stat, lnum * b + i + 1)
                            ln_power(ch, CB).then_inc(rstd_ready, 1)
                        assert ch.n == PSTEPS

        wide_attention("A", False)

        cT = sb("cT", [P, S])
        ktok = sb("ktok", [P, CB, H * A])
        ksq = sb("ksq", [P, CB * H, A])
        kss, krn = sb("kss", [P, CB * H]), sb("krn", [P, CB * H])
        qT_all, qsq = sb("qT_all", [P, PAIRS, S]), sb("qsq", [P, PAIRS, S])
        ssn = sb("ssn", [P, 8 * PAIRS])
        rqt = sb("rqt", [P, 4 * PAIRS])
        small = lambda n: sb(n, [P, PAIRS, CB, 2])
        prq, nrq, snr, mins, pn, pnarg = map(small, ["prq", "nrq", "snr", "mins", "pn", "pnarg"])
        pnt, pnT = sb("pnt", [P, CB, H]), sb("pnT", [H, S])
        nqk, wnull, blk = sb("nqk", [P, 1]), sb("wnull", [P, H]), sb("blk", [P, 2])
        nvz, nvwo = sb("nvz", [P, PAIRS, H]), sb("nvwo", [H, D])
        nulls = lambda q: ssn[:, 4 * PAIRS + 4 * q:4 * PAIRS + 4 * q + 4].rearrange("p (c h) -> p c h", c=CB)
        nkr, nks, wtmp = sb("nkr", [P, A]), sb("nks", [P, 1]), sb("wtmp", [P, H, A])

        cbq = cols[:, COLS["C_bq"][0]:COLS["C_bq"][0] + 1]

        def normalise_all(name, src, dst, gain, bias):
            stat, rs, hat_ready, tr_done = sem(name + "_stat"), sem(name + "_rstd"), sem(name + "_hat"), sem(name + "_tr")
            steps, psteps = sem(name + "_steps"), sem(name + "_psteps")
            with nc.Block() as block:
                @block.vector
                def _(dve):
                    ch = Chain(dve, steps)
                    ln_stats(ch, lambda i: src[:, i, :], NC).then_inc(stat, 1)
                    dve.wait_ge(rs, 1)
                    for i in range(NC):
                        nc.vector.tensor_scalar(hat[:, i, :], src[:, i, :], mv[:, i, 0:1], rstd[:, i:i + 1], ALU.subtract, ALU.mult)\
                            .then_inc(hat_ready, 1)
                    for g in range(NC // 4):
                        dve.wait_ge(tr_done, g + 1)
                        nc.vector.tensor_scalar(dst[:, g * 512:(g + 1) * 512], ring[:, g, :], gain, bias, ALU.mult, ALU.add)

                @block.gpsimd
                def _(pool):
                    pool.wait_ge(stat, 1)
                    ln_power(Chain(pool, psteps), NC).then_inc(rs, 1)

                @block.tensor
                def _(pe):
                    for i in range(NC):
                        pe.wait_ge(hat_ready, i + 1)
                        ins = nc.tensor.transpose(ring[:, i // 4, (i % 4) * P:(i % 4 + 1) * P], hat[:, i, :], ident[:, :])
                        if i % 4 == 3:
                            ins.then_inc(tr_done, 1)

        if upto > 0:
            b_steps, b_pow, b_ss, b_nv, b_blk = sem("b_steps"), sem("b_pow"), sem("b_ss"), sem("b_nv"), sem("b_blk")
            with nc.Block() as block:
                @block.vector
                def _(dve):
                    ch = Chain(dve, b_steps)
                    dve.wait_ge(loadB, 64)
                    nc.vector.scalar_tensor_tensor(nqk[:, :], col("B_qs"), -1.0, col("B_ks"), ALU.mult, ALU.mult)
                    ch.step(nc.vector.tensor_tensor(nkr[:, :], row("B_nk"), row("B_nk"), ALU.mult))
                    nc.vector.tensor_reduce(nks[:, :], nkr[:, :], AX.X, ALU.add).then_inc(b_ss, 1)
                    nc.vector.memset(nvz[:, :, :], 0.0)
                    ch.step(nc.vector.memset(blk[:, :], 0.0))
                    nc.vector.memset(blk[0:A, 0:1], 1.0)
                    nc.vector.memset(blk[A:P, 1:2], 1.0)
                    flat = nvz[:, :, :].rearrange("p a h -> p (a h)")
                    n = (PAIRS - 1) * (H + 2) + 1
                    nc.vector.tensor_copy(flat[0:A, 0:n:H + 2], col("B_nv", 0, 0, A).broadcast_to([A, PAIRS]))
                    nc.vector.tensor_copy(flat[A:P, 1:1 + n:H + 2], col("B_nv", 0, A, P).broadcast_to([A, PAIRS])).then_inc(b_blk, 1)
                    dve.wait_ge(b_pow, 1)
                    ch.step(nc.vector.tensor_scalar(nkr[:, :], row("B_nk"), nks[:, 0:1], -1.0, ALU.mult, ALU.mult))
                    ch.step(nc.vector.tensor_tensor(nkr[:, :], nkr[:, :], row("B_qsr"), ALU.mult))
                    ch.step(nc.vector.tensor_tensor(nkr[:, :], nkr[:, :], row("B_ksr"), ALU.mult))
                    ch.step(nc.vector.tensor_tensor(wtmp[:, :, :], B_wq[:, :].rearrange("p (h a) -> p h a", a=A),
                                                    nkr[:, :].unsqueeze(1).broadcast_to([P, H, A]), ALU.mult))
                    nc.vector.tensor_reduce(wnull[:, :], wtmp[:, :, :], AX.X, ALU.add)
                    dve.wait_ge(b_nv, 1)
                    nc.vector.tensor_copy(nvwo[:, :], misc[0:H, 0:D])

                @block.gpsimd
                def _(pool):
                    pool.wait_ge(b_ss, 1)
                    nc.gpsimd.tensor_scalar(nks[:, :], nks[:, :], NORM_EPS ** 2, None, ALU.max).then_inc(b_ss, 1)
                    pool.wait_ge(b_ss, 2)
                    nc.gpsimd.tensor_tensor(nks[:, :], nks[:, :], half[:, 0:1], ALU.pow).then_inc(b_pow, 1)

                @block.tensor
                def _(pe):
                    pe.wait_ge(loadB, 64)
                    pe.wait_ge(b_blk, 1)
                    for q in range(PAIRS):
                        ins = nc.tensor.matmul(misc[0:H, 0:D], nvz[:, q, :], B_wo[:, q, :], start=q == 0, stop=q == PAIRS - 1)
                    ins.then_inc(b_nv, 1)
            normalise_all("Bc", ctx_tok, cn_all, col("B_ctx_g"), col("B_ctx_b"))
            normalise_all("Bx", x_res, xn_all, col("B_in_g"), col("B_in_b"))
            wide_attention("B", True)
        wide.close()
        scope[0] = ctx

        if upto > 1:
            G = 4
            NG = H // G
            TU = 3
            loadCw, loadM, loadF = sem("loadCw"), sem("loadM"), sem("loadF")
            C_wq, C_wk, C_wv = sb("C_wq", [P, D]), sb("C_wk", [P, D]), sb("C_wv", [P, D])
            C_wp = sb("C_wp", [P, NG, D])
            M_gw, M_b2 = sb("M_gw", [P, E]), sb("M_b2", [E, D])
            D_w = sb("D_w", [P, 3 * D])
            F_w1, F_w2 = sb("F_w1", [P, FF]), sb("F_w2", [P, FF])
            F_h1, F_h2, F_w3 = sb("F_h1", [P, FC, FF]), sb("F_h2", [P, FC, FF]), sb("F_w3", [P, FC, D])
            ctxT = sb("ctxT", [P, B, S])
            x1 = sb("x1", [P, NC, D])
            narrow = ctx.enter_context(ExitStack())
            scope[0] = narrow
            qTc, kTc = sb("qTc", [P, NC * P]), sb("kTc", [P, NC * P])
            vpad = sb("vpad", [P, NC, H, 32])
            qTb, kTb, vb = sb("qTb", [P, S]), sb("kTb", [P, S]), sb("vb", [P, CB, H * 32])
            kzn = sb("kzn", [P, H, S])
            hmask = sb("hmask", [P, H])
            causal, identb = sb("causal", [P, P], BF16), sb("identb", [P, P], BF16)
            pr = sb("pr", [P, NG, TU, 512])
            prT = [sb(f"prT{i}", [P, G, CB, S]) for i in range(2)]
            oTn = sb("oTn", [P, NG, S])
            nmax, nsum, nrs = sb("nmax", [P, NG, 8]), sb("nsum", [P, NG, 8]), sb("nrs", [P, NG, 8])

            c_cst, c_done, c_evac, c_vz = sem("c_cst"), sem("c_done"), sem("c_evac"), sem("c_vz")
            normalise_all("Cx", x_res, xn_all, col("C_ln1_g"), col("C_ln1_b"))
            with nc.Block() as block:
                @block.sync
                def _(sp):
                    for dst, src in [(C_wq[:, :], t["C_wq"]), (C_wk[:, :], t["C_wk"]), (C_wv[:, :], t["C_wv"]),
                                     (C_wp[:, :, :], t["C_wp"].rearrange("g p d -> p g d"))]:
                        sp.dma_start(dst, src).then_inc(loadCw, 16)
                    for dst, src in [(M_gw[:, :], t["M_gw"]), (M_b2[:, :], t["M_b2"])]:
                        sp.dma_start(dst, src).then_inc(loadM, 16)
                    for dst, src in [(D_w[:, :], t["D_w"]), (ctxT[:, :, :], t["ctxT"].rearrange("b p s -> p b s")),
                                     (F_w1[:, :], t["F_w1"]), (F_w2[:, :], t["F_w2"]), (F_h1[:, :, :], t["F_h1"]),
                                     (F_h2[:, :, :], t["F_h2"]), (F_w3[:, :, :], t["F_w3"])]:
                        sp.dma_start(dst, src).then_inc(loadF, 16)

                @block.gpsimd
                def _(pool):
                    nc.gpsimd.memset(hmask[:, :], 1.0).then_inc(c_cst, 1)
                    nc.gpsimd.memset(causal[:, :], 0.0).then_inc(c_cst, 1)
                    nc.gpsimd.tensor_copy(identb[:, :], ident[:, :])
                    pool.wait_ge(c_cst, 2)
                    nc.gpsimd.affine_select(out=hmask[:, :], in_=hmask[:, :], compare_op=ALU.is_ge, fill=0.0,
                                            base=0, pattern=[[-HD, H]], channel_multiplier=1).then_inc(c_cst, 1)
                    pool.wait_ge(c_cst, 3)
                    nc.gpsimd.affine_select(out=hmask[:, :], in_=hmask[:, :], compare_op=ALU.is_ge, fill=0.0,
                                            base=HD - 1, pattern=[[HD, H]], channel_multiplier=-1)
                    nc.gpsimd.affine_select(out=causal[:, :], in_=causal[:, :], compare_op=ALU.is_ge, fill=MASKED,
                                            base=0, pattern=[[-1, P]], channel_multiplier=1)

                @block.tensor
                def _(pe):
                    pe.wait_ge(loadCw, 64)
                    for i, w in enumerate([C_wq, C_wk]):
                        for g in range(2):
                            nc.tensor.matmul(ring[:, 2 * i + g, :], w[:, :], xn_all[:, g * 512:(g + 1) * 512], start=True, stop=True)\
                                .then_inc(c_done, 1)
                    for j in range(NC):
                        ins = nc.tensor.matmul(ptb[:, j // 4, (j % 4) * P:(j % 4 + 1) * P], xn_all[:, j * P:(j + 1) * P], C_wv[:, :],
                                               start=True, stop=True)
                        if j % 4 == 3:
                            ins.then_inc(c_done, 1)

                @block.scalar
                def _(act):
                    for i, (dst, bias) in enumerate([(qTc, cbq), (kTc, col("C_bk"))]):
                        for g in range(2):
                            act.wait_ge(c_done, 2 * i + g + 1)
                            if i == 0:
                                act.wait_ge(c_vz, 1)
                            nc.scalar.activation(dst[:, g * 512:(g + 1) * 512], ring[:, 2 * i + g, :], ACT.Identity, bias=bias,
                                                 scale=-float(HD) ** -0.5 if i == 0 else 1.0)

                @block.vector
                def _(dve):
                    nc.vector.tensor_scalar(cbq, col("C_bq"), -float(HD) ** -0.5, None, ALU.mult).then_inc(c_vz, 1)
                    nc.vector.memset(vpad[:, :, :, :], 0.0).then_inc(c_vz, 1)
                    dve.wait_ge(c_vz, 2)
                    for g in range(2):
                        dve.wait_ge(c_done, 5 + g)
                        nc.vector.tensor_copy(vpad[:, 4 * g:4 * g + 4, :, 0:HD], ptb[:, g, :].rearrange("p (c h d) -> p c h d", c=4, d=HD))

            NU = NG * TU
            s_done, s_free, max_ready = sem("C_s_done"), sem("C_s_free"), sem("C_max_ready")
            norm_done, pt_done, pt_free = sem("C_norm_done"), sem("C_pt_done"), sem("C_pt_free")
            o_done, o_free, out_done, out_free = sem("C_o_done"), sem("C_o_free"), sem("C_out_done"), sem("C_out_free")
            in_ready, kz_ready, c_steps = sem("C_in_ready"), sem("C_kz_ready"), sem("C_steps")
            CSTEPS = NG + 2
            tiles = [(range(0, 4), 0), (range(0, 2), 1), (range(2, 4), 1)]
            stat_of = [0, 4, 6]
            with nc.Block() as block:
                @block.gpsimd
                def _(pool):
                    with pool.Fori(0, B) as b:
                        pool.wait_ge(out_done, b + 1)
                        nc.gpsimd.tensor_copy(kTb[:, :], kTc[:, bass.ds(S * b, S)]).then_inc(in_ready, 1)
                        nc.gpsimd.tensor_copy(qTb[:, :], qTc[:, bass.ds(S * b, S)]).then_inc(in_ready, 1)
                        nc.gpsimd.tensor_copy(vb[:, :, :], vpad[:, bass.ds(CB * b, CB), :, :].rearrange("p c h d -> p c (h d)")).then_inc(in_ready, 1)

                @block.tensor
                def _(pe):
                    pe.sem_inc(pt_done, 12)
                    pe.sem_inc(o_done, 2)
                    pe.sem_inc(out_done, 1)
                    with pe.Fori(0, B) as b:
                        pe.wait_ge(in_ready, 3 * b + 3)
                        for p in range(NG + 3):
                            if p < NG:
                                pe.wait_ge(kz_ready, NG * b + p + 1)
                                for u, (heads, c) in enumerate(tiles):
                                    r = TU * p + u
                                    pe.wait_ge(s_free, NU * b + r + 1)
                                    h0, nh, nk = G * p + heads[0], len(heads), (c + 1) * P
                                    nc.tensor.matmul(ring[:, r % 4, :], qTb[:, c * P:(c + 1) * P], kzn[:, h0:h0 + nh, 0:nk],
                                                     start=True, stop=True)
                                    nc.tensor.matmul(ring[:, r % 4, :].rearrange("p (h k) -> p h k", h=nh)[:, :, c * P:nk], identb[:, :],
                                                     causal[:, :].unsqueeze(1).broadcast_to([P, nh, P]), start=False, stop=True,
                                                     skip_group_check=True).then_inc(s_done, 1)
                            if 2 <= p < NG + 2:
                                q = p - 2
                                pe.wait_ge(norm_done, NG * b + q + 1)
                                for u, (heads, c) in enumerate(tiles):
                                    r = TU * q + u
                                    pe.wait_ge(pt_free, NU * b + r + 1)
                                    for k in range(4):
                                        ins = nc.tensor.transpose(ptb[:, r % 2, k * P:(k + 1) * P], pr[:, q, u, k * P:(k + 1) * P], ident[:, :])
                                    ins.then_inc(pt_done, 1)
                            if 3 <= p:
                                q = p - 3
                                pe.wait_ge(pt_free, NU * b + TU * (q + 1) + 2)
                                pe.wait_ge(o_free, NG * b + q + 1)
                                for kc in range(CB):
                                    for j in range(G):
                                        h = G * q + j
                                        ins = nc.tensor.matmul(obank[32 * j:32 * j + 32, kc * P:S], vb[:, kc, h * 32:(h + 1) * 32],
                                                               prT[q % 2][:, j, kc, kc * P:S], start=kc == 0, stop=True, skip_group_check=True)
                                ins.then_inc(o_done, 1)
                        pe.wait_ge(o_free, NG * b + NG + 1)
                        pe.wait_ge(out_free, b + 1)
                        for c in range(CB):
                            for q in range(NG):
                                ins = nc.tensor.matmul(misc[:, c * D:(c + 1) * D], oTn[:, q, c * P:(c + 1) * P], C_wp[:, q, :],
                                                       start=q == 0, stop=q == NG - 1)
                        ins.then_inc(out_done, 1)

                @block.scalar
                def _(act):
                    act.sem_inc(s_free, 4)
                    with act.Fori(0, B) as b:
                        for p in range(NG):
                            for u, (heads, c) in enumerate(tiles):
                                r = TU * p + u
                                nh, nk = len(heads), (c + 1) * P
                                act.wait_ge(max_ready, NU * b + r + 1)
                                act.wait_ge(pt_done, NU * b + r + 1)
                                for k in range(nh):
                                    m = stat_of[u] + k
                                    ins = nc.scalar.activation(pr[:, p, u, k * nk:(k + 1) * nk], ring[:, r % 4, k * nk:(k + 1) * nk], ACT.Exp,
                                                               bias=nmax[:, p, m:m + 1], scale=-1.0, accum_out=nsum[:, p, m:m + 1])
                                ins.then_inc(s_free, 1)

                @block.vector
                def _(dve):
                    dve.sem_inc(pt_free, 2)
                    dve.sem_inc(o_free, 1)
                    dve.sem_inc(out_free, 1)
                    with dve.Fori(0, B) as b:
                        ch = Chain(dve, c_steps, CSTEPS * b)
                        for p in range(NG + 5):
                            if p < NG:
                                if p == 0:
                                    dve.wait_ge(in_ready, 3 * b + 1)
                                for h in range(G * p, G * p + G):
                                    ins = nc.vector.tensor_scalar(kzn[:, h, :], kTb[:, :], hmask[:, h:h + 1], None, ALU.mult)
                                ins.then_inc(kz_ready, 1)
                            if 4 <= p < NG + 4:
                                q = p - 4
                                dve.wait_ge(o_done, NG * b + q + 1)
                                for u, (heads, c) in enumerate(tiles):
                                    r = TU * q + u
                                    dve.wait_ge(pt_done, NU * b + r + 1 + 12)
                                    src = ptb[:, r % 2, :].rearrange("p (h q) -> p h q", q=P)
                                    if c == 0:
                                        dst = prT[q % 2][:, :, 0, 0:P]
                                    else:
                                        dst = prT[q % 2][:, heads[0]:heads[0] + 2, :, P:S].rearrange("p h k q -> p (h k) q")
                                    nc.vector.tensor_copy(dst, src).then_inc(pt_free, 1)
                            if 5 <= p:
                                q = p - 5
                                dve.wait_ge(o_done, NG * b + q + 1 + 2)
                                if q == 0:
                                    dve.wait_ge(out_done, b + 1)
                                nc.vector.tensor_scalar(oTn[:, q, :], obank[:, 0:S], col("C_bv", q), None, ALU.add).then_inc(o_free, 1)
                            if 2 <= p < NG + 2:
                                q = p - 2
                                dve.wait_ge(s_free, NU * b + TU * (q + 1) + 4)
                                ch.step(nc.vector.reciprocal(nrs[:, q, :], nsum[:, q, :]))
                                for u, (heads, c) in enumerate(tiles):
                                    nk = (c + 1) * P
                                    for k in range(len(heads)):
                                        m = stat_of[u] + k
                                        a = pr[:, q, u, k * nk:(k + 1) * nk]
                                        ins = nc.vector.tensor_scalar(a, a, nrs[:, q, m:m + 1], None, ALU.mult)
                                ins.then_inc(norm_done, 1)
                            if 1 <= p < NG + 1:
                                q = p - 1
                                for u, (heads, c) in enumerate(tiles):
                                    r = TU * q + u
                                    dve.wait_ge(s_done, NU * b + r + 1)
                                    nc.vector.tensor_reduce(nmax[:, q, stat_of[u]:stat_of[u] + len(heads)],
                                                            ring[:, r % 4, :].rearrange("p (h k) -> p h k", h=len(heads)), AX.X, ALU.min)\
                                        .then_inc(max_ready, 1)
                        xb = x_res[:, bass.ds(CB * b, CB), :]
                        dve.wait_ge(out_done, b + 2)
                        ch.step(nc.vector.tensor_tensor(y[:, :, :], misc[:, 0:CB * D].rearrange("p (c d) -> p c d", c=CB),
                                                        row("C_bp").unsqueeze(1).broadcast_to([P, CB, D]), ALU.add))
                        ch.step(nc.vector.tensor_tensor(y2[:, :, :], y[:, :, :], xb, ALU.add))
                        nc.vector.tensor_scalar(x1[:, bass.ds(CB * b, CB), :], y2[:, :, :], 0.0, None, ALU.add).then_inc(out_free, 1)
                        nc.vector.tensor_tensor(xb, y2[:, :, :], xb, ALU.add)
                        assert ch.n == CSTEPS
            narrow.close()
            scope[0] = ctx

            moe = ctx.enter_context(ExitStack())
            scope[0] = moe
            W1 = [sb(f"W1_{i}", [P, FF]) for i in range(2)]
            W2 = [sb(f"W2_{i}", [P, FC, D]) for i in range(2)]
            b1 = [sb(f"b1_{i}", [P, FC]) for i in range(2)]
            mid = [sb(f"mid{i}", [P, FC, 512]) for i in range(2)]
            logits, top = sb("logits", [P, NC, E]), sb("top", [P, NC, E])
            topi, topf = sb("topi", [P, NC, E], U32), sb("topf", [P, NC, 2])
            iot, iof = sb("iot", [P, E], I32), sb("iof", [P, E])
            gap, e2, w01 = sb("gap", [P, NC]), sb("e2", [P, NC]), sb("w01", [P, NC, 2])
            wa, wb, wts = sb("wa", [P, NC, E]), sb("wb", [P, NC, E]), sb("wts", [P, NC, E])
            wT = sb("wT", [E, NC * P])
            normalise_all("Mx", x1, xn_all, col("C_ln2_g"), col("C_ln2_b"))
            g_mm, g_gap, g_exp, g_w, g_wT, g_wTs, g_b2, g_io, g_steps = map(sem, ["g_mm", "g_gap", "g_exp", "g_w", "g_wT", "g_wTs", "g_b2", "g_io", "g_steps"])
            with nc.Block() as block:
                @block.gpsimd
                def _(pool):
                    nc.gpsimd.iota(iot[:, :], [[1, E]], 0, 0).then_inc(g_io, 1)
                    pool.wait_ge(g_io, 1)
                    nc.gpsimd.tensor_copy(iof[:, :], iot[:, :]).then_inc(g_io, 1)

                @block.tensor
                def _(pe):
                    pe.wait_ge(loadM, 32)
                    for j in range(NC):
                        ins = nc.tensor.matmul(misc[:, j * E:(j + 1) * E], xn_all[:, j * P:(j + 1) * P], M_gw[:, :], start=True, stop=True)
                    ins.then_inc(g_mm, 1)
                    pe.wait_ge(g_w, 1)
                    for j in range(NC):
                        ins = nc.tensor.transpose(ptb[0:E, j // 4, (j % 4) * P:(j % 4 + 1) * P], wts[:, j, :], ident[:, :])
                    ins.then_inc(g_wT, 1)
                    pe.wait_ge(g_wTs, 1)
                    for j in range(NC):
                        ins = nc.tensor.matmul(ring[:, j // 4, (j % 4) * P:(j % 4 + 1) * P], wT[:, j * P:(j + 1) * P], M_b2[:, :],
                                               start=True, stop=True)
                    ins.then_inc(g_b2, 1)

                @block.scalar
                def _(act):
                    act.wait_ge(g_gap, 1)
                    nc.scalar.activation(e2[:, :], gap[:, :], ACT.Exp).then_inc(g_exp, 1)

                @block.vector
                def _(dve):
                    ch = Chain(dve, g_steps)
                    dve.wait_ge(g_mm, 1)
                    ch.step(nc.vector.tensor_tensor(logits[:, :, :], misc[:, 0:NC * E].rearrange("p (j e) -> p j e", e=E),
                                                    row("M_gb").unsqueeze(1).broadcast_to([P, NC, E]), ALU.add))
                    for j in range(NC):
                        ins = nc.vector.max(top[:, j, :], logits[:, j, :])
                    ch.step(ins)
                    for j in range(NC):
                        ins = nc.vector.max_index(topi[:, j, :], top[:, j, :], logits[:, j, :])
                    ch.done(ins)
                    nc.vector.tensor_tensor(gap[:, :], top[:, :, 1], top[:, :, 0], ALU.subtract).then_inc(g_gap, 1)
                    dve.wait_ge(g_steps, 3)
                    ch.step(nc.vector.tensor_copy(topf[:, :, :], topi[:, :, 0:2]))
                    dve.wait_ge(g_exp, 1)
                    ch.step(nc.vector.tensor_scalar(wa[:, :, 0], e2[:, :], 1.0, None, ALU.add))
                    ch.step(nc.vector.reciprocal(w01[:, :, 0], wa[:, :, 0]))
                    ch.step(nc.vector.tensor_tensor(w01[:, :, 1], w01[:, :, 0], e2[:, :], ALU.mult))
                    dve.wait_ge(g_io, 2)
                    for j in range(NC):
                        nc.vector.tensor_scalar(wa[:, j, :], iof[:, :], topf[:, j, 0:1], w01[:, j, 0:1], ALU.is_equal, ALU.mult)
                        ins = nc.vector.tensor_scalar(wb[:, j, :], iof[:, :], topf[:, j, 1:2], w01[:, j, 1:2], ALU.is_equal, ALU.mult)
                    ch.step(ins)
                    nc.vector.tensor_tensor(wts[:, :, :], wa[:, :, :], wb[:, :, :], ALU.add).then_inc(g_w, 1)
                    dve.wait_ge(g_wT, 1)
                    nc.vector.tensor_copy(wT[:, :], ptb[0:E, :, :].rearrange("p c k -> p (c k)")).then_inc(g_wTs, 1)
                    dve.wait_ge(g_b2, 1)
                    nc.vector.tensor_tensor(x_res[:, :, :], ring[:, 0:2, :].rearrange("p a (j d) -> p (a j) d", d=D), x_res[:, :, :], ALU.add)

            EPL = 2
            VU = 2 * EPL
            w_ready = [sem(f"w_ready{k}") for k in range(EPL)]
            m_done, m_free, e_done, e_free = map(sem, ["m_done", "m_free", "e_done", "e_free"])
            with nc.Block() as block:
                @block.sync
                def _(sp):
                    with sp.Fori(0, E // EPL) as i:
                        for k in range(EPL):
                            sp.wait_ge(e_done, VU * i + 2 * k + 2)
                            sp.dma_start(W1[k][:, :], t["M_w1"][bass.ds(EPL * i + k, 1)].rearrange("e p f -> p (e f)")).then_inc(w_ready[k], 16)
                            sp.dma_start(b1[k][:, :], t["M_b1"][bass.ds(EPL * i + k, 1)].rearrange("e p c -> p (e c)")).then_inc(w_ready[k], 16)
                            sp.dma_start(W2[k][:, :, :], t["M_w2"][bass.ds(EPL * i + k, 1)].rearrange("e p c d -> p (e c) d")).then_inc(w_ready[k], 16)

                @block.tensor
                def _(pe):
                    pe.sem_inc(e_done, VU)
                    with pe.Fori(0, E // EPL) as i:
                        for v in range(VU + 1):
                            if v < VU:
                                k, hf = v // 2, v % 2
                                pe.wait_ge(w_ready[k], 48 * i + 48)
                                for hc in range(FC):
                                    pe.wait_ge(m_free, FC * VU * i + FC * v + hc + 1)
                                    nc.tensor.matmul(ring[:, hc, :], W1[k][:, hc * P:(hc + 1) * P], xn_all[:, hf * 512:(hf + 1) * 512],
                                                     start=True, stop=True).then_inc(m_done, 1)
                            if v > 0:
                                w = v - 1
                                pe.wait_ge(m_free, FC * VU * i + FC * v + 4)
                                pe.wait_ge(e_free, VU * i + w + 1)
                                for tc in range(4):
                                    for hc in range(FC):
                                        ins = nc.tensor.matmul(ptb[:, w % 2, tc * P:(tc + 1) * P], mid[w % 2][:, hc, tc * P:(tc + 1) * P],
                                                               W2[w // 2][:, hc, :], start=hc == 0, stop=hc == FC - 1)
                                ins.then_inc(e_done, 1)

                @block.scalar
                def _(act):
                    act.sem_inc(m_free, 4)
                    with act.Fori(0, E // EPL) as i:
                        for v in range(VU):
                            act.wait_ge(e_done, VU * i + v + 3)
                            for hc in range(FC):
                                act.wait_ge(m_done, FC * VU * i + FC * v + hc + 1)
                                nc.scalar.activation(mid[v % 2][:, hc, :], ring[:, hc, :], ACT.Gelu,
                                                     bias=b1[v // 2][:, hc:hc + 1]).then_inc(m_free, 1)

                @block.vector
                def _(dve):
                    dve.sem_inc(e_free, 2)
                    with dve.Fori(0, E // EPL) as i:
                        for v in range(VU):
                            k, hf = v // 2, v % 2
                            dve.wait_ge(e_done, VU * i + v + 1 + VU)
                            for tc in range(4):
                                j = 4 * hf + tc
                                ins = nc.vector.scalar_tensor_tensor(x_res[:, j, :], ptb[:, v % 2, tc * P:(tc + 1) * P],
                                                                     wts[:, j, bass.ds(EPL * i + k, 1)], x_res[:, j, :], ALU.mult, ALU.add)
                            ins.then_inc(e_free, 1)
            moe.close()
            scope[0] = ctx

            def layernorm_stream(name, last=False):
                stat, rs, hat_ready, tr_done, steps, psteps = [sem(f"{name}_{x}") for x in ("stat", "rstd", "hat", "tr", "steps", "psteps")]
                with nc.Block() as block:
                    @block.vector
                    def _(dve):
                        ch = Chain(dve, steps)
                        ln_stats(ch, lambda i: x_res[:, i, :], NC).then_inc(stat, 1)
                        dve.wait_ge(rs, 1)
                        for i in range(NC):
                            nc.vector.tensor_scalar(x_res[:, i, :], x_res[:, i, :], mv[:, i, 0:1], rstd[:, i:i + 1], ALU.subtract, ALU.mult)\
                                .then_inc(hat_ready, 1)
                        if not last:
                            for g in range(NC // 4):
                                dve.wait_ge(tr_done, g + 1)
                                nc.vector.tensor_copy(xn_all[:, g * 512:(g + 1) * 512], ring[:, g, :])

                    @block.gpsimd
                    def _(pool):
                        pool.wait_ge(stat, 1)
                        ln_power(Chain(pool, psteps), NC).then_inc(rs, 1)

                    if not last:
                        @block.tensor
                        def _(pe):
                            for i in range(NC):
                                pe.wait_ge(hat_ready, i + 1)
                                ins = nc.tensor.transpose(ring[:, i // 4, (i % 4) * P:(i % 4 + 1) * P], x_res[:, i, :], ident[:, :])
                                if i % 4 == 3:
                                    ins.then_inc(tr_done, 1)
                    else:
                        @block.sync
                        def _(sp):
                            sp.wait_ge(hat_ready, NC)
                            sp.dma_start(t["out"].rearrange("(j p) d -> p j d", p=P), x_res[:, :, :]).then_inc(stored, 16)
                            sp.wait_ge(stored, 16)

            stored = sem("stored")
            layernorm_stream("Cl")

        if upto > 2:
            over = ctx.enter_context(ExitStack())
            scope[0] = over
            NT = B * (B + 1) // 2
            qkv = sb("qkv", [P, B, CB, 3 * D])
            prod = sb("prod", [P, B, CB, D])
            sc = sb("sc", [P, NT, CB * H])
            smax, ssum = sb("smax", [P, B, CB * H]), sb("ssum", [P, B, CB * H])
            att = sb("att", [P, B, CB * D])
            d_mm, d_evac, d_arg, d_exp, d_steps = map(sem, ["d_mm", "d_evac", "d_arg", "d_exp", "d_steps"])
            with nc.Block() as block:
                @block.tensor
                def _(pe):
                    pe.wait_ge(loadF, 16 * 7)
                    for j in range(NC):
                        if j >= 4:
                            pe.wait_ge(d_evac, j - 3)
                        nc.tensor.matmul(ring[:, j % 4, 0:3 * D], xn_all[:, j * P:(j + 1) * P], D_w[:, :], start=True, stop=True).then_inc(d_mm, 1)

                @block.scalar
                def _(act):
                    act.wait_ge(d_arg, 1)
                    nc.scalar.activation(sc[:, :, :], sc[:, :, :], ACT.Exp, scale=float(HD) ** -0.5).then_inc(d_exp, 1)

                @block.vector
                def _(dve):
                    ch = Chain(dve, d_steps)
                    for j in range(NC):
                        dve.wait_ge(d_mm, j + 1)
                        nc.vector.tensor_tensor(qkv[:, j // CB, j % CB, :], ring[:, j % 4, 0:3 * D], row("D_b"), ALU.add).then_inc(d_evac, 1)
                    dve.wait_ge(d_evac, NC)
                    for i in range(B):
                        t0 = i * (i + 1) // 2
                        q = qkv[:, i, :, 0:D].unsqueeze(1).broadcast_to([P, i + 1, CB, D])
                        ch.step(nc.vector.tensor_tensor(prod[:, 0:i + 1, :, :], qkv[:, 0:i + 1, :, D:2 * D], q, ALU.mult))
                        ch.step(nc.vector.tensor_reduce(sc[:, t0:t0 + i + 1, :], prod[:, 0:i + 1, :, :].rearrange("p j c (h d) -> p j (c h) d", d=HD),
                                                        AX.X, ALU.add))
                        s3 = sc[:, t0:t0 + i + 1, :]
                        ch.step(nc.vector.tensor_reduce(smax[:, i, :], s3.rearrange("p j x -> p x j"), AX.X, ALU.max))
                        ins = nc.vector.tensor_tensor(s3, s3, smax[:, i, :].unsqueeze(1).broadcast_to([P, i + 1, CB * H]), ALU.subtract)
                    ins.then_inc(d_arg, 1)
                    dve.wait_ge(d_exp, 1)
                    for i in range(B):
                        t0 = i * (i + 1) // 2
                        ins = nc.vector.tensor_reduce(ssum[:, i, :], sc[:, t0:t0 + i + 1, :].rearrange("p j x -> p x j"), AX.X, ALU.add)
                    ch.step(ins)
                    ch.step(nc.vector.tensor_scalar(ssum[:, :, :], ssum[:, :, :], 1.0, None, ALU.add))
                    ch.step(nc.vector.reciprocal(ssum[:, :, :], ssum[:, :, :]))
                    for i in range(B):
                        t0 = i * (i + 1) // 2
                        for c in range(CB):
                            pb = sc[:, t0:t0 + i + 1, c * H:(c + 1) * H].unsqueeze(3).broadcast_to([P, i + 1, H, HD])
                            ins = nc.vector.tensor_tensor(prod[:, 0:i + 1, c, :].rearrange("p j (h d) -> p j h d", d=HD),
                                                          qkv[:, 0:i + 1, c, 2 * D:3 * D].rearrange("p j (h d) -> p j h d", d=HD), pb, ALU.mult)
                        ch.step(ins)
                        ch.step(nc.vector.tensor_reduce(att[:, i, :], prod[:, 0:i + 1, :, :].rearrange("p j c d -> p (c d) j"), AX.X, ALU.add))
                    a3 = att[:, :, :].rearrange("p i (x d) -> p (i x) d", d=HD)
                    ch.step(nc.vector.tensor_tensor(a3, a3, ssum[:, :, :].rearrange("p i x -> p (i x)").unsqueeze(2).broadcast_to([P, B * CB * H, HD]), ALU.mult))
                    nc.vector.tensor_tensor(x_res[:, :, :], att[:, :, :].rearrange("p i (c d) -> p (i c) d", c=CB), x_res[:, :, :], ALU.add)
            over.close()
            scope[0] = ctx
            layernorm_stream("Dl")

        if upto > 3:
            gate = ctx.enter_context(ExitStack())
            scope[0] = gate
            gl = [sb(f"gl{i}", [P, CB, S]) for i in range(2)]
            e_x1, e_gl, e_h, e_out = map(sem, ["e_x1", "e_gl", "e_h", "e_out"])
            with nc.Block() as block:
                @block.tensor
                def _(pe):
                    for b in range(B + 1):
                        if b < B:
                            for fc in range(CB):
                                ins = nc.tensor.matmul(ring[:, b, fc * S:(fc + 1) * S], ctxT[:, b, fc * P:(fc + 1) * P], xn_all[:, b * S:(b + 1) * S],
                                                       start=True, stop=True)
                            ins.then_inc(e_x1, 1)
                        if b > 0:
                            a = b - 1
                            pe.wait_ge(e_h, b)
                            for c in range(CB):
                                for fc in range(CB):
                                    ins = nc.tensor.matmul(ptb[:, a // 2, (a % 2 * CB + c) * P:(a % 2 * CB + c + 1) * P], gl[a % 2][:, fc, c * P:(c + 1) * P],
                                                           ctx_tok[:, CB * a + fc, :], start=fc == 0, stop=fc == CB - 1)
                            ins.then_inc(e_out, 1)

                @block.scalar
                def _(act):
                    for b in range(B):
                        act.wait_ge(e_x1, b + 1)
                        if b >= 2:
                            act.wait_ge(e_out, b - 1)
                        nc.scalar.activation(gl[b % 2][:, :, :].rearrange("p c s -> p (c s)"), ring[:, b, :], ACT.Gelu_apprx_tanh).then_inc(e_gl, 1)

                @block.vector
                def _(dve):
                    for b in range(B):
                        dve.wait_ge(e_gl, b + 1)
                        g = gl[b % 2][:, :, :].rearrange("p c s -> p (c s)")
                        nc.vector.tensor_tensor(g, g, ring[:, b, :], ALU.mult).then_inc(e_h, 1)
                    for k in range(2):
                        dve.wait_ge(e_out, 2 * k + 2)
                        nc.vector.tensor_tensor(x_res[:, 4 * k:4 * k + 4, :], ptb[:, k, :].rearrange("p (j d) -> p j d", d=D), x_res[:, 4 * k:4 * k + 4, :], ALU.add)
            gate.close()
            scope[0] = ctx
            layernorm_stream("El")

        if upto > 4:
            f_a, f_b = sb("f_a", [P, 2, FC, 512]), sb("f_b", [P, 2, FC, 512])
            f_done, f_act, f_free, f_out, f_steps = map(sem, ["f_done", "f_act", "f_free", "f_out", "f_steps"])
            with nc.Block() as block:
                @block.tensor
                def _(pe):
                    n = 0
                    for hf in range(2):
                        for hc in range(FC):
                            for w in (F_w1, F_w2):
                                if n >= 4:
                                    pe.wait_ge(f_free, n - 3)
                                nc.tensor.matmul(ring[:, n % 4, :], w[:, hc * P:(hc + 1) * P], xn_all[:, hf * 512:(hf + 1) * 512], start=True,
                                                 stop=True).then_inc(f_done, 1)
                                n += 1
                    for layer, (w, src) in enumerate([(F_h1, f_a), (F_h2, f_b)]):
                        for hf in range(2):
                            pe.wait_ge(f_free, n - (FC if layer else 2 * FC) * (1 - hf) if layer else 2 * FC * (hf + 1))
                            for oc in range(FC):
                                pe.wait_ge(f_free, n - 3)
                                for kc in range(FC):
                                    ins = nc.tensor.matmul(ring[:, n % 4, :], w[:, kc, oc * P:(oc + 1) * P], src[:, hf, kc, :], start=kc == 0, stop=kc == FC - 1)
                                ins.then_inc(f_done, 1)
                                n += 1
                    for hf in range(2):
                        pe.wait_ge(f_free, n - FC * (1 - hf))
                        for tc in range(4):
                            for kc in range(FC):
                                ins = nc.tensor.matmul(ptb[:, hf, tc * P:(tc + 1) * P], f_a[:, hf, kc, tc * P:(tc + 1) * P], F_w3[:, kc, :],
                                                       start=kc == 0, stop=kc == FC - 1)
                        ins.then_inc(f_out, 1)

                @block.scalar
                def _(act):
                    n = 0
                    for hf in range(2):
                        for hc in range(FC):
                            act.wait_ge(f_done, n + 1)
                            nc.scalar.activation(f_a[:, hf, hc, :], ring[:, n % 4, :], ACT.Silu, scale=col("F_s1", hc)).then_inc(f_act, 1)
                            n += 2
                    act.wait_ge(f_free, n)
                    for layer, (dst, s) in enumerate([(f_b, "F_h1"), (f_a, "F_h2")]):
                        for hf in range(2):
                            for oc in range(FC):
                                act.wait_ge(f_done, n + 1)
                                nc.scalar.activation(dst[:, hf, oc, :], ring[:, n % 4, :], ACT.Gelu, scale=col(s, oc)).then_inc(f_free, 1)
                                n += 1

                @block.vector
                def _(dve):
                    n = 0
                    for hf in range(2):
                        for hc in range(FC):
                            dve.wait_ge(f_act, hf * FC + hc + 1)
                            dve.wait_ge(f_done, n + 2)
                            a = f_a[:, hf, hc, :]
                            nc.vector.scalar_tensor_tensor(a, ring[:, (n + 1) % 4, :], col("F_s2", hc), a, ALU.mult, ALU.mult).then_inc(f_free, 2)
                            n += 2
                    ch = Chain(dve, f_steps)
                    for hf in range(2):
                        dve.wait_ge(f_out, hf + 1)
                        ch.step(nc.vector.tensor_tensor(hat[:, 4 * hf:4 * hf + 4, :], ptb[:, hf, :].rearrange("p (j d) -> p j d", d=D),
                                                        row("F_s3").unsqueeze(1).broadcast_to([P, 4, D]), ALU.mult))
                        nc.vector.tensor_tensor(x_res[:, 4 * hf:4 * hf + 4, :], hat[:, 4 * hf:4 * hf + 4, :], x_res[:, 4 * hf:4 * hf + 4, :], ALU.add)
            layernorm_stream("Fl", last=True)

        if upto < 5:
            fin = sem("fin")
            with nc.Block() as block:
                @block.sync
                def _(sp):
                    sp.wait_ge(loadB, 64)
                    if upto > 1:
                        sp.wait_ge(loadF, 16 * 7)
                        sp.wait_ge(loadM, 32)
                    sp.dma_start(t["out"].rearrange("(j p) d -> p j d", p=P), x_res[:, :, :]).then_inc(fin, 16)
                    sp.wait_ge(fin, 16)


def layout(i):
    import numpy as np

    i = {k: np.asarray(v) for k, v in i.items()}
    a = {}
    a["x"] = i["x"].reshape(B * S, D)
    a["xT"] = i["x"].transpose(0, 2, 1)
    a["ctx"] = i["ctx_1024"].reshape(B * S, D)
    a["ctxT"] = i["ctx_1024"].transpose(0, 2, 1)
    for k in ("q", "k", "v", "o"):
        a["A_w" + k] = i["L0_attn_W" + k]
    a["B_wq"], a["B_wkv"], a["B_wo"] = i["L0_xattn_Wq"], i["L0_xattn_Wkv"], i["L0_xattn_Wo"]
    for k in ("q", "k", "v"):
        a["C_w" + k] = i["L0_ffn_W" + k]
    wp = np.zeros((4, 4, 32, D), np.float32)
    wp[:, :, :HD] = i["L0_ffn_Wp"].reshape(4, 4, HD, D)
    a["C_wp"] = wp.reshape(4, P, D)
    a["M_gw"] = i["L0_ffn_gate_W"]
    a["M_w1"], a["M_b2"] = i["L0_ffn_exp_W1"], i["L0_ffn_exp_b2"]
    a["M_b1"] = i["L0_ffn_exp_b1"].reshape(E, FC, P).transpose(0, 2, 1)
    a["M_w2"] = i["L0_ffn_exp_W2"].reshape(E, FC, P, D).transpose(0, 2, 1, 3)
    a["D_w"] = np.concatenate([i[f"L1_attn_W{k}"].T for k in "qkv"], axis=1)
    a["F_w1"], a["F_w2"] = i["L1_ffn_w1_w"].T, i["L1_ffn_w2_w"].T
    for k in ("h1", "h2", "w3"):
        w = i[f"L1_ffn_{k}_w"].T
        a["F_" + k] = w.reshape(FC, P, w.shape[1]).transpose(1, 0, 2)
    bv = np.zeros((4, 4, 32), np.float32)
    bv[:, :, :HD] = i["L0_ffn_bv"].reshape(4, 4, HD)
    two = lambda v: np.concatenate([v, v])
    c = {
        "A_bq": i["L0_attn_bq"].reshape(PAIRS, P).T, "A_bk": i["L0_attn_bk"].reshape(PAIRS, P).T,
        "A_bv": i["L0_attn_bv"].reshape(PAIRS, P).T, "B_qs": two(i["L0_xattn_q_scale"]), "B_ks": two(i["L0_xattn_k_scale"]),
        "B_nv": two(i["L0_xattn_null_kv"][1]),
        "B_in_g": i["L0_xattn_ln_in_g"], "B_in_b": i["L0_xattn_ln_in_b"], "B_ctx_g": i["L0_xattn_ln_ctx_g"],
        "B_ctx_b": i["L0_xattn_ln_ctx_b"], "C_ln1_g": i["L0_ffn_ln1_g"], "C_ln1_b": i["L0_ffn_ln1_b"],
        "C_ln2_g": i["L0_ffn_ln2_g"], "C_ln2_b": i["L0_ffn_ln2_b"], "C_bq": i["L0_ffn_bq"], "C_bk": i["L0_ffn_bk"],
        "C_bv": bv.reshape(4, P).T,
        "F_s1": i["L1_ffn_w1_s"].reshape(FC, P).T, "F_s2": i["L1_ffn_w2_s"].reshape(FC, P).T,
        "F_h1": i["L1_ffn_h1_s"].reshape(FC, P).T, "F_h2": i["L1_ffn_h2_s"].reshape(FC, P).T,
    }
    a["cols"] = np.concatenate([np.reshape(c[n], (P, w)) for n, (_, w) in COLS.items()], axis=1)
    r = {"A_bo": i["L0_attn_bo"], "B_out_g": i["L0_xattn_ln_out_g"], "B_out_b": i["L0_xattn_ln_out_b"],
         "B_nk": i["L0_xattn_null_kv"][0], "B_qsr": i["L0_xattn_q_scale"], "B_ksr": i["L0_xattn_k_scale"], "C_bp": i["L0_ffn_bp"], "M_gb": i["L0_ffn_gate_b"],
         "D_b": np.concatenate([i[f"L1_attn_b{k}"] for k in "qkv"]), "F_s3": i["L1_ffn_w3_s"]}
    a["rows"] = np.concatenate([r[n] for n in ROWS])
    return {k: np.ascontiguousarray(v) for k, v in a.items()}


def kernel(**inputs):
    import numpy as _np
    import concourse.bacc as _bacc
    from concourse import mybir as _mybir
    from concourse.bass_utils import run_bass_kernel_spmd as _run

    nc = _bacc.Bacc("TRN2", target_bir_lowering=False, num_devices=1)
    arrays, t = {}, {}
    for name, a in layout(inputs).items():
        arrays[f"in_{name}_dram"] = a
        t[name] = nc.dram_tensor(f"in_{name}_dram", a.shape, _mybir.dt.from_np(a.dtype), kind="ExternalInput").ap()
    t["out"] = nc.dram_tensor("out_0_dram", (B * S, D), _mybir.dt.float32, kind="ExternalOutput").ap()
    decoder(nc, t)
    r = _run(nc, [arrays], core_ids=[0])
    return _np.asarray(r.results[0]["out_0_dram"]).reshape(B, S, D)
```

```python
from contextlib import ExitStack

import concourse.bass as bass
from concourse import mybir

F32 = mybir.dt.float32
BF16 = mybir.dt.bfloat16
I32 = mybir.dt.int32
U32 = mybir.dt.uint32
ALU = mybir.AluOpType
ACT = mybir.ActivationFunctionType
AX = mybir.AxisListType

B, S, D = 4, 256, 128
P = 128
NC = B * S // P
CB = S // P
H, A = 16, 64
PAIRS = H // 2
HD = D // H
E, FF = 8, 4 * D
FC = FF // P
LN_EPS = 1e-5
NORM_EPS = 1e-12
MASKED = 1e30

COLS = {}
for _n, _w in [("A_bq", PAIRS), ("A_bk", PAIRS), ("A_bv", PAIRS), ("B_qs", 1), ("B_ks", 1), ("B_nv", 1),
               ("B_in_g", 1), ("B_in_b", 1), ("B_ctx_g", 1), ("B_ctx_b", 1), ("C_ln1_g", 1), ("C_ln1_b", 1),
               ("C_ln2_g", 1), ("C_ln2_b", 1), ("C_bq", 1), ("C_bk", 1), ("C_bv", 1),
               ("F_s1", FC), ("F_s2", FC), ("F_h1", FC), ("F_h2", FC)]:
    COLS[_n] = (sum(w for _, w in COLS.values()), _w)
NCOLS = sum(w for _, w in COLS.values())
ROWS = {}
for _n, _w in [("A_bo", D), ("B_out_g", D), ("B_out_b", D), ("B_nk", A), ("B_qsr", A), ("B_ksr", A), ("C_bp", D), ("M_gb", E), ("D_b", 3 * D),
               ("F_s3", D)]:
    ROWS[_n] = (sum(w for _, w in ROWS.values()), _w)
NROWS = sum(w for _, w in ROWS.values())


class Chain:

    def __init__(self, eng, sem, base=0):
        self.eng, self.sem, self.base, self.n = eng, sem, base, 0

    def done(self, ins):
        self.n += 1
        ins.then_inc(self.sem, 1)

    def step(self, ins):
        self.done(ins)
        self.eng.wait_ge(self.sem, self.base + self.n)


def decoder(nc, t, upto=99):
    ctx = ExitStack()
    with ctx:
        wide = ctx.enter_context(ExitStack())
        scope = [ctx]

        def sb(name, shape, dt=F32):
            return scope[0].enter_context(nc.sbuf_tensor(name, shape, dt))

        def sem(name):
            return ctx.enter_context(nc.semaphore(name))

        RING = 4
        ring = ctx.enter_context(nc.psum_tensor("ring", [P, RING, 512], F32))
        ptb = ctx.enter_context(nc.psum_tensor("ptb", [P, CB, 512], F32))
        obank = ctx.enter_context(nc.psum_tensor("obank", [P, 512], F32))
        misc = ctx.enter_context(nc.psum_tensor("misc", [P, 512], F32))

        x_res = sb("x_res", [P, NC, D])
        ctx_tok = sb("ctx_tok", [P, NC, D])
        cols = sb("cols", [P, NCOLS])
        rows = sb("rows", [P, NROWS])
        ident = sb("ident", [P, P])
        CONSTS = [-0.5, LN_EPS, float(A) ** 0.5, -float(A) ** 0.5]
        const = sb("const", [P, len(CONSTS), 64])
        C_wq, C_wk, C_wv, C_wp = [sb("C_w" + n, [P, D]) for n in "qkvp"]
        M_gw, M_b2 = sb("M_gw", [P, E]), sb("M_b2", [E, D])
        hmask = sb("hmask", [P, H])
        causal, identb = sb("causal", [P, P], BF16), sb("identb", [P, P], BF16)
        half = const[:, 0, :]

        def col(name, i=0, lo=0, hi=P):
            o = COLS[name][0] + i
            return cols[lo:hi, o:o + 1]

        def row(name):
            o, w = ROWS[name]
            return rows[:, o:o + w]

        def rowb(name, n):
            return row(name).unsqueeze(1).broadcast_to([P, n, ROWS[name][1]])

        st = sb("st", [P, NC, 6])
        mv = sb("mv", [P, NC, 2])
        veps = sb("veps", [P, NC])
        rstd = sb("rstd", [P, NC])
        xn_all = sb("xn_all", [P, NC * P])
        hat = sb("hat", [P, NC, D])
        y = sb("y", [P, CB, D])
        y2 = sb("y2", [P, CB, D])
        scrap = sb("scrap", [P, 1])

        scope[0] = wide
        A_wq, A_wk, A_wv = sb("A_wq", [P, H * A]), sb("A_wk", [P, H * A]), sb("A_wv", [P, H * A])
        A_wo = sb("A_wo", [P, PAIRS, D])
        B_wq, B_wkv = sb("B_wq", [P, H * A]), sb("B_wkv", [P, 2 * H * A])
        B_wo = sb("B_wo", [P, PAIRS, D])
        xTa, cn_all = sb("xTa", [P, NC * P]), sb("cn_all", [P, NC * P])
        vtok = [sb(f"vtok{i}", [P, CB, H * A]) for i in range(2)]
        ktok = [sb(f"ktok{i}", [P, CB, H * A]) for i in range(2)]
        ksq = sb("ksq", [P, CB * H, A])
        kss, krn = sb("kss", [P, CB * H]), sb("krn", [P, CB * H])
        qT = [sb(f"qT{i}", [P, S]) for i in range(2)]
        qT_all = [sb(f"qT_all{i}", [P, PAIRS, S]) for i in range(2)]
        qsq = sb("qsq", [P, PAIRS, S])
        kz = [sb(f"kz{i}", [P, 2, S]) for i in range(2)]
        probs = [sb(f"probs{i}", [P, CB, 2, S]) for i in range(4)]
        probsT = [sb(f"probsT{i}", [P, 2, CB, S]) for i in range(2)]
        oT = [sb(f"oT{i}", [P, PAIRS, S]) for i in range(2)]
        ssn = sb("ssn", [P, 2, 8 * PAIRS])
        rqt = sb("rqt", [P, 4 * PAIRS])

        def stats(n):
            return sb(n, [P, 2, PAIRS, CB, 2])
        negmax, sums, rsum, prq, nrq, snr, mins, pn, pnarg = map(
            stats, ["negmax", "sums", "rsum", "prq", "nrq", "snr", "mins", "pn", "pnarg"])
        pnt, pnT = sb("pnt", [P, CB, H]), sb("pnT", [H, S])
        nqk, wnull, blk = sb("nqk", [P, 1]), sb("wnull", [P, H]), sb("blk", [P, 2])
        nvz, nvwo = sb("nvz", [P, PAIRS, H]), sb("nvwo", [H, D])
        nkr, nks = sb("nkr", [P, A]), sb("nks", [P, 1])
        wtmp = ksq[:, 0:H, :]
        lst, lmv = sb("lst", [P, CB, 6]), sb("lmv", [P, 2, CB, 2])
        lve, lrs = sb("lve", [P, CB]), sb("lrs", [P, 2, CB])

        loadN = sem("loadN")
        loadA, loadC, loadX = sem("loadA"), sem("loadC"), sem("loadX")
        loadW = {n: sem("load_" + n) for n in ("A_wq", "A_wk", "A_wv", "A_wo", "B_wq", "B_wkv", "B_wo")}

        def ln_stats(ch, src, n):
            for i in range(n):
                ins = nc.vector.bn_stats(st[:, i, :], src(i))
            ch.step(ins)
            for i in range(n):
                ins = nc.vector.bn_aggr(mv[:, i, :], st[:, i, :])
            return ins

        def ln_power(ch, n):
            ch.step(nc.gpsimd.tensor_tensor(veps[:, 0:n], mv[:, 0:n, 1], const[:, 1, 0:n], ALU.add))
            return nc.gpsimd.tensor_tensor(rstd[:, 0:n], veps[:, 0:n], half[:, 0:n], ALU.pow)

        TL = 3
        NP = 2 * B * PAIRS
        STEPS = NP + 2 * TL + 8
        extras = {s: [] for s in range(STEPS)}
        dve_extras = {s: [] for s in range(STEPS)}
        ssq_at = {}
        for bb in range(2 * B):
            s0, b, cross = PAIRS * bb, bb % B, bb >= B
            for r in range(4):
                extras[s0 - 4 + r if bb else r].append(("V", bb, r))
                if cross:
                    extras[s0 - 8 + r].append(("K", b, r))
                    extras[s0 - 7 + r].append(("Q", b, r))
                    ssq_at[s0 - 5 + r] = (b, r)
            if cross:
                dve_extras[s0 - 4].append(("ksum", b))
                dve_extras[s0 - 2].append(("khat", b))
                dve_extras[s0 - 1].append(("qsum", b))
                dve_extras[s0 + 10].append(("pnt", b))
                extras[s0 + 11].append(("pnT", b, 0))
            else:
                extras[s0 + 17].append(("X", b, 0))
                dve_extras[s0 + 15].append(("xnorm", b))
                dve_extras[s0 + 16].append(("xhat", b))
            for c in range(CB):
                extras[s0 + 12 + c].append(("out", bb, c))
            dve_extras[s0 + 14].append(("apply", bb))
            if cross:
                dve_extras[s0 + 15].append(("apply2", b))
                dve_extras[s0 + 16].append(("cnorm", b))
                dve_extras[s0 + 17].append(("chat", b))
                extras[s0 + 18].append(("CX", b, 0))
        dve_extras[5].append(("ctx_norm", 0))
        dve_extras[6].append(("ctx_hat", 0))
        extras[8].append(("C", 0, 0))
        extras[9].append(("C", 1, 0))
        dve_extras[8].append(("null_value", 0))
        dve_extras[9].append(("null_key", 0))
        extras[10].append(("NV", 0, 0))
        misc_extras = {s: [e for e in extras[s] if e[0] not in ("V", "K", "Q")] for s in extras}
        ring_extras = {s: [e for e in extras[s] if e[0] in ("V", "K", "Q")] for s in extras}
        ring_at, misc_at = {}, {}
        for s in range(STEPS):
            if s < NP:
                misc_at["pair", s] = len(misc_at)
            if 1 <= s <= NP:
                for c in range(CB):
                    ring_at["S", s - 1, c] = len(ring_at)
            for e in misc_extras[s]:
                misc_at[e] = len(misc_at)
            for e in ring_extras[s]:
                ring_at[e] = len(ring_at)

        def nulls(b, q):
            o = 4 * PAIRS + 4 * q
            return ssn[:, b % 2, o:o + 4].rearrange("p (c h) -> p c h", c=CB)

        cst, ring_done, ring_free = sem("cst"), sem("ring_done"), sem("ring_free")
        misc_done, misc_free = sem("misc_done"), sem("misc_free")
        max_ready, norm_done, ssn_ready = sem("max_ready"), sem("norm_done"), sem("ssn_ready")
        load_first = sem("load_first")
        pt_done, pt_free, o_done, o_free = sem("pt_done"), sem("pt_free"), sem("o_done"), sem("o_free")
        khat_ready, ksum_ready, krn_ready = sem("khat_ready"), sem("ksum_ready"), sem("krn_ready")
        qsum_ready, rq_ready, pnt_ready = sem("qsum_ready"), sem("rq_ready"), sem("pnt_ready")
        var_ready, rstd_ready = sem("var_ready"), sem("rstd_ready")
        xhat_ready, c_hat_ready = sem("xhat_ready"), sem("c_hat_ready")
        cstat, crstd, chat = sem("cstat"), sem("crstd"), sem("chat")
        null_ss, null_pow, null_ready, consts_ready = sem("null_ss"), sem("null_pow"), sem("null_ready"), sem("consts_ready")
        wide_dve, wide_pool = sem("wide_dve"), sem("wide_pool")

        def ln_rstd(pool, ch, n):
            pool.wait_ge(var_ready, n + 1)
            ch.step(nc.gpsimd.tensor_tensor(lve[:, :], lmv[:, n % 2, :, 1], const[:, 1, 0:CB], ALU.add))
            nc.gpsimd.tensor_tensor(lrs[:, n % 2, :], lve[:, :], half[:, 0:CB], ALU.pow).then_inc(rstd_ready, 1)
            return n + 1

        with nc.Block() as block:
            @block.sync
            def _(sp):
                sp.dma_start(xTa[:, 0:S], t["xT"][0]).then_inc(load_first, 16)
                sp.dma_start(A_wq[:, 0:2 * P], t["A_wq"][:, 0:2 * P]).then_inc(load_first, 16)
                sp.dma_start(A_wq[:, 2 * P:], t["A_wq"][:, 2 * P:]).then_inc(loadW["A_wq"], 16)
                sp.dma_start(A_wv[:, :], t["A_wv"]).then_inc(loadW["A_wv"], 16)
                sp.dma_start(xTa[:, S:].rearrange("p (b s) -> p b s", b=B - 1), t["xT"][1:B].rearrange("b p s -> p b s")).then_inc(loadX, 16)
                sp.dma_start(x_res[:, :, :], t["x"].rearrange("(j p) d -> p j d", p=P)).then_inc(loadA, 16)
                sp.dma_start(A_wo[:, :, :], t["A_wo"].rearrange("(a p) d -> p a d", p=P)).then_inc(loadW["A_wo"], 16)
                sp.dma_start(B_wkv[:, :], t["B_wkv"]).then_inc(loadW["B_wkv"], 16)
                for dst, src in [(C_wq, "C_wq"), (C_wk, "C_wk"), (C_wv, "C_wv"), (C_wp, "C_wp"), (M_gw, "M_gw"), (M_b2, "M_b2")]:
                    sp.dma_start(dst[:, :], t[src]).then_inc(loadN, 16)

            @block.scalar
            def _(act):
                act.dma_start(A_wk[:, 0:2 * P], t["A_wk"][:, 0:2 * P]).then_inc(load_first, 16)
                act.dma_start(cols[:, :], t["cols"]).then_inc(loadC, 16)
                act.dma_start(A_wk[:, 2 * P:], t["A_wk"][:, 2 * P:]).then_inc(loadW["A_wk"], 16)
                act.dma_start(ctx_tok[:, :, :], t["ctx"].rearrange("(j p) d -> p j d", p=P)).then_inc(loadA, 16)
                act.dma_start(rows[:, :], t["rows"].partition_broadcast(P)).then_inc(loadA, 16)
                act.dma_start(B_wo[:, :, :], t["B_wo"].rearrange("(a p) d -> p a d", p=P)).then_inc(loadW["B_wo"], 16)
                act.dma_start(B_wq[:, :], t["B_wq"]).then_inc(loadW["B_wq"], 16)
                act.wait_ge(consts_ready, 2)
                for s in range(STEPS):
                    if s - 1 in ssq_at and ssq_at[s - 1][1] == 3:
                        b = ssq_at[s - 1][0]
                        act.wait_ge(o_done, s - TL - 1)
                        nc.scalar.copy(ssn[:, b % 2, :], obank[:, S:S + 8 * PAIRS]).then_inc(ssn_ready, 1)
                    if TL + 2 <= s < NP + TL + 2:
                        g = s - TL - 2
                        bb, q = g // PAIRS, g % PAIRS
                        act.wait_ge(o_done, g + 1)
                        if bb >= 2 and q == 0:
                            act.wait_ge(misc_done, misc_at["out", bb - 2, CB - 1] + 1)
                        if bb < B:
                            nc.scalar.activation(oT[bb % 2][:, q, :], obank[:, 0:S], ACT.Identity, bias=col("A_bv", q)).then_inc(o_free, 1)
                        else:
                            nc.scalar.copy(oT[bb % 2][:, q, :], obank[:, 0:S]).then_inc(o_free, 1)
                    if s < NP:
                        q = s % PAIRS
                        act.wait_ge(misc_done, misc_at["pair", s] + 1)
                        if s >= 2:
                            act.wait_ge(ring_done, ring_at["S", s - 2, 1] + 1)
                        lo, hi = slice(0, A), slice(A, P)
                        if s < B * PAIRS:
                            nc.scalar.activation(qT[s % 2][:, :], misc[:, 0:S], ACT.Identity, bias=col("A_bq", q), scale=-float(A) ** -0.5)
                            nc.scalar.activation(kz[s % 2][lo, 0, :], misc[lo, S:2 * S], ACT.Identity, bias=col("A_bk", q, 0, A))
                            ins = nc.scalar.activation(kz[s % 2][hi, 1, :], misc[hi, S:2 * S], ACT.Identity, bias=col("A_bk", q, A, P))
                        else:
                            nc.scalar.copy(kz[s % 2][lo, 0, :], misc[lo, 0:S])
                            ins = nc.scalar.copy(kz[s % 2][hi, 1, :], misc[hi, 0:S])
                        ins.then_inc(misc_free, 1)
                    for e in misc_extras[s]:
                        if e[0] == "pnT":
                            act.wait_ge(misc_done, misc_at[e] + 1)
                            nc.scalar.copy(pnT[:, :], misc[0:H, 0:S]).then_inc(misc_free, 1)
                    if 1 <= s <= NP:
                        g = s - 1
                        bb, q = g // PAIRS, g % PAIRS
                        i = bb % 2
                        act.wait_ge(max_ready, g + 1)
                        if g >= 4:
                            act.wait_ge(pt_done, g - 3)
                        if bb >= B:
                            nc.scalar.activation(pn[:, i, q, :, :], pnarg[:, i, q, :, :], ACT.Exp)
                        for c in range(CB):
                            for h in range(2):
                                ins = nc.scalar.activation(
                                    probs[g % 4][:, c, h, :], ring[:, ring_at["S", g, c] % RING, h * S:(h + 1) * S], ACT.Exp,
                                    bias=negmax[:, i, q, c, h:h + 1], scale=-1.0 if bb < B else nrq[:, i, q, c, h:h + 1],
                                    accum_out=sums[:, i, q, c, h:h + 1])
                            ins.then_inc(ring_free, 1)
                    for e in ring_extras[s]:
                        kind, b, r = e
                        src = ring[:, ring_at[e] % RING, :]
                        act.wait_ge(ring_done, ring_at[e] + 1)
                        c, hf = r // 2, r % 2
                        if kind == "V":
                            if b >= 2 and r == 0:
                                act.wait_ge(o_done, PAIRS * (b - 1))
                            nc.scalar.copy(vtok[b % 2][:, c, hf * 512:(hf + 1) * 512], src).then_inc(ring_free, 1)
                        elif kind == "K":
                            if b >= 1 and r == 0:
                                act.wait_ge(ksum_ready, b)
                            if b >= 2 and r == 0:
                                act.wait_ge(misc_done, misc_at["pair", PAIRS * (B + b - 1) - 1] + 1)
                            nc.scalar.activation(ksq[:, c * H + hf * 8:c * H + hf * 8 + 8, :].rearrange("p h a -> p (h a)"), src, ACT.Square)
                            nc.scalar.copy(ktok[b % 2][:, c, hf * 512:(hf + 1) * 512], src).then_inc(ring_free, 1)
                        elif kind == "Q":
                            if b >= 1 and r == 0:
                                act.wait_ge(ssn_ready, b)
                            if b >= 2 and r == 0:
                                act.wait_ge(ring_done, ring_at["S", PAIRS * (B + b - 1) - 1, 1] + 1)
                            a = src.rearrange("p (a s) -> p a s", a=2)
                            nc.scalar.activation(qsq[:, 2 * r:2 * r + 2, :], a, ACT.Square)
                            nc.scalar.activation(qT_all[b % 2][:, 2 * r:2 * r + 2, :], a, ACT.Copy, scale=nqk[:, 0:1]).then_inc(ring_free, 1)

            @block.tensor
            def _(pe):
                def ring_bank(key):
                    n = ring_at[key]
                    if n >= RING:
                        pe.wait_ge(ring_free, n - RING + 1)
                    return ring[:, n % RING, :]

                def misc_bank(key):
                    if misc_at[key]:
                        pe.wait_ge(misc_free, misc_at[key])

                pe.wait_ge(load_first, 48)
                for s in range(STEPS):
                    if s < NP:
                        bb, q = s // PAIRS, s % PAIRS
                        misc_bank(("pair", s))
                        if s == 2:
                            pe.wait_ge(loadW["A_wq"], 16)
                            pe.wait_ge(loadW["A_wk"], 16)
                        if s == PAIRS - 4:
                            pe.wait_ge(loadX, 16)
                        if bb < B:
                            xb = xTa[:, bb * S:(bb + 1) * S]
                            nc.tensor.matmul(misc[:, 0:S], A_wq[:, q * P:(q + 1) * P], xb, start=True, stop=True)
                            ins = nc.tensor.matmul(misc[:, S:2 * S], A_wk[:, q * P:(q + 1) * P], xb, start=True, stop=True)
                        else:
                            if q == 0:
                                pe.wait_ge(khat_ready, bb - B + 1)
                            for c in range(CB):
                                ins = nc.tensor.transpose(misc[:, c * P:(c + 1) * P], ktok[bb % 2][:, c, q * P:(q + 1) * P], ident[:, :])
                        ins.then_inc(misc_done, 1)
                    if 1 <= s <= NP:
                        g = s - 1
                        bb, q = g // PAIRS, g % PAIRS
                        pe.wait_ge(misc_free, misc_at["pair", g] + 1)
                        qs = qT[g % 2][:, :] if bb < B else qT_all[bb % 2][:, q, :]
                        for c in range(CB):
                            nc.tensor.matmul(ring_bank(("S", g, c)), qs[:, c * P:(c + 1) * P], kz[g % 2][:, :, :], start=True,
                                             stop=True).then_inc(ring_done, 1)
                    for e in misc_extras[s]:
                        kind, b, r = e
                        if kind == "pnT":
                            misc_bank(e)
                            pe.wait_ge(pnt_ready, b + 1)
                            for c in range(CB):
                                ins = nc.tensor.transpose(misc[0:H, c * P:(c + 1) * P], pnt[:, c, :], ident[:, :])
                            ins.then_inc(misc_done, 1)
                        elif kind == "out":
                            c = r
                            misc_bank(e)
                            pe.wait_ge(loadW["A_wo" if b < B else "B_wo"], 16)
                            pe.wait_ge(o_free, PAIRS * (b + 1))
                            wo = A_wo if b < B else B_wo
                            for q in range(PAIRS):
                                ins = nc.tensor.matmul(misc[:, 0:D], oT[b % 2][:, q, c * P:(c + 1) * P], wo[:, q, :],
                                                       start=q == 0, stop=q == PAIRS - 1 and b < B)
                            if b >= B:
                                pe.wait_ge(misc_free, misc_at["pnT", b - B, 0] + 1)
                                ins = nc.tensor.matmul(misc[:, 0:D], pnT[:, c * P:(c + 1) * P], nvwo[:, :], start=False, stop=True)
                            ins.then_inc(misc_done, 1)
                        elif kind in ("X", "CX"):
                            misc_bank(e)
                            pe.wait_ge(xhat_ready if kind == "X" else c_hat_ready, b + 1)
                            for c in range(CB):
                                ins = nc.tensor.transpose(misc[:, c * P:(c + 1) * P], y2[:, c, :], ident[:, :])
                            ins.then_inc(misc_done, 1)
                        elif kind == "C":
                            misc_bank(e)
                            pe.wait_ge(chat, 4 * b + 4)
                            for i in range(4):
                                ins = nc.tensor.transpose(misc[:, i * P:(i + 1) * P], hat[:, 4 * b + i, :], ident[:, :])
                            ins.then_inc(misc_done, 1)
                        elif kind == "NV":
                            misc_bank(e)
                            pe.wait_ge(consts_ready, 3)
                            pe.wait_ge(loadW["B_wo"], 16)
                            for q in range(PAIRS):
                                ins = nc.tensor.matmul(misc[0:H, 0:D], nvz[:, q, :], B_wo[:, q, :], start=q == 0, stop=q == PAIRS - 1)
                            ins.then_inc(misc_done, 1)
                    if TL <= s < NP + TL:
                        g = s - TL
                        pe.wait_ge(norm_done, g + 1)
                        if g == 0:
                            pe.wait_ge(cst, 2)
                        else:
                            pe.wait_ge(pt_free, g)
                        for c in range(CB):
                            for k in range(4):
                                ins = nc.tensor.transpose(ptb[:, c, k * P:(k + 1) * P],
                                                          probs[g % 4][:, c, k // 2, (k % 2) * P:(k % 2 + 1) * P], ident[:, :])
                        ins.then_inc(pt_done, 1)
                    if TL < s <= NP + TL:
                        g = s - TL - 1
                        bb, q = g // PAIRS, g % PAIRS
                        pe.wait_ge(pt_free, g + 1)
                        pe.wait_ge(ring_free, ring_at["V", bb, 3] + 1)
                        if g >= 1:
                            pe.wait_ge(o_free, g)
                        for kc in range(CB):
                            for h in range(2):
                                ins = nc.tensor.matmul(obank[h * A:(h + 1) * A, 0:S], vtok[bb % 2][:, kc, (2 * q + h) * A:(2 * q + h + 1) * A],
                                                       probsT[g % 2][:, h, kc, :], start=kc == 0, stop=kc == CB - 1)
                        if s in ssq_at:
                            b, r = ssq_at[s]
                            ss = obank[:, S:S + 8 * PAIRS]
                            pe.wait_ge(ring_free, ring_at["Q", b, r] + 1)
                            if r == 0:
                                pe.wait_ge(null_ready, 1)
                                for c in range(CB):
                                    nullc = ss[:, 4 * PAIRS:].rearrange("p (a c h) -> p a c h", c=CB, h=2)[:, :, c, :]
                                    j = b * CB + c
                                    nc.tensor.matmul(nullc, xn_all[:, j * P:(j + 1) * P], wnull[:, :].rearrange("p (a h) -> p a h", h=2),
                                                     start=True, stop=True)
                            for p in (2 * r, 2 * r + 1):
                                for c in range(CB):
                                    o = 4 * p + 2 * c
                                    ins = nc.tensor.matmul(ss[:, o:o + 2], qsq[:, p, c * P:(c + 1) * P], blk[:, :], start=True, stop=True)
                        ins.then_inc(o_done, 1)
                    for e in ring_extras[s]:
                        kind, b, r = e
                        c, hf = r // 2, r % 2
                        if kind == "V":
                            pe.wait_ge(loadW["A_wv" if b < B else "B_wkv"], 16)
                            j = (b % B) * CB + c
                            src = (xTa if b < B else cn_all)[:, j * P:(j + 1) * P]
                            w = A_wv[:, hf * 512:(hf + 1) * 512] if b < B else B_wkv[:, H * A + hf * 512:H * A + (hf + 1) * 512]
                            nc.tensor.matmul(ring_bank(e), src, w, start=True, stop=True).then_inc(ring_done, 1)
                        elif kind == "K":
                            pe.wait_ge(loadW["B_wkv"], 16)
                            j = b * CB + c
                            if b == 0:
                                pe.wait_ge(misc_free, misc_at["C", 1, 0] + 1)
                            nc.tensor.matmul(ring_bank(e), cn_all[:, j * P:(j + 1) * P], B_wkv[:, hf * 512:(hf + 1) * 512], start=True,
                                             stop=True).then_inc(ring_done, 1)
                        elif kind == "Q":
                            pe.wait_ge(loadW["B_wq"], 16)
                            pe.wait_ge(misc_free, misc_at["X", b, 0] + 1)
                            bank = ring_bank(e)
                            for k in range(2):
                                p = 2 * r + k
                                ins = nc.tensor.matmul(bank[:, k * S:(k + 1) * S], B_wq[:, p * P:(p + 1) * P], xn_all[:, b * S:(b + 1) * S],
                                                       start=True, stop=True)
                            ins.then_inc(ring_done, 1)

            @block.vector
            def _(dve):
                ch = Chain(dve, wide_dve)
                dve.wait_ge(loadC, 16)
                nc.vector.tensor_scalar(cols[:, 0:PAIRS], cols[:, 0:PAIRS], -float(A) ** -0.5, None, ALU.mult).then_inc(consts_ready, 1)
                for i in range(2):
                    ins = nc.vector.memset(kz[i][:, :, :], 0.0)
                ins.then_inc(consts_ready, 1)
                ch.step(nc.vector.memset(blk[:, :], 0.0))
                nc.vector.memset(blk[0:A, 0:1], 1.0)
                nc.vector.memset(blk[A:P, 1:2], 1.0)

                lns = [0]

                def ln_begin(src):
                    i = lns[0] % 2
                    for c in range(CB):
                        ins = nc.vector.bn_stats(lst[:, c, :], src[:, c, :])
                    ch.step(ins)
                    for c in range(CB):
                        ins = nc.vector.bn_aggr(lmv[:, i, c, :], lst[:, c, :])
                    ins.then_inc(var_ready, 1)
                    lns[0] += 1

                def ln_end(dst, src):
                    i = (lns[0] - 1) % 2
                    dve.wait_ge(rstd_ready, lns[0])
                    for c in range(CB):
                        ins = nc.vector.tensor_scalar(dst[:, c, :], src[:, c, :], lmv[:, i, c, 0:1], lrs[:, i, c:c + 1], ALU.subtract, ALU.mult)
                    return ins

                for s in range(STEPS):
                    if TL < s <= NP + TL:
                        g = s - TL - 1
                        if g >= 2:
                            dve.wait_ge(o_done, g - 1)
                        dve.wait_ge(pt_done, g + 1)
                        nc.vector.tensor_copy(probsT[g % 2][:, :, :, :].rearrange("p h k (c q) -> p c (h k) q", c=CB),
                                              ptb[:, :, :].rearrange("p c (k q) -> p c k q", q=P)).then_inc(pt_free, 1)
                    if 2 <= s <= NP + 1:
                        g = s - 2
                        bb, q = g // PAIRS, g % PAIRS
                        i = bb % 2
                        dve.wait_ge(ring_free, ring_at["S", g, CB - 1] + 1)
                        if bb >= B:
                            ch.step(nc.vector.tensor_tensor(sums[:, i, q, :, :], sums[:, i, q, :, :], pn[:, i, q, :, :], ALU.add))
                        ch.step(nc.vector.reciprocal(rsum[:, i, q, :, :], sums[:, i, q, :, :]))
                        for c in range(CB):
                            for h in range(2):
                                a = probs[g % 4][:, c, h, :]
                                ins = nc.vector.tensor_scalar(a, a, rsum[:, i, q, c, h:h + 1], None, ALU.mult)
                        ins.then_inc(norm_done, 1)
                    if 1 <= s <= NP:
                        g = s - 1
                        bb, q = g // PAIRS, g % PAIRS
                        i = bb % 2
                        dve.wait_ge(ring_done, ring_at["S", g, CB - 1] + 1)
                        r = ring_at["S", g, 0] % RING
                        dst = negmax if bb < B else mins
                        if r + CB <= RING:
                            ins = nc.vector.tensor_reduce(dst[:, i, q, :, :], ring[:, r:r + CB, :].rearrange("p c (h k) -> p c h k", h=2), AX.X, ALU.min)
                        else:
                            for c in range(CB):
                                r = ring_at["S", g, c] % RING
                                ins = nc.vector.tensor_reduce(dst[:, i, q, c, :], ring[:, r, :].rearrange("p (h k) -> p h k", h=2), AX.X, ALU.min)
                        if bb >= B:
                            if q == 0:
                                dve.wait_ge(rq_ready, bb - B + 1)
                            ch.step(ins)
                            ch.step(nc.vector.tensor_tensor(mins[:, i, q, :, :], mins[:, i, q, :, :], nulls(bb - B, q), ALU.min))
                            ch.step(nc.vector.tensor_tensor(negmax[:, i, q, :, :], mins[:, i, q, :, :], prq[:, i, q, :, :], ALU.mult))
                            ins = nc.vector.tensor_tensor(pnarg[:, i, q, :, :], negmax[:, i, q, :, :], snr[:, i, q, :, :], ALU.add)
                        ins.then_inc(max_ready, 1)
                    for e in misc_extras[s]:
                        kind, b, r = e
                        if kind == "out":
                            dve.wait_ge(misc_done, misc_at[e] + 1)
                            if b < B:
                                nc.vector.tensor_tensor(y[:, r, :], misc[:, 0:D], x_res[:, CB * b + r, :], ALU.add).then_inc(misc_free, 1)
                            else:
                                nc.vector.tensor_copy(y[:, r, :], misc[:, 0:D]).then_inc(misc_free, 1)
                            if r == CB - 1:
                                dve.wait_ge(misc_free, misc_at[e] + 1)
                                ln_begin(y)
                        elif kind in ("X", "CX"):
                            gain, bias = ("B_in_g", "B_in_b") if kind == "X" else ("C_ln1_g", "C_ln1_b")
                            dve.wait_ge(misc_done, misc_at[e] + 1)
                            nc.vector.tensor_scalar(xn_all[:, b * S:(b + 1) * S], misc[:, 0:S], col(gain), col(bias), ALU.mult,
                                                    ALU.add).then_inc(misc_free, 1)
                        elif kind == "C":
                            dve.wait_ge(misc_done, misc_at[e] + 1)
                            nc.vector.tensor_scalar(cn_all[:, b * 512:(b + 1) * 512], misc[:, :], col("B_ctx_g"), col("B_ctx_b"), ALU.mult,
                                                    ALU.add).then_inc(misc_free, 1)
                        elif kind == "NV":
                            dve.wait_ge(misc_done, misc_at[e] + 1)
                            nc.vector.tensor_copy(nvwo[:, :], misc[0:H, 0:D]).then_inc(misc_free, 1)
                    for e in dve_extras[s]:
                        kind, b = e
                        xb = x_res[:, CB * (b % B):CB * (b % B) + CB, :]
                        k3 = ktok[b % 2][:, :, :].rearrange("p c (h a) -> p (c h) a", a=A)
                        if kind == "ctx_norm":
                            dve.wait_ge(loadA, 48)
                            ln_stats(ch, lambda i: ctx_tok[:, i, :], NC).then_inc(cstat, 1)
                            ch.step(nc.vector.tensor_tensor(x_res[:, :, :], x_res[:, :, :], rowb("A_bo", NC), ALU.add))
                        elif kind == "ctx_hat":
                            dve.wait_ge(crstd, 1)
                            for i in range(NC):
                                nc.vector.tensor_scalar(hat[:, i, :], ctx_tok[:, i, :], mv[:, i, 0:1], rstd[:, i:i + 1], ALU.subtract, ALU.mult)\
                                    .then_inc(chat, 1)
                        elif kind == "null_value":
                            ch.step(nc.vector.memset(nvz[:, :, :], 0.0))
                            flat = nvz[:, :, :].rearrange("p a h -> p (a h)")
                            n = (PAIRS - 1) * (H + 2) + 1
                            nc.vector.tensor_copy(flat[0:A, 0:n:H + 2], col("B_nv", 0, 0, A).broadcast_to([A, PAIRS]))
                            nc.vector.tensor_copy(flat[A:P, 1:1 + n:H + 2], col("B_nv", 0, A, P).broadcast_to([A, PAIRS])).then_inc(consts_ready, 1)
                            nc.vector.tensor_scalar(col("C_bq"), col("C_bq"), -float(HD) ** -0.5, None, ALU.mult)
                            nc.vector.scalar_tensor_tensor(nqk[:, :], col("B_qs"), -1.0, col("B_ks"), ALU.mult, ALU.mult)
                        elif kind == "null_key":
                            ch.step(nc.vector.tensor_tensor(nkr[:, :], row("B_nk"), row("B_nk"), ALU.mult))
                            ch.step(nc.vector.tensor_reduce(nks[:, :], nkr[:, :], AX.X, ALU.add))
                            nc.vector.tensor_scalar(nks[:, :], nks[:, :], NORM_EPS ** 2, None, ALU.max).then_inc(null_ss, 1)
                            dve.wait_ge(null_pow, 1)
                            dve.wait_ge(loadW["B_wq"], 16)
                            ch.step(nc.vector.tensor_scalar(nkr[:, :], row("B_nk"), nks[:, 0:1], -1.0, ALU.mult, ALU.mult))
                            ch.step(nc.vector.tensor_tensor(nkr[:, :], nkr[:, :], row("B_qsr"), ALU.mult))
                            ch.step(nc.vector.tensor_tensor(nkr[:, :], nkr[:, :], row("B_ksr"), ALU.mult))
                            ch.step(nc.vector.tensor_tensor(wtmp, B_wq[:, :].rearrange("p (h a) -> p h a", a=A),
                                                            nkr[:, :].unsqueeze(1).broadcast_to([P, H, A]), ALU.mult))
                            nc.vector.tensor_reduce(wnull[:, :], wtmp, AX.X, ALU.add).then_inc(null_ready, 1)
                        elif kind == "ksum":
                            dve.wait_ge(ring_free, ring_at["K", b, 3] + 1)
                            ch.step(nc.vector.tensor_reduce(kss[:, :], ksq[:, :, :], AX.X, ALU.add))
                            nc.vector.tensor_scalar(kss[:, :], kss[:, :], NORM_EPS ** 2, None, ALU.max).then_inc(ksum_ready, 1)
                        elif kind == "khat":
                            dve.wait_ge(krn_ready, b + 1)
                            nc.vector.tensor_tensor(k3, k3, krn[:, :].unsqueeze(2).broadcast_to([P, CB * H, A]), ALU.mult).then_inc(khat_ready, 1)
                        elif kind == "qsum":
                            dve.wait_ge(ssn_ready, b + 1)
                            nc.vector.tensor_scalar(rqt[:, :], ssn[:, b % 2, 0:4 * PAIRS], NORM_EPS ** 2, None, ALU.max).then_inc(qsum_ready, 1)
                        elif kind == "pnt":
                            nc.vector.tensor_tensor(pnt[:, :, :].rearrange("p c (a h) -> p a c h", h=2), pn[:, b % 2, :, :, :],
                                                    rsum[:, b % 2, :, :, :], ALU.mult).then_inc(pnt_ready, 1)
                        elif kind == "apply":
                            if b < B:
                                ch.step(ln_end(xb, y))
                            else:
                                ch.step(ln_end(y2, y))
                                ch.step(nc.vector.tensor_tensor(y2[:, :, :], y2[:, :, :], rowb("B_out_g", CB), ALU.mult))
                                ch.step(nc.vector.tensor_tensor(y2[:, :, :], y2[:, :, :], rowb("B_out_b", CB), ALU.add))
                                ch.step(nc.vector.tensor_tensor(y[:, :, :], y2[:, :, :], xb, ALU.add))
                                ln_begin(y)
                        elif kind == "apply2":
                            ch.step(ln_end(xb, y))
                        elif kind in ("xnorm", "cnorm"):
                            ln_begin(xb)
                        elif kind in ("xhat", "chat"):
                            ln_end(y2, xb).then_inc(xhat_ready if kind == "xhat" else c_hat_ready, 1)

            @block.gpsimd
            def _(pool):
                nc.gpsimd.memset(ident[:, :], 0.0).then_inc(cst, 1)
                pool.wait_ge(cst, 1)
                nc.gpsimd.affine_select(out=ident[:, :], in_=ident[:, :], compare_op=ALU.not_equal, fill=1.0,
                                        base=0, pattern=[[-1, P]], channel_multiplier=1).then_inc(cst, 1)
                for k, value in enumerate(CONSTS):
                    nc.gpsimd.memset(const[:, k, :], value).then_inc(cst, 1)
                pool.wait_ge(cst, 2 + len(CONSTS))
                ch = Chain(pool, wide_pool)
                pool.wait_ge(cstat, 1)
                ln_power(ch, NC).then_inc(crstd, 1)
                pool.wait_ge(null_ss, 1)
                nc.gpsimd.tensor_tensor(nks[:, :], nks[:, :], half[:, 0:1], ALU.pow).then_inc(null_pow, 1)
                ch.step(nc.gpsimd.memset(hmask[:, :], 1.0))
                ch.step(nc.gpsimd.affine_select(out=hmask[:, :], in_=hmask[:, :], compare_op=ALU.is_ge, fill=0.0,
                                                base=0, pattern=[[-HD, H]], channel_multiplier=1))
                nc.gpsimd.affine_select(out=hmask[:, :], in_=hmask[:, :], compare_op=ALU.is_ge, fill=0.0,
                                        base=HD - 1, pattern=[[HD, H]], channel_multiplier=-1)
                ch.step(nc.gpsimd.memset(causal[:, :], 0.0))
                nc.gpsimd.affine_select(out=causal[:, :], in_=causal[:, :], compare_op=ALU.is_ge, fill=MASKED,
                                        base=0, pattern=[[-1, P]], channel_multiplier=1)
                nc.gpsimd.tensor_copy(identb[:, :], ident[:, :])
                lns = 0
                for s in range(STEPS):
                    for kind, b, r in misc_extras[s]:
                        if kind == "out" and r == CB - 1:
                            lns = ln_rstd(pool, ch, lns)
                    for kind, b in dve_extras[s]:
                        if kind == "ksum":
                            pool.wait_ge(ksum_ready, b + 1)
                            nc.gpsimd.tensor_tensor(krn[:, :], kss[:, :], half[:, 0:CB * H], ALU.pow).then_inc(krn_ready, 1)
                        elif kind == "qsum":
                            def flat(x):
                                return x[:, b % 2, :, :, :].rearrange("p a c h -> p (a c h)")
                            pool.wait_ge(qsum_ready, b + 1)
                            ch.step(nc.gpsimd.tensor_tensor(rqt[:, :], rqt[:, :], half[:, 0:4 * PAIRS], ALU.pow))
                            nc.gpsimd.tensor_tensor(flat(prq), rqt[:, :], const[:, 2, 0:4 * PAIRS], ALU.mult)
                            ch.step(nc.gpsimd.tensor_tensor(flat(nrq), rqt[:, :], const[:, 3, 0:4 * PAIRS], ALU.mult))
                            nc.gpsimd.tensor_tensor(flat(snr), flat(nrq), ssn[:, b % 2, 4 * PAIRS:], ALU.mult).then_inc(rq_ready, 1)
                        if kind in ("xnorm", "cnorm") or (kind == "apply" and b >= B):
                            lns = ln_rstd(pool, ch, lns)

        wide.close()
        scope[0] = ctx

        if upto > 1:
            G = 4
            NG = H // G
            NGR = B * NG
            CT = 2
            tiles = [(range(0, 4), 0), (range(0, 2), 1), (range(2, 4), 1)]
            stat_of = [0, 4, 6]
            VW = 32
            TU = len(tiles)
            loadF = sem("loadF")
            loadE = [sem(f"loadE{e}") for e in range(E)]
            D_w = sb("D_w", [P, 3 * D])
            F_w1, F_w2 = sb("F_w1", [P, FF]), sb("F_w2", [P, FF])
            F_h1, F_h2, F_w3 = sb("F_h1", [P, FC, FF]), sb("F_h2", [P, FC, FF]), sb("F_w3", [P, FC, D])
            ctxT = sb("ctxT", [P, B, S])
            M_w1, M_w2, M_b1 = sb("M_w1", [P, E, FF]), sb("M_w2", [P, E, FC, D]), sb("M_b1", [P, E, FC])
            logits = sb("logits", [P, NC, E])
            lmv2, lve2, lrs2 = sb("lmv2", [P, B, CB, 2]), sb("lve2", [P, B, CB]), sb("lrs2", [P, B, CB])
            narrow = ctx.enter_context(ExitStack())
            scope[0] = narrow
            qTc, kTc = sb("qTc", [P, NC * P]), sb("kTc", [P, NC * P])
            vtn = sb("vtn", [P, NC, H, VW])
            oT4 = [sb(f"oT4_{i}", [P, S]) for i in range(2)]
            kzn = [sb(f"kzn{i}", [P, H, S]) for i in range(2)]
            PR = 4
            pr = sb("pr", [P, PR, TU, 512])
            prT = [sb(f"prT{i}", [P, G, CB, S]) for i in range(2)]
            oN = sb("oN", [P, 2, CB, D])
            oTn = sb("oTn", [P, 2, S])
            nmax, nrs = sb("nmax", [P, NGR, 8]), sb("nrs", [P, NGR, 8])
            x1 = sb("x1", [P, 2, CB, D])

            FIRST = -3
            CSTEPS = NGR + CT + 6
            c_extras = {s: [] for s in range(FIRST, CSTEPS)}
            c_dve = {s: [] for s in range(FIRST, CSTEPS)}
            for b in range(B):
                s0 = NG * b
                c_extras[s0 - 3].insert(0, ("QK", b))
                c_extras[s0 - 1].insert(0, ("V", b))
                c_extras[s0 + NG + CT + 2].append(("OT", b))
                c_extras[s0 + NG + CT + 3].append(("OUT", b))
                c_dve[s0 + NG + CT + 4].append(("hat", b))
                late = int(b < B - 1)
                c_extras[s0 + NG + CT + 4 + late].append(("X2", b))
                c_extras[s0 + NG + CT + 5 + late].append(("GATE", b))
            c_misc_at = {e: n for n, e in enumerate(e for s in range(FIRST, CSTEPS) for e in c_extras[s])}

            (c_ring_done, c_ring_free, c_misc_done, c_misc_free, c_max, c_pt_done, c_pt_free, c_o_done, c_o_free, c_ot_done, c_ot_free, c_ones, kz_dve, kz_act, kz_pool,
             c_var, c_rstd, c_xhat, c_dve_steps, c_pool_steps) = map(sem, [
                 "c_ring_done", "c_ring_free", "c_misc_done", "c_misc_free", "c_max", "c_pt_done", "c_pt_free", "c_o_done", "c_o_free", "c_ot_done", "c_ot_free", "c_ones",
                 "kz_dve", "kz_act", "kz_pool", "c_var", "c_rstd", "c_xhat", "c_dve_steps", "c_pool_steps"])
            with nc.Block() as block:
                @block.sync
                def _(sp):
                    for e in range(E):
                        for dst, src in [(M_w1[:, e, :], t["M_w1"][e]), (M_b1[:, e, :], t["M_b1"][e]), (M_w2[:, e, :, :], t["M_w2"][e])]:
                            sp.dma_start(dst, src).then_inc(loadE[e], 16)
                    for dst, src in [(D_w[:, :], t["D_w"]), (ctxT[:, :, :], t["ctxT"].rearrange("b p s -> p b s")),
                                     (F_w1[:, :], t["F_w1"]), (F_w2[:, :], t["F_w2"]), (F_h1[:, :, :], t["F_h1"]),
                                     (F_h2[:, :, :], t["F_h2"]), (F_w3[:, :, :], t["F_w3"])]:
                        sp.dma_start(dst, src).then_inc(loadF, 16)

                @block.tensor
                def _(pe):
                    pe.wait_ge(loadN, 96)
                    for s in range(FIRST, CSTEPS):
                        for u, (heads, c) in enumerate(tiles):
                            if 0 <= s < NGR:
                                b, q = s // NG, s % NG
                                if u == 0:
                                    for ready in (kz_dve, kz_act, kz_pool):
                                        pe.wait_ge(ready, s + 1)
                                n = TU * s + u
                                if n >= RING:
                                    pe.wait_ge(c_ring_free, n - RING + 1)
                                h0, nh, nk = G * q + heads[0], len(heads), (c + 1) * P
                                j = b * CB + c
                                nc.tensor.matmul(ring[:, n % RING, :], qTc[:, j * P:(j + 1) * P], kzn[b % 2][:, h0:h0 + nh, 0:nk],
                                                 start=True, stop=True)
                                nc.tensor.matmul(ring[:, n % RING, :].rearrange("p (h k) -> p h k", h=nh)[:, :, c * P:nk], identb[:, :],
                                                 causal[:, :].unsqueeze(1).broadcast_to([P, nh, P]), start=False, stop=True,
                                                 skip_group_check=True).then_inc(c_ring_done, 1)
                            if CT <= s < NGR + CT:
                                g = s - CT
                                n = TU * g + u
                                pe.wait_ge(c_ring_free, n + 1)
                                if n >= 2:
                                    pe.wait_ge(c_pt_free, n - 1)
                                for k in range(4):
                                    ins = nc.tensor.transpose(ptb[:, n % 2, k * P:(k + 1) * P], pr[:, g % PR, u, k * P:(k + 1) * P], ident[:, :])
                                ins.then_inc(c_pt_done, 1)
                            if u == 0 and CT + 1 < s <= NGR + CT + 1:
                                g = s - CT - 2
                                pe.wait_ge(c_o_free, g + 1)
                                for c in range(CB):
                                    ins = nc.tensor.transpose(obank[:, S + c * P:S + (c + 1) * P], oT4[g % 2][:, c * P:(c + 1) * P], ident[:, :])
                                ins.then_inc(c_ot_done, 1)
                        if CT < s <= NGR + CT:
                            g = s - CT - 1
                            b, q = g // NG, g % NG
                            pe.wait_ge(c_pt_free, TU * (g + 1))
                            pe.wait_ge(c_misc_free, c_misc_at["V", b] + 1)
                            pe.wait_ge(c_ones, b + 1)
                            if g >= 1:
                                pe.wait_ge(c_ot_free, g)
                            for kc in range(CB):
                                for j in range(G):
                                    ins = nc.tensor.matmul(obank[VW * j:VW * j + VW, kc * P:S], vtn[:, b * CB + kc, G * q + j, :],
                                                           prT[g % 2][:, j, kc, kc * P:S], start=kc == 0, stop=True, skip_group_check=True)
                            ins.then_inc(c_o_done, 1)
                        for e in c_extras[s]:
                            kind, b = e
                            if c_misc_at[e]:
                                pe.wait_ge(c_misc_free, c_misc_at[e])
                            xb = xn_all[:, b * S:(b + 1) * S]
                            if kind == "QK":
                                nc.tensor.matmul(misc[:, 0:S], C_wq[:, :], xb, start=True, stop=True)
                                ins = nc.tensor.matmul(misc[:, S:2 * S], C_wk[:, :], xb, start=True, stop=True)
                            for c in range(CB):
                                xc = xn_all[:, b * S + c * P:b * S + (c + 1) * P]
                                out = misc[:, c * P:(c + 1) * P]
                                if kind == "V":
                                    ins = nc.tensor.matmul(out, xc, C_wv[:, :], start=True, stop=True)
                                elif kind == "OT":
                                    if c == 0:
                                        pe.wait_ge(c_ot_free, NG * (b + 1))
                                    ins = nc.tensor.transpose(out, oN[:, b % 2, c, :], ident[:, :])
                                elif kind == "OUT":
                                    if c == 0:
                                        pe.wait_ge(c_misc_free, c_misc_at["OT", b] + 1)
                                    ins = nc.tensor.matmul(out, oTn[:, b % 2, c * P:(c + 1) * P], C_wp[:, :], start=True, stop=True)
                                elif kind == "X2":
                                    if c == 0:
                                        pe.wait_ge(c_xhat, b + 1)
                                    ins = nc.tensor.transpose(out, hat[:, CB * b + c, :], ident[:, :])
                                elif kind == "GATE":
                                    if c == 0:
                                        pe.wait_ge(c_misc_free, c_misc_at["X2", b] + 1)
                                    ins = nc.tensor.matmul(misc[:, c * E:(c + 1) * E], xc, M_gw[:, :], start=True, stop=True)
                            ins.then_inc(c_misc_done, 1)

                @block.scalar
                def _(act):
                    for s in range(FIRST, CSTEPS):
                        if -1 <= s < NGR - 1:
                            g = s + 1
                            b, h = g // NG, G * (g % NG) + 3
                            act.wait_ge(c_misc_free, c_misc_at["QK", b] + 1)
                            nc.scalar.activation(kzn[b % 2][:, h, :], kTc[:, b * S:(b + 1) * S], ACT.Copy, scale=hmask[:, h:h + 1])\
                                .then_inc(kz_act, 1)
                        if 0 <= s < NGR:
                            for u, (heads, c) in enumerate(tiles):
                                n = TU * s + u
                                nh, nk = len(heads), (c + 1) * P
                                act.wait_ge(c_max, n + 1)
                                if s >= PR:
                                    act.wait_ge(c_pt_done, n - TU * PR + 1)
                                for k in range(nh):
                                    m = stat_of[u] + k
                                    ins = nc.scalar.activation(pr[:, s % PR, u, k * nk:(k + 1) * nk], ring[:, n % RING, k * nk:(k + 1) * nk],
                                                               ACT.Exp, bias=nmax[:, s, m:m + 1], scale=-1.0)
                                ins.then_inc(c_ring_free, 1)
                        if CT < s <= NGR + CT:
                            g = s - CT - 1
                            act.wait_ge(c_o_done, g + 1)
                            if g >= 2:
                                act.wait_ge(c_ot_done, g - 1)
                            nc.scalar.copy(oT4[g % 2][:, :], obank[:, 0:S]).then_inc(c_o_free, 1)
                        for e in c_extras[s]:
                            kind, b = e
                            if kind in ("QK", "V", "OT"):
                                act.wait_ge(c_misc_done, c_misc_at[e] + 1)
                            if kind == "QK":
                                nc.scalar.activation(kTc[:, b * S:(b + 1) * S], misc[:, S:2 * S], ACT.Identity, bias=col("C_bk"))
                                ins = nc.scalar.activation(qTc[:, b * S:(b + 1) * S], misc[:, 0:S], ACT.Identity, bias=col("C_bq"),
                                                           scale=-float(HD) ** -0.5)
                            elif kind == "V":
                                act.wait_ge(c_ones, b + 1)
                                ins = nc.scalar.copy(vtn[:, CB * b:CB * b + CB, :, 0:HD], misc[:, 0:S].rearrange("p (c h d) -> p c h d", c=CB, d=HD))
                            elif kind == "OT":
                                ins = nc.scalar.activation(oTn[:, b % 2, :], misc[:, 0:S], ACT.Identity, bias=col("C_bv"))
                            if kind in ("QK", "V", "OT"):
                                ins.then_inc(c_misc_free, 1)

                @block.vector
                def _(dve):
                    ch = Chain(dve, c_dve_steps)
                    for s in range(FIRST, CSTEPS):
                        if (s + 2) % NG == 0 and s < NGR - 2:
                            b = (s + 2) // NG
                            vb = vtn[:, CB * b:CB * b + CB, :, :]
                            ch.step(nc.vector.memset(vb, 0.0))
                            nc.vector.memset(vb[:, :, :, HD], 1.0).then_inc(c_ones, 1)
                        if -1 <= s < NGR - 1:
                            g = s + 1
                            b, h = g // NG, G * (g % NG)
                            dve.wait_ge(c_misc_free, c_misc_at["QK", b] + 1)
                            nc.vector.tensor_scalar(kzn[b % 2][:, h, :], kTc[:, b * S:(b + 1) * S], hmask[:, h:h + 1], None, ALU.mult)\
                                .then_inc(kz_dve, 1)
                        for u, (heads, c) in enumerate(tiles):
                            if 0 <= s < NGR:
                                n = TU * s + u
                                dve.wait_ge(c_ring_done, n + 1)
                                nc.vector.tensor_reduce(nmax[:, s, stat_of[u]:stat_of[u] + len(heads)],
                                                        ring[:, n % RING, :].rearrange("p (h k) -> p h k", h=len(heads)), AX.X, ALU.min)\
                                    .then_inc(c_max, 1)
                            if CT <= s < NGR + CT:
                                g = s - CT
                                if g >= 2 and u == 0:
                                    dve.wait_ge(c_o_done, g - 1)
                                n = TU * g + u
                                dve.wait_ge(c_pt_done, n + 1)
                                src = ptb[:, n % 2, :].rearrange("p (h q) -> p h q", q=P)
                                if c == 0:
                                    dst = prT[g % 2][:, :, 0, 0:P]
                                else:
                                    dst = prT[g % 2][:, heads[0]:heads[0] + 2, :, P:S].rearrange("p h k q -> p (h k) q")
                                nc.vector.tensor_copy(dst, src).then_inc(c_pt_free, 1)
                            if u == 0 and CT + 1 < s <= NGR + CT + 1:
                                g = s - CT - 2
                                b, q = g // NG, g % NG
                                prod4 = obank[:, S:2 * S].rearrange("p (c h v) -> p c h v", c=CB, v=VW)
                                rs = nrs[:, g, :].rearrange("p (c h) -> p c h", c=CB)
                                dve.wait_ge(c_ot_done, g + 1)
                                ch.step(nc.vector.reciprocal(rs, prod4[:, :, :, HD]))
                                if b >= 2 and q == 0:
                                    dve.wait_ge(c_misc_done, c_misc_at["OT", b - 2] + 1)
                                nc.vector.tensor_tensor(oN[:, b % 2, :, G * q * HD:G * (q + 1) * HD].rearrange("p c (h d) -> p c h d", d=HD),
                                                        prod4[:, :, :, 0:HD], rs.unsqueeze(3).broadcast_to([P, CB, G, HD]), ALU.mult)\
                                    .then_inc(c_ot_free, 1)
                        for kind, b in c_dve[s]:
                            dve.wait_ge(c_rstd, b + 1)
                            for c in range(CB):
                                ins = nc.vector.tensor_scalar(hat[:, CB * b + c, :], x1[:, b % 2, c, :], lmv2[:, b, c, 0:1], lrs2[:, b, c:c + 1],
                                                              ALU.subtract, ALU.mult)
                            ins.then_inc(c_xhat, 1)
                        for e in c_extras[s]:
                            kind, b = e
                            if kind in ("OUT", "X2", "GATE"):
                                dve.wait_ge(c_misc_done, c_misc_at[e] + 1)
                            xb = x_res[:, CB * b:CB * b + CB, :]
                            if kind == "OUT":
                                nc.vector.tensor_tensor(y[:, :, :], misc[:, 0:CB * D].rearrange("p (c d) -> p c d", c=CB),
                                                        rowb("C_bp", CB), ALU.add).then_inc(c_misc_free, 1)
                                dve.wait_ge(c_misc_free, c_misc_at[e] + 1)
                                ch.step(nc.vector.tensor_tensor(x1[:, b % 2, :, :], y[:, :, :], xb, ALU.add))
                                nc.vector.tensor_tensor(xb, x1[:, b % 2, :, :], xb, ALU.add)
                                for c in range(CB):
                                    ins = nc.vector.bn_stats(st[:, c, :], x1[:, b % 2, c, :])
                                ch.step(ins)
                                for c in range(CB):
                                    ins = nc.vector.bn_aggr(lmv2[:, b, c, :], st[:, c, :])
                                ins.then_inc(c_var, 1)
                            elif kind == "X2":
                                nc.vector.tensor_scalar(xn_all[:, b * S:(b + 1) * S], misc[:, 0:S], col("C_ln2_g"), col("C_ln2_b"), ALU.mult,
                                                        ALU.add).then_inc(c_misc_free, 1)
                            elif kind == "GATE":
                                nc.vector.tensor_tensor(logits[:, CB * b:CB * b + CB, :], misc[:, 0:CB * E].rearrange("p (c e) -> p c e", c=CB),
                                                        rowb("M_gb", CB), ALU.add).then_inc(c_misc_free, 1)

                @block.gpsimd
                def _(pool):
                    ch = Chain(pool, c_pool_steps)
                    for s in range(FIRST, CSTEPS):
                        if -1 <= s < NGR - 1:
                            g = s + 1
                            b, h = g // NG, G * (g % NG) + 1
                            pool.wait_ge(c_misc_free, c_misc_at["QK", b] + 1)
                            if b >= 2:
                                pool.wait_ge(c_ring_done, TU * (g - 2 * NG + 1))
                            nc.gpsimd.tensor_tensor(kzn[b % 2][:, h:h + 2, :], kTc[:, b * S:(b + 1) * S].unsqueeze(1).broadcast_to([P, 2, S]),
                                                    hmask[:, h:h + 2].unsqueeze(2).broadcast_to([P, 2, S]), ALU.mult).then_inc(kz_pool, 1)
                        for kind, b in c_extras[s]:
                            if kind == "OUT":
                                pool.wait_ge(c_var, b + 1)
                                ch.step(nc.gpsimd.tensor_tensor(lve2[:, b, :], lmv2[:, b, :, 1], const[:, 1, 0:CB], ALU.add))
                                nc.gpsimd.tensor_tensor(lrs2[:, b, :], lve2[:, b, :], half[:, 0:CB], ALU.pow).then_inc(c_rstd, 1)
            narrow.close()
            scope[0] = ctx

            U = 2 * E
            HT = NC // 2
            HB = B // 2
            steps = []
            for u in range(U):
                steps.append(("mid", u, 0))
                if u:
                    steps.append(("out", u - 1, 0))
            steps.append(("out", U - 1, 0))
            for hf in range(2):
                steps += [("gated", hf, i) for i in range(FC)]
                steps += [("hid1", hf, i) for i in range(FC)] + [("hid2", hf, i) for i in range(FC)]
                steps.append(("last", hf, 0))
            before = {e: [] for e in steps + [("end", 0, 0)]}
            before["mid", 1, 0] += [("gate", 0, 0)]
            before["out", 0, 0] += [("wT", 0, 0), ("wT", 1, 0)]
            before["mid", 2, 0] += [("b2", 0, 0), ("b2", 1, 0)]
            for hf, at in enumerate([
                    {"ln_c": ("mid", 9, 0), "le_c": ("mid", 9, 0), "T_c": ("mid", 10, 0), "proj": ("out", 9, 0), "score": ("out", 9, 0),
                     "mix": ("out", 10, 0), "ln_d": ("mid", 12, 0), "le_d": ("mid", 12, 0), "T_d": ("out", 12, 0), "gate1": ("mid", 14, 0),
                     "gate2": ("out", 13, 0), "ln_e": ("mid", 15, 0), "le_e": ("mid", 15, 0), "T_e": ("out", 15, 0),
                     "fin": ("gated", 1, 1), "ln_f": ("gated", 1, 2), "le_f": ("gated", 1, 3)},
                    {"ln_c": ("gated", 0, 0), "le_c": ("gated", 0, 1), "T_c": ("gated", 0, 3), "proj": ("hid1", 0, 0), "score": ("hid1", 0, 0),
                     "mix": ("hid1", 0, 2), "ln_d": ("hid1", 0, 2), "le_d": ("hid1", 0, 2), "T_d": ("hid2", 0, 1), "gate1": ("hid2", 0, 2),
                     "gate2": ("hid2", 0, 3), "ln_e": ("hid2", 0, 3), "le_e": ("hid2", 0, 3), "T_e": ("gated", 1, 0),
                     "fin": ("end", 0, 0), "ln_f": ("end", 0, 0), "le_f": ("end", 0, 0)}]):
                for name, e in at.items():
                    n = HT if name == "proj" else HB if name == "gate1" else 1
                    before[e] += [(name, hf, i) for i in range(n)]
            ORDER = steps + [("end", 0, 0)]
            x_at, t_ring_at, ln_at = {}, {}, {}
            for e in ORDER:
                for f in before[e]:
                    if f[0] in ("wT", "b2", "T_c", "proj", "T_d", "gate1", "gate2", "T_e"):
                        x_at[f] = len(x_at)
                    if f[0].startswith("ln_"):
                        ln_at[f] = len(ln_at)
                kind, u, i = e
                if kind == "mid":
                    for hc in range(FC):
                        t_ring_at["mid", u, hc] = len(t_ring_at)
                elif kind == "gated":
                    for w in range(2):
                        t_ring_at["gated", u, i, w] = len(t_ring_at)
                elif kind in ("hid1", "hid2"):
                    t_ring_at[kind, u, i] = len(t_ring_at)

            def xbank(f):
                return (obank, misc)[x_at[f] % 2]

            mid = [sb(f"mid{i}", [P, FC, 512]) for i in range(2)]
            top = sb("top", [P, NC, E])
            topi, topf = sb("topi", [P, NC, E], U32), sb("topf", [P, NC, 2])
            iot, iof = sb("iot", [P, E], I32), sb("iof", [P, E])
            gap, e2, w01 = sb("gap", [P, NC]), sb("e2", [P, NC]), sb("w01", [P, NC, 2])
            wa, wb, wts = sb("wa", [P, NC, E]), sb("wb", [P, NC, E]), sb("wts", [P, NC, E])
            wT = sb("wT", [E, NC * P])
            NT = B * (B + 1) // 2
            qkv = sb("qkv", [P, B, CB, 3 * D])
            prod = sb("prod", [P, B, CB, D])
            sc = sb("sc", [P, NT, CB * H])
            smax, ssum = sb("smax", [P, B, CB * H]), sb("ssum", [P, B, CB * H])
            att = sb("att", [P, B, CB * D])
            gl = [sb(f"gl{i}", [P, CB, S]) for i in range(HB)]
            f_a, f_b = sb("f_a", [P, 2, FC, 512]), sb("f_b", [P, 2, FC, 512])
            (t_ring_done, t_ring_free, out_done, out_free, x_done, x_free, t_var, t_rstd, t_hat, gap_ready, e2_ready, wts_ready, iot_ready,
             d_arg, d_exp, gl_ready, h_ready, silu_ready, t_dve, t_pool, stored) = map(sem, [
                 "t_ring_done", "t_ring_free", "out_done", "out_free", "x_done", "x_free", "t_var", "t_rstd", "t_hat", "gap_ready", "e2_ready",
                 "wts_ready", "iot_ready", "d_arg", "d_exp", "gl_ready", "h_ready", "silu_ready", "t_dve", "t_pool", "stored"])

            with nc.Block() as block:
                @block.tensor
                def _(pe):
                    def t_bank(key):
                        n = t_ring_at[key]
                        if n >= RING:
                            pe.wait_ge(t_ring_free, n - RING + 1)
                        return ring[:, n % RING, :]

                    for step in ORDER:
                        for f in before[step]:
                            kind, hf, i = f
                            if f not in x_at:
                                continue
                            if x_at[f] >= 2:
                                pe.wait_ge(x_free, x_at[f] - 1)
                            bank = xbank(f)
                            if kind == "wT":
                                pe.wait_ge(wts_ready, 1)
                                for j in range(HT):
                                    ins = nc.tensor.transpose(bank[0:E, j * P:(j + 1) * P], wts[:, HT * hf + j, :], ident[:, :])
                            elif kind == "b2":
                                pe.wait_ge(x_free, x_at["wT", 1, 0] + 1)
                                for j in range(HT):
                                    ins = nc.tensor.matmul(bank[:, j * P:(j + 1) * P], wT[:, (HT * hf + j) * P:(HT * hf + j + 1) * P], M_b2[:, :],
                                                           start=True, stop=True)
                            elif kind in ("T_c", "T_d", "T_e"):
                                n = ln_at["ln" + kind[1:], hf, 0]
                                for j in range(HT):
                                    pe.wait_ge(t_hat, HT * n + j + 1)
                                    ins = nc.tensor.transpose(bank[:, j * P:(j + 1) * P], x_res[:, HT * hf + j, :], ident[:, :])
                            elif kind == "proj":
                                if i == 0:
                                    pe.wait_ge(x_free, x_at["T_c", hf, 0] + 1)
                                    pe.wait_ge(loadF, 16 * 7)
                                j = HT * hf + i
                                ins = nc.tensor.matmul(bank[:, 0:3 * D], xn_all[:, j * P:(j + 1) * P], D_w[:, :], start=True, stop=True)
                            elif kind == "gate1":
                                b = HB * hf + i
                                pe.wait_ge(x_free, x_at["T_d", hf, 0] + 1)
                                for c in range(CB):
                                    ins = nc.tensor.matmul(bank[:, c * S:(c + 1) * S], ctxT[:, b, c * P:(c + 1) * P], xn_all[:, b * S:(b + 1) * S],
                                                           start=True, stop=True)
                            elif kind == "gate2":
                                pe.wait_ge(h_ready, HB * (hf + 1))
                                for k in range(HB):
                                    for c in range(CB):
                                        for fc in range(CB):
                                            ins = nc.tensor.matmul(bank[:, (CB * k + c) * P:(CB * k + c + 1) * P], gl[k][:, fc, c * P:(c + 1) * P],
                                                                   ctx_tok[:, CB * (HB * hf + k) + fc, :], start=fc == 0, stop=fc == CB - 1)
                            ins.then_inc(x_done, 1)
                        kind, u, i = step
                        if kind == "mid":
                            e, hf = u % E, u // E
                            pe.wait_ge(loadE[e], 48)
                            for hc in range(FC):
                                nc.tensor.matmul(t_bank(("mid", u, hc)), M_w1[:, e, hc * P:(hc + 1) * P], xn_all[:, hf * 512:(hf + 1) * 512],
                                                 start=True, stop=True).then_inc(t_ring_done, 1)
                        elif kind == "out":
                            pe.wait_ge(t_ring_free, t_ring_at["mid", u, FC - 1] + 1)
                            if u >= 2:
                                pe.wait_ge(out_free, u - 1)
                            for tc in range(HT):
                                for hc in range(FC):
                                    ins = nc.tensor.matmul(ptb[:, u % 2, tc * P:(tc + 1) * P], mid[u % 2][:, hc, tc * P:(tc + 1) * P],
                                                           M_w2[:, u % E, hc, :], start=hc == 0, stop=hc == FC - 1)
                            ins.then_inc(out_done, 1)
                        elif kind == "gated":
                            hf = u
                            if i == 0:
                                pe.wait_ge(x_free, x_at["T_e", hf, 0] + 1)
                            for w, weights in enumerate((F_w1, F_w2)):
                                nc.tensor.matmul(t_bank(("gated", hf, i, w)), weights[:, i * P:(i + 1) * P], xn_all[:, hf * 512:(hf + 1) * 512],
                                                 start=True, stop=True).then_inc(t_ring_done, 1)
                        elif kind in ("hid1", "hid2"):
                            hf = u
                            w, src = (F_h1, f_a) if kind == "hid1" else (F_h2, f_b)
                            bank = t_bank((kind, hf, i))
                            for kc in range(FC):
                                if i == 0:
                                    n = t_ring_at["gated", hf, kc, 1] if kind == "hid1" else t_ring_at["hid1", hf, kc]
                                    pe.wait_ge(t_ring_free, n + 1)
                                ins = nc.tensor.matmul(bank, w[:, kc, i * P:(i + 1) * P], src[:, hf, kc, :], start=kc == 0, stop=kc == FC - 1)
                            ins.then_inc(t_ring_done, 1)
                        elif kind == "last":
                            hf = u
                            pe.wait_ge(out_free, U + hf - 1)
                            for tc in range(HT):
                                for kc in range(FC):
                                    if tc == 0:
                                        pe.wait_ge(t_ring_free, t_ring_at["hid2", hf, kc] + 1)
                                    ins = nc.tensor.matmul(ptb[:, hf, tc * P:(tc + 1) * P], f_a[:, hf, kc, tc * P:(tc + 1) * P], F_w3[:, kc, :],
                                                           start=kc == 0, stop=kc == FC - 1)
                            ins.then_inc(out_done, 1)

                @block.scalar
                def _(act):
                    for step in ORDER:
                        for f in before[step]:
                            kind, hf, i = f
                            if kind == "gate":
                                act.wait_ge(gap_ready, 1)
                                nc.scalar.activation(e2[:, :], gap[:, :], ACT.Exp).then_inc(e2_ready, 1)
                            elif kind == "mix":
                                act.wait_ge(d_arg, hf + 1)
                                t0, t1 = [HB * k * (HB * k + 1) // 2 for k in (hf, hf + 1)]
                                nc.scalar.activation(sc[:, t0:t1, :], sc[:, t0:t1, :], ACT.Exp, scale=float(HD) ** -0.5).then_inc(d_exp, 1)
                            elif kind == "gate1":
                                act.wait_ge(x_done, x_at[f] + 1)
                                if hf:
                                    act.wait_ge(x_done, x_at["gate2", 0, 0] + 1)
                                nc.scalar.activation(gl[i][:, :, :].rearrange("p c s -> p (c s)"), xbank(f)[:, :], ACT.Gelu_apprx_tanh)\
                                    .then_inc(gl_ready, 1)
                        kind, u, i = step
                        if kind == "mid":
                            if u >= 2:
                                act.wait_ge(out_done, u - 1)
                            for hc in range(FC):
                                n = t_ring_at["mid", u, hc]
                                act.wait_ge(t_ring_done, n + 1)
                                nc.scalar.activation(mid[u % 2][:, hc, :], ring[:, n % RING, :], ACT.Gelu, bias=M_b1[:, u % E, hc:hc + 1])\
                                    .then_inc(t_ring_free, 1)
                        elif kind == "gated":
                            n = t_ring_at["gated", u, i, 0]
                            act.wait_ge(t_ring_done, n + 1)
                            nc.scalar.activation(f_a[:, u, i, :], ring[:, n % RING, :], ACT.Silu, scale=col("F_s1", i)).then_inc(silu_ready, 1)
                        elif kind in ("hid1", "hid2"):
                            n = t_ring_at[kind, u, i]
                            dst, s = (f_b, "F_h1") if kind == "hid1" else (f_a, "F_h2")
                            act.wait_ge(t_ring_done, n + 1)
                            nc.scalar.activation(dst[:, u, i, :], ring[:, n % RING, :], ACT.Gelu, scale=col(s, i)).then_inc(t_ring_free, 1)

                @block.gpsimd
                def _(pool):
                    nc.gpsimd.iota(iot[:, :], [[1, E]], 0, 0).then_inc(iot_ready, 1)
                    pool.wait_ge(iot_ready, 1)
                    nc.gpsimd.tensor_copy(iof[:, :], iot[:, :]).then_inc(iot_ready, 1)
                    ch = Chain(pool, t_pool)
                    for step in ORDER:
                        for f in before[step]:
                            if f in ln_at:
                                j = HT * f[1]
                                pool.wait_ge(t_var, ln_at[f] + 1)
                                ch.step(nc.gpsimd.tensor_tensor(veps[:, j:j + HT], mv[:, j:j + HT, 1], const[:, 1, 0:HT], ALU.add))
                                nc.gpsimd.tensor_tensor(rstd[:, j:j + HT], veps[:, j:j + HT], half[:, 0:HT], ALU.pow).then_inc(t_rstd, 1)

                @block.vector
                def _(dve):
                    ch = Chain(dve, t_dve)

                    def gate():
                        for j in range(NC):
                            ins = nc.vector.max(top[:, j, :], logits[:, j, :])
                        ch.step(ins)
                        nc.vector.tensor_tensor(gap[:, :], top[:, :, 1], top[:, :, 0], ALU.subtract).then_inc(gap_ready, 1)
                        for j in range(NC):
                            ins = nc.vector.max_index(topi[:, j, :], top[:, j, :], logits[:, j, :])
                        ch.step(ins)
                        ch.step(nc.vector.tensor_copy(topf[:, :, :], topi[:, :, 0:2]))
                        dve.wait_ge(e2_ready, 1)
                        ch.step(nc.vector.tensor_scalar(wa[:, :, 0], e2[:, :], 1.0, None, ALU.add))
                        ch.step(nc.vector.reciprocal(w01[:, :, 0], wa[:, :, 0]))
                        ch.step(nc.vector.tensor_tensor(w01[:, :, 1], w01[:, :, 0], e2[:, :], ALU.mult))
                        dve.wait_ge(iot_ready, 2)
                        for k, dst in enumerate([wa, wb]):
                            ch.step(nc.vector.tensor_tensor(dst[:, :, :], iof[:, :].unsqueeze(1).broadcast_to([P, NC, E]),
                                                            topf[:, :, k:k + 1].broadcast_to([P, NC, E]), ALU.is_equal))
                            ch.step(nc.vector.tensor_tensor(dst[:, :, :], dst[:, :, :], w01[:, :, k:k + 1].broadcast_to([P, NC, E]), ALU.mult))
                        nc.vector.tensor_tensor(wts[:, :, :], wa[:, :, :], wb[:, :, :], ALU.add).then_inc(wts_ready, 1)

                    def ln_begin(f):
                        j0 = HT * f[1]
                        for j in range(j0, j0 + HT):
                            ins = nc.vector.bn_stats(st[:, j, :], x_res[:, j, :])
                        ch.step(ins)
                        for j in range(j0, j0 + HT):
                            ins = nc.vector.bn_aggr(mv[:, j, :], st[:, j, :])
                        ins.then_inc(t_var, 1)

                    def ln_end(f):
                        j0 = HT * f[1]
                        dve.wait_ge(t_rstd, ln_at["ln" + f[0][2:], f[1], 0] + 1)
                        for j in range(j0, j0 + HT):
                            nc.vector.tensor_scalar(x_res[:, j, :], x_res[:, j, :], mv[:, j, 0:1], rstd[:, j:j + 1], ALU.subtract, ALU.mult)\
                                .then_inc(t_hat, 1)

                    def scores(hf):
                        for i in range(HB * hf, HB * hf + HB):
                            t0 = i * (i + 1) // 2
                            s3 = sc[:, t0:t0 + i + 1, :]
                            q = qkv[:, i, :, 0:D].unsqueeze(1).broadcast_to([P, i + 1, CB, D])
                            ch.step(nc.vector.tensor_tensor(prod[:, 0:i + 1, :, :], qkv[:, 0:i + 1, :, D:2 * D], q, ALU.mult))
                            ch.step(nc.vector.tensor_reduce(s3, prod[:, 0:i + 1, :, :].rearrange("p j c (h d) -> p j (c h) d", d=HD), AX.X, ALU.add))
                            ch.step(nc.vector.tensor_reduce(smax[:, i, :], s3.rearrange("p j x -> p x j"), AX.X, ALU.max))
                            ins = nc.vector.tensor_tensor(s3, s3, smax[:, i, :].unsqueeze(1).broadcast_to([P, i + 1, CB * H]), ALU.subtract)
                        ins.then_inc(d_arg, 1)

                    def mix(hf):
                        dve.wait_ge(d_exp, hf + 1)
                        i0, i1 = HB * hf, HB * hf + HB
                        for i in range(i0, i1):
                            t0 = i * (i + 1) // 2
                            ins = nc.vector.tensor_reduce(ssum[:, i, :], sc[:, t0:t0 + i + 1, :].rearrange("p j x -> p x j"), AX.X, ALU.add)
                        ch.step(ins)
                        ss = ssum[:, i0:i1, :]
                        ch.step(nc.vector.tensor_scalar(ss, ss, 1.0, None, ALU.add))
                        ch.step(nc.vector.reciprocal(ss, ss))
                        for i in range(i0, i1):
                            t0 = i * (i + 1) // 2
                            for c in range(CB):
                                pb = sc[:, t0:t0 + i + 1, c * H:(c + 1) * H].unsqueeze(3).broadcast_to([P, i + 1, H, HD])
                                ins = nc.vector.tensor_tensor(prod[:, 0:i + 1, c, :].rearrange("p j (h d) -> p j h d", d=HD),
                                                              qkv[:, 0:i + 1, c, 2 * D:3 * D].rearrange("p j (h d) -> p j h d", d=HD), pb, ALU.mult)
                            ch.step(ins)
                            ch.step(nc.vector.tensor_reduce(att[:, i, :], prod[:, 0:i + 1, :, :].rearrange("p j c d -> p (c d) j"), AX.X, ALU.add))
                        a3 = att[:, i0:i1, :].rearrange("p i (x d) -> p (i x) d", d=HD)
                        ch.step(nc.vector.tensor_tensor(a3, a3, ss.rearrange("p i x -> p (i x)").unsqueeze(2).broadcast_to([P, HB * CB * H, HD]),
                                                        ALU.mult))
                        xh = x_res[:, HT * hf:HT * hf + HT, :]
                        ch.step(nc.vector.tensor_tensor(xh, att[:, i0:i1, :].rearrange("p i (c d) -> p (i c) d", c=CB), xh, ALU.add))

                    for step in ORDER:
                        for f in before[step]:
                            kind, hf, i = f
                            xh = x_res[:, HT * hf:HT * hf + HT, :]
                            if f in x_at:
                                if kind == "gate1":
                                    dve.wait_ge(gl_ready, HB * hf + i + 1)
                                else:
                                    dve.wait_ge(x_done, x_at[f] + 1)
                                bank = xbank(f)
                                tok = bank[:, :].rearrange("p (j d) -> p j d", d=D)
                                if kind == "wT":
                                    ins = nc.vector.tensor_copy(wT[:, hf * 512:(hf + 1) * 512], bank[0:E, :])
                                elif kind in ("T_c", "T_d", "T_e"):
                                    ins = nc.vector.tensor_copy(xn_all[:, hf * 512:(hf + 1) * 512], bank[:, :])
                                elif kind in ("b2", "gate2"):
                                    ins = nc.vector.tensor_tensor(xh, tok, xh, ALU.add)
                                elif kind == "proj":
                                    j = HT * hf + i
                                    ins = nc.vector.tensor_tensor(qkv[:, j // CB, j % CB, :], bank[:, 0:3 * D], row("D_b"), ALU.add)
                                elif kind == "gate1":
                                    g = gl[i][:, :, :].rearrange("p c s -> p (c s)")
                                    ins = nc.vector.tensor_tensor(g, g, bank[:, :], ALU.mult)
                                ins.then_inc(x_free, 1)
                                if kind == "gate1":
                                    dve.wait_ge(x_free, x_at[f] + 1)
                                    dve.sem_inc(h_ready, 1)
                                if kind in ("gate2", "b2", "proj"):
                                    dve.wait_ge(x_free, x_at[f] + 1)
                            elif kind == "gate":
                                gate()
                            elif f in ln_at:
                                ln_begin(f)
                            elif kind.startswith("le_"):
                                ln_end(f)
                            elif kind == "fin":
                                hh = hat[:, HT * hf:HT * hf + HT, :]
                                dve.wait_ge(out_done, U + hf + 1)
                                ch.step(nc.vector.tensor_tensor(hh, ptb[:, hf, :].rearrange("p (j d) -> p j d", d=D), rowb("F_s3", HT), ALU.mult))
                                ch.step(nc.vector.tensor_tensor(xh, hh, xh, ALU.add))
                            elif kind == "score":
                                scores(hf)
                            elif kind == "mix":
                                mix(hf)
                        kind, u, i = step
                        if kind == "out":
                            hf = u // E
                            dve.wait_ge(out_done, u + 1)
                            for tc in range(HT):
                                j = HT * hf + tc
                                ins = nc.vector.scalar_tensor_tensor(x_res[:, j, :], ptb[:, u % 2, tc * P:(tc + 1) * P],
                                                                     wts[:, j, u % E:u % E + 1], x_res[:, j, :], ALU.mult, ALU.add)
                            ins.then_inc(out_free, 1)
                            dve.wait_ge(out_free, u + 1)
                        elif kind == "gated":
                            n = t_ring_at["gated", u, i, 1]
                            dve.wait_ge(silu_ready, FC * u + i + 1)
                            dve.wait_ge(t_ring_done, n + 1)
                            a = f_a[:, u, i, :]
                            nc.vector.scalar_tensor_tensor(a, ring[:, n % RING, :], col("F_s2", i), a, ALU.mult, ALU.mult).then_inc(t_ring_free, 2)

                @block.sync
                def _(sp):
                    for hf in range(2):
                        sp.wait_ge(t_hat, HT * (ln_at["ln_f", hf, 0] + 1))
                        sp.dma_start(t["out"].rearrange("(j p) d -> p j d", p=P)[:, HT * hf:HT * hf + HT, :], x_res[:, HT * hf:HT * hf + HT, :])\
                            .then_inc(stored, 16)
                    sp.wait_ge(stored, 32)

        if upto < 2:
            fin = sem("fin")
            with nc.Block() as block:
                @block.sync
                def _(sp):
                    sp.wait_ge(loadN, 96)
                    if upto > 1:
                        sp.wait_ge(loadF, 16 * 7)
                        for e in range(E):
                            sp.wait_ge(loadE[e], 48)
                    sp.dma_start(t["out"].rearrange("(j p) d -> p j d", p=P), x_res[:, :, :]).then_inc(fin, 16)
                    sp.wait_ge(fin, 16)


def layout(i):
    import numpy as np

    i = {k: np.asarray(v) for k, v in i.items()}
    a = {}
    a["x"] = i["x"].reshape(B * S, D)
    a["xT"] = i["x"].transpose(0, 2, 1)
    a["ctx"] = i["ctx_1024"].reshape(B * S, D)
    a["ctxT"] = i["ctx_1024"].transpose(0, 2, 1)
    for k in ("q", "k", "v", "o"):
        a["A_w" + k] = i["L0_attn_W" + k]
    a["B_wq"], a["B_wkv"], a["B_wo"] = i["L0_xattn_Wq"], i["L0_xattn_Wkv"], i["L0_xattn_Wo"]
    for k in ("q", "k", "v"):
        a["C_w" + k] = i["L0_ffn_W" + k]
    a["C_wp"] = i["L0_ffn_Wp"]
    a["M_gw"] = i["L0_ffn_gate_W"]
    a["M_w1"], a["M_b2"] = i["L0_ffn_exp_W1"], i["L0_ffn_exp_b2"]
    a["M_b1"] = i["L0_ffn_exp_b1"].reshape(E, FC, P).transpose(0, 2, 1)
    a["M_w2"] = i["L0_ffn_exp_W2"].reshape(E, FC, P, D).transpose(0, 2, 1, 3)
    a["D_w"] = np.concatenate([i[f"L1_attn_W{k}"].T for k in "qkv"], axis=1)
    a["F_w1"], a["F_w2"] = i["L1_ffn_w1_w"].T, i["L1_ffn_w2_w"].T
    for k in ("h1", "h2", "w3"):
        w = i[f"L1_ffn_{k}_w"].T
        a["F_" + k] = w.reshape(FC, P, w.shape[1]).transpose(1, 0, 2)
    two = lambda v: np.concatenate([v, v])
    c = {
        "A_bq": i["L0_attn_bq"].reshape(PAIRS, P).T, "A_bk": i["L0_attn_bk"].reshape(PAIRS, P).T,
        "A_bv": i["L0_attn_bv"].reshape(PAIRS, P).T, "B_qs": two(i["L0_xattn_q_scale"]), "B_ks": two(i["L0_xattn_k_scale"]),
        "B_nv": two(i["L0_xattn_null_kv"][1]),
        "B_in_g": i["L0_xattn_ln_in_g"], "B_in_b": i["L0_xattn_ln_in_b"], "B_ctx_g": i["L0_xattn_ln_ctx_g"],
        "B_ctx_b": i["L0_xattn_ln_ctx_b"], "C_ln1_g": i["L0_ffn_ln1_g"], "C_ln1_b": i["L0_ffn_ln1_b"],
        "C_ln2_g": i["L0_ffn_ln2_g"], "C_ln2_b": i["L0_ffn_ln2_b"], "C_bq": i["L0_ffn_bq"], "C_bk": i["L0_ffn_bk"],
        "C_bv": i["L0_ffn_bv"],
        "F_s1": i["L1_ffn_w1_s"].reshape(FC, P).T, "F_s2": i["L1_ffn_w2_s"].reshape(FC, P).T,
        "F_h1": i["L1_ffn_h1_s"].reshape(FC, P).T, "F_h2": i["L1_ffn_h2_s"].reshape(FC, P).T,
    }
    a["cols"] = np.concatenate([np.reshape(c[n], (P, w)) for n, (_, w) in COLS.items()], axis=1)
    r = {"A_bo": i["L0_attn_bo"], "B_out_g": i["L0_xattn_ln_out_g"], "B_out_b": i["L0_xattn_ln_out_b"],
         "B_nk": i["L0_xattn_null_kv"][0], "B_qsr": i["L0_xattn_q_scale"], "B_ksr": i["L0_xattn_k_scale"], "C_bp": i["L0_ffn_bp"], "M_gb": i["L0_ffn_gate_b"],
         "D_b": np.concatenate([i[f"L1_attn_b{k}"] for k in "qkv"]), "F_s3": i["L1_ffn_w3_s"]}
    a["rows"] = np.concatenate([r[n] for n in ROWS])
    return {k: np.ascontiguousarray(v) for k, v in a.items()}


def kernel(**inputs):
    import numpy as _np
    import concourse.bacc as _bacc
    from concourse import mybir as _mybir
    from concourse.bass_utils import run_bass_kernel_spmd as _run

    nc = _bacc.Bacc("TRN2", target_bir_lowering=False, num_devices=1)
    arrays, t = {}, {}
    for name, a in layout(inputs).items():
        arrays[f"in_{name}_dram"] = a
        t[name] = nc.dram_tensor(f"in_{name}_dram", a.shape, _mybir.dt.from_np(a.dtype), kind="ExternalInput").ap()
    t["out"] = nc.dram_tensor("out_0_dram", (B * S, D), _mybir.dt.float32, kind="ExternalOutput").ap()
    decoder(nc, t)
    r = _run(nc, [arrays], core_ids=[0])
    return _np.asarray(r.results[0]["out_0_dram"]).reshape(B, S, D)
```

```python
from contextlib import ExitStack

import concourse.bass as bass
from concourse import mybir

F32 = mybir.dt.float32
BF16 = mybir.dt.bfloat16
I32 = mybir.dt.int32
U32 = mybir.dt.uint32
ALU = mybir.AluOpType
ACT = mybir.ActivationFunctionType
AX = mybir.AxisListType

B, S, D = 4, 256, 128
P = 128
NC = B * S // P
CB = S // P
H, A = 16, 64
PAIRS = H // 2
HD = D // H
E, FF = 8, 4 * D
FILL = [1, 1, 1, 1, 2, 3, 2]
ARENA = 40000
FC = FF // P
LN_EPS = 1e-5
NORM_EPS = 1e-12
MASKED = 1e30

COLS = {}
for _n, _w in [("A_bq", PAIRS), ("A_bk", PAIRS), ("A_bv", PAIRS), ("B_qs", 1), ("B_ks", 1), ("B_nv", 1),
               ("B_in_g", 1), ("B_in_b", 1), ("B_ctx_g", 1), ("B_ctx_b", 1), ("C_ln1_g", 1), ("C_ln1_b", 1),
               ("C_ln2_g", 1), ("C_ln2_b", 1), ("C_bq", 1), ("C_bk", 1), ("C_bv", 1),
               ("F_s1", FC), ("F_s2", FC), ("F_h1", FC), ("F_h2", FC)]:
    COLS[_n] = (sum(w for _, w in COLS.values()), _w)
NCOLS = sum(w for _, w in COLS.values())
ROWS = {}
for _n, _w in [("A_bo", D), ("B_out_g", D), ("B_out_b", D), ("B_nk", A), ("B_qsr", A), ("B_ksr", A), ("C_bp", D), ("M_gb", E), ("D_b", 3 * D),
               ("F_s3", D)]:
    ROWS[_n] = (sum(w for _, w in ROWS.values()), _w)
NROWS = sum(w for _, w in ROWS.values())


class Chain:

    def __init__(self, eng, sem):
        self.eng, self.sem, self.n = eng, sem, 0

    def done(self, ins):
        self.n += 1
        ins.then_inc(self.sem, 1)

    def mark(self, ins):
        self.done(ins)
        return self.n

    def after(self, mark):
        self.eng.wait_ge(self.sem, mark)

    def step(self, ins):
        self.done(ins)
        self.eng.wait_ge(self.sem, self.n)


def decoder(nc, t):
    ctx = ExitStack()
    with ctx:
        def sb(name, shape, dt=F32):
            return ctx.enter_context(nc.sbuf_tensor(name, shape, dt))

        def sem(name):
            return ctx.enter_context(nc.semaphore(name))

        RING = 4
        ring = ctx.enter_context(nc.psum_tensor("ring", [P, RING, 512], F32))
        ptb = ctx.enter_context(nc.psum_tensor("ptb", [P, CB, 512], F32))
        obank = ctx.enter_context(nc.psum_tensor("obank", [P, 512], F32))
        misc = ctx.enter_context(nc.psum_tensor("misc", [P, 512], F32))

        x_res = sb("x_res", [P, NC, D])
        ctx_tok = sb("ctx_tok", [P, NC, D])
        cols = sb("cols", [P, NCOLS])
        rows = sb("rows", [P, NROWS])
        ident = sb("ident", [P, P])
        CONSTS = [-0.5, LN_EPS, float(A) ** 0.5, -float(A) ** 0.5]
        const = sb("const", [P, len(CONSTS), 64])
        C_wq, C_wk, C_wv, C_wp = [sb("C_w" + n, [P, D]) for n in "qkvp"]
        M_gw, M_b2 = sb("M_gw", [P, E]), sb("M_b2", [E, D])
        hmask = sb("hmask", [P, H])
        causal, identb = sb("causal", [P, P], BF16), sb("identb", [P, P], BF16)
        half = const[:, 0, :]

        def col(name, i=0, lo=0, hi=P):
            o = COLS[name][0] + i
            return cols[lo:hi, o:o + 1]

        def row(name):
            o, w = ROWS[name]
            return rows[:, o:o + w]

        def rowb(name, n):
            return row(name).unsqueeze(1).broadcast_to([P, n, ROWS[name][1]])

        st = sb("st", [P, NC, 6])
        mv = sb("mv", [P, NC, 2])
        veps = sb("veps", [P, NC])
        rstd = sb("rstd", [P, NC])
        xn_all = sb("xn_all", [P, NC * P])
        hat = sb("hat", [P, NC, D])
        y = sb("y", [P, CB, D])
        y2, xhat = sb("y2", [P, CB, D]), sb("xhat", [P, CB, D])
        scrap = sb("scrap", [P, 1])
        topi, iot, iof = sb("topi", [P, NC, E], U32), sb("iot", [P, E], I32), sb("iof", [P, E])

        arena = sb("arena", [P, ARENA])
        taken = [0]

        def take(shape):
            lo, n = taken[0], 1
            for d in shape[1:]:
                n *= d
            taken[0] += n
            assert taken[0] <= ARENA
            names = "abcd"[:len(shape) - 1]
            return arena[0:shape[0], lo:lo + n].rearrange(f"p ({' '.join(names)}) -> p {' '.join(names)}",
                                                          **dict(zip(names, shape[1:])))

        A_wq, A_wk, A_wv = take([P, H * A]), take([P, H * A]), take([P, H * A])
        A_wo = take([P, PAIRS, D])
        B_wq, B_wkv = take([P, H * A]), take([P, 2 * H * A])
        xTa, cn_all = take([P, NC * P]), take([P, NC * P])
        ksq, qsq = take([P, CB * H, A]), take([P, PAIRS, S])
        ktok = [take([P, CB, H * A]) for i in range(2)]
        qT_all = [take([P, PAIRS, S]) for i in range(2)]
        vtok = [take([P, CB, H * A]) for i in range(2)]
        B_wo = take([P, PAIRS, D])
        kss, krn = take([P, CB * H]), take([P, CB * H])
        qT = [take([P, S]) for i in range(2)]
        kz = [take([P, 2, S]) for i in range(2)]
        probs = [take([P, CB, 2, S]) for i in range(4)]
        probsT = [take([P, 2, CB, S]) for i in range(2)]
        oT = [take([P, PAIRS, S]) for i in range(2)]
        ssn = take([P, 2, 8 * PAIRS])
        rqt = take([P, 4 * PAIRS])
        negmax, sums, rsum, prq, nrq, snr, mins, pn, pnarg = [take([P, 2, PAIRS, CB, 2]) for i in range(9)]
        pnt, pnT = take([P, CB, H]), take([H, S])
        nqk, wnull, blk = take([P, 1]), take([P, H]), take([P, 2])
        nvz, nvwo = take([P, PAIRS, H]), take([H, D])
        nkr, nks = take([P, A]), take([P, 1])
        wtmp = ksq[:, 0:H, :]
        lst, lmv = take([P, CB, 6]), take([P, 2, CB, 2])
        lve, lrs = take([P, CB]), take([P, 2, CB])

        loadN = sem("loadN")
        loadA, loadC, loadX = sem("loadA"), sem("loadC"), sem("loadX")
        loadW = {n: sem("load_" + n) for n in ("A_wq", "A_wk", "A_wv", "A_wo", "B_wq", "B_wkv", "B_wo")}

        def ln_stats(ch, src, n):
            for i in range(n):
                ins = nc.vector.bn_stats(st[:, i, :], src(i))
            ch.step(ins)
            for i in range(n):
                ins = nc.vector.bn_aggr(mv[:, i, :], st[:, i, :])
            return ins

        def ln_power(ch, n):
            ch.step(nc.gpsimd.tensor_tensor(veps[:, 0:n], mv[:, 0:n, 1], const[:, 1, 0:n], ALU.add))
            return nc.gpsimd.tensor_tensor(rstd[:, 0:n], veps[:, 0:n], half[:, 0:n], ALU.pow)

        TL = 3
        NP = 2 * B * PAIRS
        STEPS = NP + 2 * TL + 8
        extras = {s: [] for s in range(STEPS)}
        dve_extras = {s: [] for s in range(STEPS)}
        pool_extras = {s: [] for s in range(STEPS)}
        ssq_at = {}
        for bb in range(2 * B):
            s0, b, cross = PAIRS * bb, bb % B, bb >= B
            for r in range(4):
                extras[s0 - 4 + r if bb else (1, 2, 3, 3)[r]].append(("V", bb, r))
                if cross:
                    extras[s0 - 10 + r].append(("K", b, r))
                    extras[s0 - 8 + r].append(("Q", b, r))
                    ssq_at[s0 - 6 + r] = (b, r)
            if cross:
                dve_extras[s0 - 6].append(("ksum", b))
                for r in range(4):
                    pool_extras[s0 - 6 + r].append(("khat", b, r))
                dve_extras[s0 - 2].append(("qsum", b))
                dve_extras[s0 + 9].append(("pnt", b))
                extras[s0 + 11].append(("pnT", b, 0))
            else:
                extras[s0 + 18].append(("X", b, 0))
                dve_extras[s0 + 15].append(("xnorm", b))
            for c in range(CB):
                extras[s0 + 12 + c].append(("out", bb, c))
            if cross:
                dve_extras[s0 + 16].append(("norm2", b))
                dve_extras[s0 + 17].append(("cnorm", b))
                extras[s0 + (22 if b < B - 1 else 19)].append(("CX", b, 0))
        dve_extras[5].append(("ctx_norm", 0))
        extras[8].append(("C", 0, 0))
        extras[9].append(("C", 1, 0))
        dve_extras[9].append(("null_value", 0))
        dve_extras[11].append(("null_key", 0))
        extras[14].append(("NV", 0, 0))
        misc_extras = {s: [e for e in extras[s] if e[0] not in ("V", "K", "Q")] for s in extras}
        ring_extras = {s: [e for e in extras[s] if e[0] in ("V", "K", "Q")] for s in extras}

        def nulls(b, q):
            o = 4 * PAIRS + 4 * q
            return ssn[:, b % 2, o:o + 4].rearrange("p (c h) -> p c h", c=CB)

        cst, ring_done, ring_free = sem("cst"), sem("ring_done"), sem("ring_free")
        misc_done, misc_free = sem("misc_done"), sem("misc_free")
        max_ready, norm_done, ssn_ready = sem("max_ready"), sem("norm_done"), sem("ssn_ready")
        load_first, bo_added = sem("load_first"), sem("bo_added")
        pt_done, pt_free, o_done, o_free = sem("pt_done"), sem("pt_free"), sem("o_done"), sem("o_free")
        khat_ready, ksum_ready = sem("khat_ready"), sem("ksum_ready")
        qsum_ready, rq_ready, pnt_ready = sem("qsum_ready"), sem("rq_ready"), sem("pnt_ready")
        var_ready = sem("var_ready")
        normed, B_LNS = sem("normed"), 2
        xhat_ready, c_hat_ready = sem("xhat_ready"), sem("c_hat_ready")
        cstat, chat = sem("cstat"), sem("chat")
        null_ss, null_pow, null_ready, consts_ready = sem("null_ss"), sem("null_pow"), sem("null_ready"), sem("consts_ready")
        wide_dve, wide_pool = sem("wide_dve"), sem("wide_pool")

        def pool_ln(pool, ch, n, dst, src):
            i = n % 2
            pool.wait_ge(var_ready, n + 1)
            ch.step(nc.gpsimd.tensor_tensor(lve[:, :], lmv[:, i, :, 1], const[:, 1, 0:CB], ALU.add))
            ch.step(nc.gpsimd.tensor_tensor(lrs[:, i, :], lve[:, :], half[:, 0:CB], ALU.pow))
            for c in range(CB):
                ins = nc.gpsimd.tensor_scalar(dst[:, c, :], src[:, c, :], lmv[:, i, c, 0:1], lrs[:, i, c:c + 1], ALU.subtract, ALU.mult)
            return ins

        G = 4
        NG = H // G
        NGR = B * NG
        CT = 2
        tiles = [(range(0, 4), 0), (range(0, 2), 1), (range(2, 4), 1)]
        stat_of = [0, 4, 6]
        KR, PR = 3, 4
        VW = 32
        TU = len(tiles)
        loadF = sem("loadF")
        loadE = [sem(f"loadE{e}") for e in range(E)]
        taken[0] = 0
        qTc, kTc = take([P, 2, S]), take([P, 2, S])
        kzn = take([P, KR, G, S])
        vtn = take([P, 2, CB, H, VW])
        oT4 = [take([P, S]) for i in range(2)]
        pr = take([P, PR, TU, 512])
        prT = [take([P, G, CB, S]) for i in range(2)]
        oN, oTn = take([P, 2, CB, D]), take([P, 2, S])
        nmax, nrs = take([P, NGR, 8]), take([P, NGR, 8])
        x1 = take([P, 2, CB, D])
        lmv2, lve2, lrs2 = take([P, B, CB, 2]), take([P, B, CB]), take([P, B, CB])
        ARENA_TOP = taken[0]
        M_w1, M_w2, M_b1 = take([P, E, FF]), take([P, E, FC, D]), take([P, E, FC])
        ctxT, D_w = take([P, B, S]), take([P, 3 * D])
        F_w1, F_w2 = take([P, FF]), take([P, FF])
        F_h1, F_h2, F_w3 = take([P, FC, FF]), take([P, FC, FF]), take([P, FC, D])
        mid = [take([P, FC, 512]) for i in range(2)]
        logits, top = take([P, NC, E]), take([P, NC, E])
        topf = take([P, NC, 2])
        gap, e2, w01 = take([P, NC]), take([P, NC]), take([P, NC, 2])
        wa, wb, wts = take([P, NC, E]), take([P, NC, E]), take([P, NC, E])
        wT = take([E, NC * P])

        FIRST = -3
        C_AT = NP + 1
        CSTEPS = NGR + CT + 6
        c_extras = {s: [] for s in range(FIRST, CSTEPS)}
        c_dve = {s: [] for s in range(FIRST, CSTEPS)}
        for b in range(B):
            s0 = NG * b
            c_extras[s0 - (3 if b < B - 1 else 2)].insert(0, ("QK", b))
            c_extras[s0 - 1].insert(0, ("V", b))
            c_extras[s0 + NG + CT + 2].append(("OT", b))
            c_extras[s0 + NG + CT + 3].append(("OUT", b))
            c_dve[s0 + NG + CT + 4].append(("hat", b))
            late = int(b < B - 1)
            c_extras[s0 + NG + CT + 4 + late].append(("X2", b))
            c_extras[s0 + NG + CT + 5 + late].append(("GATE", b))

        (c_ring_done, c_ring_free, c_max, c_pt_done, c_pt_free, c_o_done, c_o_free, c_ot_done, c_ot_free, c_ones, kz_dve, kz_act, kz_pool,
         c_var, c_rstd, c_xhat, c_dve_steps, c_pool_steps) = map(sem, [
             "c_ring_done", "c_ring_free", "c_max", "c_pt_done", "c_pt_free", "c_o_done", "c_o_free", "c_ot_done", "c_ot_free", "c_ones",
             "kz_dve", "kz_act", "kz_pool", "c_var", "c_rstd", "c_xhat", "c_dve_steps", "c_pool_steps"])
        ring_at, misc_at = {}, {}
        for s in range(STEPS):
            if s < NP:
                misc_at["pair", s] = len(misc_at)
            if 1 <= s <= NP:
                for c in range(CB):
                    ring_at["S", s - 1, c] = len(ring_at)
            for e in misc_extras[s]:
                misc_at[e] = len(misc_at)
            for e in ring_extras[s]:
                ring_at[e] = len(ring_at)
            for e in c_extras.get(s - C_AT, []):
                misc_at[e] = len(misc_at)
        for s in range(STEPS - C_AT, CSTEPS):
            for e in c_extras[s]:
                misc_at[e] = len(misc_at)

        U = 2 * E
        HT = NC // 2
        HB = B // 2
        steps = []
        for u in range(U):
            steps.append(("mid", u, 0))
            if u:
                steps.append(("out", u - 1, 0))
        steps.append(("out", U - 1, 0))
        for hf in range(2):
            steps += [("gated", hf, i) for i in range(FC)]
            steps += [("hid1", hf, i) for i in range(FC)] + [("hid2", hf, i) for i in range(FC)]
            steps.append(("last", hf, 0))
        before = {e: [] for e in steps + [("end", 0, 0)]}
        before["out", 0, 0] += [("gate", 0, 0)]
        before["mid", 6, 0] += [("wT", 0, 0)]
        before["out", 5, 0] += [("b2", 0, 0), ("gate", 1, 0)]
        before["mid", 7, 0] += [("wT", 1, 0)]
        before["out", 6, 0] += [("b2", 1, 0)]
        for hf, at in enumerate([
                {"ln_c": ("mid", 9, 0), "le_c": ("mid", 9, 0), "T_c": ("mid", 10, 0), "proj": ("out", 9, 0), "score": ("out", 9, 0),
                 "mix": ("out", 10, 0), "ln_d": ("mid", 12, 0), "le_d": ("mid", 12, 0), "T_d": ("out", 12, 0), "gate1": ("mid", 14, 0),
                 "gate2": ("out", 13, 0), "ln_e": ("mid", 15, 0), "le_e": ("mid", 15, 0), "T_e": ("out", 15, 0),
                 "fin": ("gated", 1, 0), "ln_f": ("gated", 1, 2), "le_f": ("gated", 1, 3)},
                {"ln_c": ("gated", 0, 0), "le_c": ("gated", 0, 2), "T_c": ("gated", 0, 3), "proj": ("hid1", 0, 0), "score": ("hid1", 0, 0),
                 "mix": ("hid1", 0, 1), "ln_d": ("hid1", 0, 1), "le_d": ("hid1", 0, 1), "T_d": ("hid2", 0, 1), "gate1": ("hid2", 0, 2),
                 "gate2": ("hid2", 0, 3), "ln_e": ("hid2", 0, 3), "le_e": ("hid2", 0, 3), "T_e": ("last", 0, 0)}]):
            for name, e in at.items():
                n = {"proj": HT, "gate1": HB, "fin": 2, "ln_f": 2, "le_f": 2}.get(name, 1)
                before[e] += [(name, hf, i) for i in range(n)]
        before["end", 0, 0] += [("fin", 1, 0), ("ln_f", 1, 0), ("fin", 1, 1), ("ln_f", 1, 1), ("le_f", 1, 0), ("le_f", 1, 1)]
        ORDER = steps + [("end", 0, 0)]
        fill, n = {}, 0
        for s, k in zip(range(NGR + CT - 1, CSTEPS), FILL):
            fill[s] = steps[n:n + k]
            n += k
        FILLED = n

        def ln_chunks(f):
            kind, hf, i = f
            return range(HT * hf + 2 * i, HT * hf + 2 * i + 2) if kind[2:] == "_f" else range(HT * hf, HT * hf + HT)

        x_at, t_ring_at, ln_at, hat_at = {}, {}, {}, {}
        for e in ORDER:
            for f in before[e]:
                if f[0] in ("wT", "b2", "T_c", "proj", "T_d", "gate1", "gate2", "T_e"):
                    x_at[f] = len(x_at)
                if f[0].startswith("ln_"):
                    ln_at[f] = len(ln_at)
                    hat_at[f] = sum(len(ln_chunks(g)) for g in hat_at)
            kind, u, i = e
            if kind == "mid":
                for hc in range(FC):
                    t_ring_at["mid", u, hc] = len(t_ring_at)
            elif kind == "gated":
                for w in range(2):
                    t_ring_at["gated", u, i, w] = len(t_ring_at)
            elif kind in ("hid1", "hid2"):
                t_ring_at[kind, u, i] = len(t_ring_at)

        def xbank(f):
            return (obank, misc)[x_at[f] % 2]

        taken[0] = 0
        NT = B * (B + 1) // 2
        qkv = take([P, B, CB, 3 * D])
        prod = take([P, B, CB, D])
        sc = take([P, NT, CB * H])
        smax, ssum = take([P, B, CB * H]), take([P, B, CB * H])
        att = take([P, B, CB * D])
        gl = [take([P, CB, S]) for i in range(HB)]
        f_a, f_b = take([P, 2, FC, 512]), take([P, 2, FC, 512])
        assert taken[0] <= ARENA_TOP
        (t_ring_done, t_ring_free, out_done, out_free, x_done, x_free, t_var, t_rstd, t_hat, gap_ready, e2_ready, wts_ready, iot_ready,
         last_done, fin_read, d_arg, d_exp, gl_ready, h_ready, silu_ready, t_dve, t_pool, stored) = map(sem, [
             "t_ring_done", "t_ring_free", "out_done", "out_free", "x_done", "x_free", "t_var", "t_rstd", "t_hat", "gap_ready", "e2_ready",
             "wts_ready", "iot_ready", "last_done", "fin_read", "d_arg", "d_exp", "gl_ready", "h_ready", "silu_ready", "t_dve", "t_pool", "stored"])

        with nc.Block() as block:
            @block.sync
            def _(sp):
                sp.dma_start(xTa[:, 0:S], t["xT"][0]).then_inc(load_first, 16)
                sp.dma_start(A_wq[:, 0:2 * P], t["A_wq"][:, 0:2 * P]).then_inc(load_first, 16)
                sp.dma_start(A_wv[:, :], t["A_wv"]).then_inc(loadW["A_wv"], 16)
                sp.dma_start(A_wq[:, 2 * P:], t["A_wq"][:, 2 * P:]).then_inc(loadW["A_wq"], 16)
                sp.dma_start(A_wk[:, 2 * P:], t["A_wk"][:, 2 * P:]).then_inc(loadW["A_wk"], 16)
                sp.dma_start(xTa[:, S:].rearrange("p (b s) -> p b s", b=B - 1), t["xT"][1:B].rearrange("b p s -> p b s")).then_inc(loadX, 16)
                sp.dma_start(x_res[:, :, :], t["x"].rearrange("(j p) d -> p j d", p=P)).then_inc(loadA, 16)
                sp.dma_start(ctx_tok[:, :, :], t["ctx"].rearrange("(j p) d -> p j d", p=P)).then_inc(loadA, 16)
                sp.dma_start(rows[:, :], t["rows"].partition_broadcast(P)).then_inc(loadA, 16)
                sp.dma_start(B_wo[:, :, :], t["B_wo"].rearrange("(a p) d -> p a d", p=P)).then_inc(loadW["B_wo"], 16)
                sp.dma_start(B_wq[:, :], t["B_wq"]).then_inc(loadW["B_wq"], 16)
                sp.dma_start(A_wo[:, :, :], t["A_wo"].rearrange("(a p) d -> p a d", p=P)).then_inc(loadW["A_wo"], 16)
                sp.dma_start(B_wkv[:, :], t["B_wkv"]).then_inc(loadW["B_wkv"], 16)
                for dst, src in [(C_wq, "C_wq"), (C_wk, "C_wk"), (C_wv, "C_wv"), (C_wp, "C_wp"), (M_gw, "M_gw"), (M_b2, "M_b2")]:
                    sp.dma_start(dst[:, :], t[src]).then_inc(loadN, 16)
                sp.wait_ge(misc_free, misc_at["CX", B - 1, 0] + 1)
                for e in range(E):
                    for dst, src in [(M_w1[:, e, :], t["M_w1"][e]), (M_b1[:, e, :], t["M_b1"][e]), (M_w2[:, e, :, :], t["M_w2"][e])]:
                        sp.dma_start(dst, src).then_inc(loadE[e], 16)
                for dst, src in [(D_w[:, :], t["D_w"]), (ctxT[:, :, :], t["ctxT"].rearrange("b p s -> p b s")),
                                 (F_w1[:, :], t["F_w1"]), (F_w2[:, :], t["F_w2"]), (F_h1[:, :, :], t["F_h1"]),
                                 (F_h2[:, :, :], t["F_h2"]), (F_w3[:, :, :], t["F_w3"])]:
                    sp.dma_start(dst, src).then_inc(loadF, 16)
                for hf in range(2):
                    for i in range(2):
                        j = HT * hf + 2 * i
                        sp.wait_ge(t_hat, hat_at["ln_f", hf, i] + 2)
                        sp.dma_start(t["out"].rearrange("(j p) d -> p j d", p=P)[:, j:j + 2, :], x_res[:, j:j + 2, :]).then_inc(stored, 16)
                sp.wait_ge(stored, 64)

            @block.scalar
            def _(act):
                act.dma_start(cols[:, :], t["cols"]).then_inc(loadC, 16)
                act.dma_start(A_wk[:, 0:2 * P], t["A_wk"][:, 0:2 * P]).then_inc(load_first, 16)
                act.wait_ge(cst, 3)
                nc.scalar.activation(scrap[:, :], const[:, 0, 0:1], ACT.Exp)
                act.wait_ge(consts_ready, 2)

                def narrow_step(s):
                    if -1 <= s < NGR - 1:
                        g = s + 1
                        b, h = g // NG, G * (g % NG) + 3
                        act.wait_ge(misc_free, misc_at["QK", b] + 1)
                        if g >= KR:
                            act.wait_ge(c_ring_done, TU * (g - KR + 1))
                        nc.scalar.activation(kzn[:, g % KR, 3, :], kTc[:, b % 2, :], ACT.Copy, scale=hmask[:, h:h + 1])\
                            .then_inc(kz_act, 1)
                    if 0 <= s < NGR:
                        for u, (heads, c) in enumerate(tiles):
                            n = TU * s + u
                            nh, nk = len(heads), (c + 1) * P
                            act.wait_ge(c_max, n + 1)
                            if s >= PR:
                                act.wait_ge(c_pt_done, n - TU * PR + 1)
                            for k in range(nh):
                                m = stat_of[u] + k
                                ins = nc.scalar.activation(pr[:, s % PR, u, k * nk:(k + 1) * nk], ring[:, n % RING, k * nk:(k + 1) * nk],
                                                           ACT.Exp, bias=nmax[:, s, m:m + 1], scale=-1.0)
                            ins.then_inc(c_ring_free, 1)
                    if CT < s <= NGR + CT:
                        g = s - CT - 1
                        act.wait_ge(c_o_done, g + 1)
                        if g >= 2:
                            act.wait_ge(c_ot_done, g - 1)
                        nc.scalar.copy(oT4[g % 2][:, :], obank[:, 0:S]).then_inc(c_o_free, 1)
                    for e in c_extras[s]:
                        kind, b = e
                        if kind in ("QK", "V", "OT"):
                            act.wait_ge(misc_done, misc_at[e] + 1)
                        if kind == "QK":
                            if b >= 2:
                                act.wait_ge(kz_pool, NG * (b - 1))
                            nc.scalar.activation(kTc[:, b % 2, :], misc[:, S:2 * S], ACT.Identity, bias=col("C_bk"))
                            ins = nc.scalar.activation(qTc[:, b % 2, :], misc[:, 0:S], ACT.Identity, bias=col("C_bq"),
                                                       scale=-float(HD) ** -0.5)
                        elif kind == "V":
                            act.wait_ge(c_ones, 1)
                            if b >= 2:
                                act.wait_ge(c_o_done, NG * (b - 1))
                            ins = nc.scalar.copy(vtn[:, b % 2, :, :, 0:HD], misc[:, 0:S].rearrange("p (c h d) -> p c h d", c=CB, d=HD))
                        elif kind == "OT":
                            ins = nc.scalar.activation(oTn[:, b % 2, :], misc[:, 0:S], ACT.Identity, bias=col("C_bv"))
                        if kind in ("QK", "V", "OT"):
                            ins.then_inc(misc_free, 1)

                def tail_step(step):
                    for f in before[step]:
                        kind, hf, i = f
                        if kind == "gate":
                            act.wait_ge(gap_ready, hf + 1)
                            nc.scalar.activation(e2[:, HT * hf:HT * hf + HT], gap[:, HT * hf:HT * hf + HT], ACT.Exp).then_inc(e2_ready, 1)
                        elif kind == "mix":
                            act.wait_ge(d_arg, hf + 1)
                            t0, t1 = [HB * k * (HB * k + 1) // 2 for k in (hf, hf + 1)]
                            nc.scalar.activation(sc[:, t0:t1, :], sc[:, t0:t1, :], ACT.Exp, scale=float(HD) ** -0.5).then_inc(d_exp, 1)
                        elif kind == "gate1":
                            act.wait_ge(x_done, x_at[f] + 1)
                            if hf:
                                act.wait_ge(x_done, x_at["gate2", 0, 0] + 1)
                            nc.scalar.activation(gl[i][:, :, :].rearrange("p c s -> p (c s)"), xbank(f)[:, :], ACT.Gelu_apprx_tanh)\
                                .then_inc(gl_ready, 1)
                    kind, u, i = step
                    if kind == "mid":
                        if u >= 2:
                            act.wait_ge(out_done, u - 1)
                        for hc in range(FC):
                            n = t_ring_at["mid", u, hc]
                            act.wait_ge(t_ring_done, n + 1)
                            nc.scalar.activation(mid[u % 2][:, hc, :], ring[:, n % RING, :], ACT.Gelu, bias=M_b1[:, u % E, hc:hc + 1])\
                                .then_inc(t_ring_free, 1)
                    elif kind == "gated":
                        n = t_ring_at["gated", u, i, 0]
                        act.wait_ge(t_ring_done, n + 1)
                        nc.scalar.activation(f_a[:, u, i, :], ring[:, n % RING, :], ACT.Silu, scale=col("F_s1", i)).then_inc(silu_ready, 1)
                    elif kind in ("hid1", "hid2"):
                        n = t_ring_at[kind, u, i]
                        dst, s = (f_b, "F_h1") if kind == "hid1" else (f_a, "F_h2")
                        act.wait_ge(t_ring_done, n + 1)
                        nc.scalar.activation(dst[:, u, i, :], ring[:, n % RING, :], ACT.Gelu, scale=col(s, i)).then_inc(t_ring_free, 1)

                for s in range(STEPS):
                    if s - 1 in ssq_at and ssq_at[s - 1][1] == 3:
                        b = ssq_at[s - 1][0]
                        act.wait_ge(o_done, s - TL - 1)
                        nc.scalar.copy(ssn[:, b % 2, :], obank[:, S:S + 8 * PAIRS]).then_inc(ssn_ready, 1)
                    if TL + 2 <= s < NP + TL + 2:
                        g = s - TL - 2
                        bb, q = g // PAIRS, g % PAIRS
                        act.wait_ge(o_done, g + 1)
                        if bb >= 2 and q == 0:
                            act.wait_ge(misc_done, misc_at["out", bb - 2, CB - 1] + 1)
                        if bb < B:
                            nc.scalar.activation(oT[bb % 2][:, q, :], obank[:, 0:S], ACT.Identity, bias=col("A_bv", q)).then_inc(o_free, 1)
                        else:
                            nc.scalar.copy(oT[bb % 2][:, q, :], obank[:, 0:S]).then_inc(o_free, 1)
                    if s < NP:
                        q = s % PAIRS
                        act.wait_ge(misc_done, misc_at["pair", s] + 1)
                        if s >= 2:
                            act.wait_ge(ring_done, ring_at["S", s - 2, 1] + 1)
                        lo, hi = slice(0, A), slice(A, P)
                        if s < B * PAIRS:
                            nc.scalar.activation(qT[s % 2][:, :], misc[:, 0:S], ACT.Identity, bias=col("A_bq", q), scale=-float(A) ** -0.5)
                            nc.scalar.activation(kz[s % 2][lo, 0, :], misc[lo, S:2 * S], ACT.Identity, bias=col("A_bk", q, 0, A))
                            ins = nc.scalar.activation(kz[s % 2][hi, 1, :], misc[hi, S:2 * S], ACT.Identity, bias=col("A_bk", q, A, P))
                        else:
                            nc.scalar.copy(kz[s % 2][lo, 0, :], misc[lo, 0:S])
                            ins = nc.scalar.copy(kz[s % 2][hi, 1, :], misc[hi, 0:S])
                        ins.then_inc(misc_free, 1)
                    for e in misc_extras[s]:
                        if e[0] == "pnT":
                            act.wait_ge(misc_done, misc_at[e] + 1)
                            nc.scalar.copy(pnT[:, :], misc[0:H, 0:S]).then_inc(misc_free, 1)
                    if 1 <= s <= NP:
                        g = s - 1
                        bb, q = g // PAIRS, g % PAIRS
                        i = bb % 2
                        act.wait_ge(max_ready, g + 1)
                        if g >= 4:
                            act.wait_ge(pt_done, CB * (g - 3))
                        if bb >= B:
                            nc.scalar.activation(pn[:, i, q, :, :], pnarg[:, i, q, :, :], ACT.Exp)
                        for c in range(CB):
                            for h in range(2):
                                ins = nc.scalar.activation(
                                    probs[g % 4][:, c, h, :], ring[:, ring_at["S", g, c] % RING, h * S:(h + 1) * S], ACT.Exp,
                                    bias=negmax[:, i, q, c, h:h + 1], scale=-1.0 if bb < B else nrq[:, i, q, c, h:h + 1],
                                    accum_out=sums[:, i, q, c, h:h + 1])
                            ins.then_inc(ring_free, 1)
                    for e in ring_extras[s]:
                        kind, b, r = e
                        src = ring[:, ring_at[e] % RING, :]
                        act.wait_ge(ring_done, ring_at[e] + 1)
                        c, hf = r // 2, r % 2
                        if kind == "V":
                            if b >= 2 and r == 0:
                                act.wait_ge(o_done, PAIRS * (b - 1))
                            nc.scalar.copy(vtok[b % 2][:, c, hf * 512:(hf + 1) * 512], src).then_inc(ring_free, 1)
                        elif kind == "K":
                            if b >= 1 and r == 0:
                                act.wait_ge(ksum_ready, b)
                            if b >= 2 and r == 0:
                                act.wait_ge(misc_done, misc_at["pair", PAIRS * (B + b - 1) - 1] + 1)
                            nc.scalar.activation(ksq[:, c * H + hf * 8:c * H + hf * 8 + 8, :].rearrange("p h a -> p (h a)"), src, ACT.Square)
                            nc.scalar.copy(ktok[b % 2][:, c, hf * 512:(hf + 1) * 512], src).then_inc(ring_free, 1)
                        elif kind == "Q":
                            if b >= 1 and r == 0:
                                act.wait_ge(ssn_ready, b)
                            if b >= 2 and r == 0:
                                act.wait_ge(ring_done, ring_at["S", PAIRS * (B + b - 1) - 1, 1] + 1)
                            a = src.rearrange("p (a s) -> p a s", a=2)
                            nc.scalar.activation(qsq[:, 2 * r:2 * r + 2, :], a, ACT.Square)
                            nc.scalar.activation(qT_all[b % 2][:, 2 * r:2 * r + 2, :], a, ACT.Copy, scale=nqk[:, 0:1]).then_inc(ring_free, 1)
                    if s - C_AT >= FIRST:
                        narrow_step(s - C_AT)
                for s in range(STEPS - C_AT, CSTEPS):
                    narrow_step(s)
                    for step in fill.get(s, []):
                        tail_step(step)
                for step in ORDER[FILLED:]:
                    tail_step(step)

            @block.tensor
            def _(pe):
                def ring_bank(key):
                    n = ring_at[key]
                    if n >= RING:
                        pe.wait_ge(ring_free, n - RING + 1)
                    return ring[:, n % RING, :]

                def misc_bank(key):
                    if misc_at[key]:
                        pe.wait_ge(misc_free, misc_at[key])

                pe.wait_ge(load_first, 48)

                def t_bank(key):
                    n = t_ring_at[key]
                    if n >= RING:
                        pe.wait_ge(t_ring_free, n - RING + 1)
                    else:
                        pe.wait_ge(c_ring_free, TU * NGR)
                    return ring[:, n % RING, :]

                def narrow_step(s):
                    for u, (heads, c) in enumerate(tiles):
                        if 0 <= s < NGR:
                            b, q = s // NG, s % NG
                            if u == 0:
                                for ready in (kz_dve, kz_act, kz_pool):
                                    pe.wait_ge(ready, s + 1)
                            n = TU * s + u
                            if n >= RING:
                                pe.wait_ge(c_ring_free, n - RING + 1)
                            else:
                                pe.wait_ge(ring_free, len(ring_at))
                            nh, nk = len(heads), (c + 1) * P
                            nc.tensor.matmul(ring[:, n % RING, :], qTc[:, b % 2, c * P:(c + 1) * P], kzn[:, s % KR, heads[0]:heads[0] + nh, 0:nk],
                                             start=True, stop=True)
                            nc.tensor.matmul(ring[:, n % RING, :].rearrange("p (h k) -> p h k", h=nh)[:, :, c * P:nk], identb[:, :],
                                             causal[:, :].unsqueeze(1).broadcast_to([P, nh, P]), start=False, stop=True,
                                             skip_group_check=True).then_inc(c_ring_done, 1)
                        if CT <= s < NGR + CT:
                            g = s - CT
                            n = TU * g + u
                            pe.wait_ge(c_ring_free, n + 1)
                            if n >= 2:
                                pe.wait_ge(c_pt_free, n - 1)
                            else:
                                pe.wait_ge(pt_free, CB * NP)
                            for k in range(4):
                                ins = nc.tensor.transpose(ptb[:, n % 2, k * P:(k + 1) * P], pr[:, g % PR, u, k * P:(k + 1) * P], ident[:, :])
                            ins.then_inc(c_pt_done, 1)
                        if u == 0 and CT + 1 < s <= NGR + CT + 1:
                            g = s - CT - 2
                            pe.wait_ge(c_o_free, g + 1)
                            for c in range(CB):
                                ins = nc.tensor.transpose(obank[:, S + c * P:S + (c + 1) * P], oT4[g % 2][:, c * P:(c + 1) * P], ident[:, :])
                            ins.then_inc(c_ot_done, 1)
                    if CT < s <= NGR + CT:
                        g = s - CT - 1
                        b, q = g // NG, g % NG
                        pe.wait_ge(c_pt_free, TU * (g + 1))
                        pe.wait_ge(misc_free, misc_at["V", b] + 1)
                        pe.wait_ge(c_ones, 1)
                        if g >= 1:
                            pe.wait_ge(c_ot_free, g)
                        else:
                            pe.wait_ge(o_free, NP)
                        for kc in range(CB):
                            for j in range(G):
                                ins = nc.tensor.matmul(obank[VW * j:VW * j + VW, kc * P:S], vtn[:, b % 2, kc, G * q + j, :],
                                                       prT[g % 2][:, j, kc, kc * P:S], start=kc == 0, stop=True, skip_group_check=True)
                        ins.then_inc(c_o_done, 1)
                    for e in c_extras[s]:
                        kind, b = e
                        if misc_at[e]:
                            pe.wait_ge(misc_free, misc_at[e])
                        xb = xn_all[:, b * S:(b + 1) * S]
                        if s == FIRST:
                            pe.wait_ge(loadN, 96)
                        if kind == "QK":
                            nc.tensor.matmul(misc[:, 0:S], C_wq[:, :], xb, start=True, stop=True)
                            ins = nc.tensor.matmul(misc[:, S:2 * S], C_wk[:, :], xb, start=True, stop=True)
                        for c in range(CB):
                            xc = xn_all[:, b * S + c * P:b * S + (c + 1) * P]
                            out = misc[:, c * P:(c + 1) * P]
                            if kind == "V":
                                ins = nc.tensor.matmul(out, xc, C_wv[:, :], start=True, stop=True)
                            elif kind == "OT":
                                if c == 0:
                                    pe.wait_ge(c_ot_free, NG * (b + 1))
                                ins = nc.tensor.transpose(out, oN[:, b % 2, c, :], ident[:, :])
                            elif kind == "OUT":
                                if c == 0:
                                    pe.wait_ge(misc_free, misc_at["OT", b] + 1)
                                ins = nc.tensor.matmul(out, oTn[:, b % 2, c * P:(c + 1) * P], C_wp[:, :], start=True, stop=True)
                            elif kind == "X2":
                                if c == 0:
                                    pe.wait_ge(c_xhat, b + 1)
                                ins = nc.tensor.transpose(out, hat[:, CB * b + c, :], ident[:, :])
                            elif kind == "GATE":
                                if c == 0:
                                    pe.wait_ge(misc_free, misc_at["X2", b] + 1)
                                ins = nc.tensor.matmul(misc[:, c * E:(c + 1) * E], xc, M_gw[:, :], start=True, stop=True)
                        ins.then_inc(misc_done, 1)

                def tail_step(step):
                    for f in before[step]:
                        kind, hf, i = f
                        if f not in x_at:
                            continue
                        if x_at[f] >= 2:
                            pe.wait_ge(x_free, x_at[f] - 1)
                        else:
                            pe.wait_ge(c_ot_free, NGR)
                            pe.wait_ge(misc_free, len(misc_at))
                        bank = xbank(f)
                        if kind == "wT":
                            pe.wait_ge(wts_ready, hf + 1)
                            for j in range(HT):
                                ins = nc.tensor.transpose(bank[0:E, j * P:(j + 1) * P], wts[:, HT * hf + j, :], ident[:, :])
                        elif kind == "b2":
                            pe.wait_ge(x_free, x_at["wT", hf, 0] + 1)
                            for j in range(HT):
                                ins = nc.tensor.matmul(bank[:, j * P:(j + 1) * P], wT[:, (HT * hf + j) * P:(HT * hf + j + 1) * P], M_b2[:, :],
                                                       start=True, stop=True)
                        elif kind in ("T_c", "T_d", "T_e"):
                            n = hat_at["ln" + kind[1:], hf, 0]
                            for j in range(HT):
                                pe.wait_ge(t_hat, n + j + 1)
                                ins = nc.tensor.transpose(bank[:, j * P:(j + 1) * P], x_res[:, HT * hf + j, :], ident[:, :])
                        elif kind == "proj":
                            if i == 0:
                                pe.wait_ge(x_free, x_at["T_c", hf, 0] + 1)
                                pe.wait_ge(loadF, 16 * 7)
                            j = HT * hf + i
                            ins = nc.tensor.matmul(bank[:, 0:3 * D], xn_all[:, j * P:(j + 1) * P], D_w[:, :], start=True, stop=True)
                        elif kind == "gate1":
                            b = HB * hf + i
                            pe.wait_ge(x_free, x_at["T_d", hf, 0] + 1)
                            for c in range(CB):
                                ins = nc.tensor.matmul(bank[:, c * S:(c + 1) * S], ctxT[:, b, c * P:(c + 1) * P], xn_all[:, b * S:(b + 1) * S],
                                                       start=True, stop=True)
                        elif kind == "gate2":
                            pe.wait_ge(h_ready, HB * (hf + 1))
                            for k in range(HB):
                                for c in range(CB):
                                    for fc in range(CB):
                                        ins = nc.tensor.matmul(bank[:, (CB * k + c) * P:(CB * k + c + 1) * P], gl[k][:, fc, c * P:(c + 1) * P],
                                                               ctx_tok[:, CB * (HB * hf + k) + fc, :], start=fc == 0, stop=fc == CB - 1)
                        ins.then_inc(x_done, 1)
                    kind, u, i = step
                    if kind == "mid":
                        e, hf = u % E, u // E
                        pe.wait_ge(loadE[e], 48)
                        for hc in range(FC):
                            nc.tensor.matmul(t_bank(("mid", u, hc)), M_w1[:, e, hc * P:(hc + 1) * P], xn_all[:, hf * 512:(hf + 1) * 512],
                                             start=True, stop=True).then_inc(t_ring_done, 1)
                    elif kind == "out":
                        pe.wait_ge(t_ring_free, t_ring_at["mid", u, FC - 1] + 1)
                        if u >= 2:
                            pe.wait_ge(out_free, u - 1)
                        else:
                            pe.wait_ge(c_pt_free, TU * NGR)
                        for tc in range(HT):
                            for hc in range(FC):
                                ins = nc.tensor.matmul(ptb[:, u % 2, tc * P:(tc + 1) * P], mid[u % 2][:, hc, tc * P:(tc + 1) * P],
                                                       M_w2[:, u % E, hc, :], start=hc == 0, stop=hc == FC - 1)
                        ins.then_inc(out_done, 1)
                    elif kind == "gated":
                        hf = u
                        if i == 0:
                            pe.wait_ge(x_free, x_at["T_e", hf, 0] + 1)
                        for w, weights in enumerate((F_w1, F_w2)):
                            nc.tensor.matmul(t_bank(("gated", hf, i, w)), weights[:, i * P:(i + 1) * P], xn_all[:, hf * 512:(hf + 1) * 512],
                                             start=True, stop=True).then_inc(t_ring_done, 1)
                    elif kind in ("hid1", "hid2"):
                        hf = u
                        w, src = (F_h1, f_a) if kind == "hid1" else (F_h2, f_b)
                        bank = t_bank((kind, hf, i))
                        for kc in range(FC):
                            if i == 0:
                                n = t_ring_at["gated", hf, kc, 1] if kind == "hid1" else t_ring_at["hid1", hf, kc]
                                pe.wait_ge(t_ring_free, n + 1)
                            ins = nc.tensor.matmul(bank, w[:, kc, i * P:(i + 1) * P], src[:, hf, kc, :], start=kc == 0, stop=kc == FC - 1)
                        ins.then_inc(t_ring_done, 1)
                    elif kind == "last":
                        hf = u
                        for tc in range(HT):
                            piece = tc // 2
                            if tc % 2 == 0 and hf == 0:
                                pe.wait_ge(out_free, U - 1 + piece)
                            elif tc % 2 == 0:
                                pe.wait_ge(fin_read, piece + 1)
                            for kc in range(FC):
                                if tc == 0:
                                    pe.wait_ge(t_ring_free, t_ring_at["hid2", hf, kc] + 1)
                                ins = nc.tensor.matmul(ptb[:, piece, tc % 2 * P:(tc % 2 + 1) * P], f_a[:, hf, kc, tc * P:(tc + 1) * P],
                                                       F_w3[:, kc, :], start=kc == 0, stop=kc == FC - 1)
                            if tc % 2:
                                ins.then_inc(last_done, 1)

                for s in range(STEPS):
                    if s < NP:
                        bb, q = s // PAIRS, s % PAIRS
                        misc_bank(("pair", s))
                        if s == 2:
                            pe.wait_ge(loadW["A_wq"], 16)
                            pe.wait_ge(loadW["A_wk"], 16)
                        if s == PAIRS - 4:
                            pe.wait_ge(loadX, 16)
                        if bb < B:
                            xb = xTa[:, bb * S:(bb + 1) * S]
                            nc.tensor.matmul(misc[:, 0:S], A_wq[:, q * P:(q + 1) * P], xb, start=True, stop=True)
                            ins = nc.tensor.matmul(misc[:, S:2 * S], A_wk[:, q * P:(q + 1) * P], xb, start=True, stop=True)
                        else:
                            if q == 0:
                                pe.wait_ge(khat_ready, 4 * (bb - B + 1))
                            for c in range(CB):
                                ins = nc.tensor.transpose(misc[:, c * P:(c + 1) * P], ktok[bb % 2][:, c, q * P:(q + 1) * P], ident[:, :])
                        ins.then_inc(misc_done, 1)
                    if 1 <= s <= NP:
                        g = s - 1
                        bb, q = g // PAIRS, g % PAIRS
                        pe.wait_ge(misc_free, misc_at["pair", g] + 1)
                        qs = qT[g % 2][:, :] if bb < B else qT_all[bb % 2][:, q, :]
                        for c in range(CB):
                            nc.tensor.matmul(ring_bank(("S", g, c)), qs[:, c * P:(c + 1) * P], kz[g % 2][:, :, :], start=True,
                                             stop=True).then_inc(ring_done, 1)
                    for e in misc_extras[s]:
                        kind, b, r = e
                        if kind == "pnT":
                            misc_bank(e)
                            pe.wait_ge(pnt_ready, b + 1)
                            for c in range(CB):
                                ins = nc.tensor.transpose(misc[0:H, c * P:(c + 1) * P], pnt[:, c, :], ident[:, :])
                            ins.then_inc(misc_done, 1)
                        elif kind == "out":
                            c = r
                            misc_bank(e)
                            pe.wait_ge(loadW["A_wo" if b < B else "B_wo"], 16)
                            pe.wait_ge(o_free, PAIRS * (b + 1))
                            wo = A_wo if b < B else B_wo
                            for q in range(PAIRS):
                                ins = nc.tensor.matmul(misc[:, 0:D], oT[b % 2][:, q, c * P:(c + 1) * P], wo[:, q, :],
                                                       start=q == 0, stop=q == PAIRS - 1 and b < B)
                            if b >= B:
                                pe.wait_ge(misc_free, misc_at["pnT", b - B, 0] + 1)
                                ins = nc.tensor.matmul(misc[:, 0:D], pnT[:, c * P:(c + 1) * P], nvwo[:, :], start=False, stop=True)
                            ins.then_inc(misc_done, 1)
                        elif kind in ("X", "CX"):
                            misc_bank(e)
                            pe.wait_ge(xhat_ready if kind == "X" else c_hat_ready, b + 1)
                            for c in range(CB):
                                ins = nc.tensor.transpose(misc[:, c * P:(c + 1) * P], xhat[:, c, :], ident[:, :])
                            ins.then_inc(misc_done, 1)
                        elif kind == "C":
                            misc_bank(e)
                            pe.wait_ge(chat, 4 * b + 4)
                            for i in range(4):
                                ins = nc.tensor.transpose(misc[:, i * P:(i + 1) * P], hat[:, 4 * b + i, :], ident[:, :])
                            ins.then_inc(misc_done, 1)
                        elif kind == "NV":
                            misc_bank(e)
                            pe.wait_ge(consts_ready, 3)
                            pe.wait_ge(loadW["B_wo"], 16)
                            for q in range(PAIRS):
                                ins = nc.tensor.matmul(misc[0:H, 0:D], nvz[:, q, :], B_wo[:, q, :], start=q == 0, stop=q == PAIRS - 1)
                            ins.then_inc(misc_done, 1)
                    if TL <= s < NP + TL:
                        g = s - TL
                        pe.wait_ge(norm_done, g + 1)
                        if g == 0:
                            pe.wait_ge(cst, 2)
                        for c in range(CB):
                            if g >= 1:
                                pe.wait_ge(pt_free, CB * (g - 1) + c + 1)
                            for k in range(4):
                                ins = nc.tensor.transpose(ptb[:, c, k * P:(k + 1) * P],
                                                          probs[g % 4][:, c, k // 2, (k % 2) * P:(k % 2 + 1) * P], ident[:, :])
                            ins.then_inc(pt_done, 1)
                    if TL < s <= NP + TL:
                        g = s - TL - 1
                        bb, q = g // PAIRS, g % PAIRS
                        pe.wait_ge(pt_free, CB * (g + 1))
                        pe.wait_ge(ring_free, ring_at["V", bb, 3] + 1)
                        if g >= 1:
                            pe.wait_ge(o_free, g)
                        for kc in range(CB):
                            for h in range(2):
                                ins = nc.tensor.matmul(obank[h * A:(h + 1) * A, 0:S], vtok[bb % 2][:, kc, (2 * q + h) * A:(2 * q + h + 1) * A],
                                                       probsT[g % 2][:, h, kc, :], start=kc == 0, stop=kc == CB - 1)
                        if s in ssq_at:
                            b, r = ssq_at[s]
                            ss = obank[:, S:S + 8 * PAIRS]
                            pe.wait_ge(ring_free, ring_at["Q", b, r] + 1)
                            if r == 0:
                                pe.wait_ge(null_ready, 1)
                                for c in range(CB):
                                    nullc = ss[:, 4 * PAIRS:].rearrange("p (a c h) -> p a c h", c=CB, h=2)[:, :, c, :]
                                    j = b * CB + c
                                    nc.tensor.matmul(nullc, xn_all[:, j * P:(j + 1) * P], wnull[:, :].rearrange("p (a h) -> p a h", h=2),
                                                     start=True, stop=True)
                            for p in (2 * r, 2 * r + 1):
                                for c in range(CB):
                                    o = 4 * p + 2 * c
                                    ins = nc.tensor.matmul(ss[:, o:o + 2], qsq[:, p, c * P:(c + 1) * P], blk[:, :], start=True, stop=True)
                        ins.then_inc(o_done, 1)
                    for e in ring_extras[s]:
                        kind, b, r = e
                        c, hf = r // 2, r % 2
                        if kind == "V":
                            pe.wait_ge(loadW["A_wv" if b < B else "B_wkv"], 16)
                            j = (b % B) * CB + c
                            src = (xTa if b < B else cn_all)[:, j * P:(j + 1) * P]
                            w = A_wv[:, hf * 512:(hf + 1) * 512] if b < B else B_wkv[:, H * A + hf * 512:H * A + (hf + 1) * 512]
                            nc.tensor.matmul(ring_bank(e), src, w, start=True, stop=True).then_inc(ring_done, 1)
                        elif kind == "K":
                            pe.wait_ge(loadW["B_wkv"], 16)
                            j = b * CB + c
                            if b == 0:
                                pe.wait_ge(misc_free, misc_at["C", 1, 0] + 1)
                            nc.tensor.matmul(ring_bank(e), cn_all[:, j * P:(j + 1) * P], B_wkv[:, hf * 512:(hf + 1) * 512], start=True,
                                             stop=True).then_inc(ring_done, 1)
                        elif kind == "Q":
                            pe.wait_ge(loadW["B_wq"], 16)
                            pe.wait_ge(misc_free, misc_at["X", b, 0] + 1)
                            bank = ring_bank(e)
                            for k in range(2):
                                p = 2 * r + k
                                ins = nc.tensor.matmul(bank[:, k * S:(k + 1) * S], B_wq[:, p * P:(p + 1) * P], xn_all[:, b * S:(b + 1) * S],
                                                       start=True, stop=True)
                            ins.then_inc(ring_done, 1)
                    if s - C_AT >= FIRST:
                        narrow_step(s - C_AT)
                for s in range(STEPS - C_AT, CSTEPS):
                    narrow_step(s)
                    for step in fill.get(s, []):
                        tail_step(step)
                for step in ORDER[FILLED:]:
                    tail_step(step)

            @block.vector
            def _(dve):
                ch = Chain(dve, wide_dve)
                dve.wait_ge(loadC, 16)
                nc.vector.tensor_scalar(cols[:, 0:PAIRS], cols[:, 0:PAIRS], -float(A) ** -0.5, None, ALU.mult).then_inc(consts_ready, 1)
                for i in range(2):
                    ins = nc.vector.memset(kz[i][:, :, :], 0.0)
                ins.then_inc(consts_ready, 1)
                ch.step(nc.vector.memset(blk[:, :], 0.0))
                nc.vector.memset(blk[0:A, 0:1], 1.0)
                nc.vector.memset(blk[A:P, 1:2], 1.0)

                lns = [0]

                def ln_begin(src):
                    i = lns[0] % 2
                    for c in range(CB):
                        ins = nc.vector.bn_stats(lst[:, c, :], src[:, c, :])
                    ch.step(ins)
                    for c in range(CB):
                        ins = nc.vector.bn_aggr(lmv[:, i, c, :], lst[:, c, :])
                    ins.then_inc(var_ready, 1)
                    lns[0] += 1

                c_ch = Chain(dve, c_dve_steps)
                t_ch = Chain(dve, t_dve)

                def gate(hf):
                    js = slice(HT * hf, HT * hf + HT)
                    for j in range(HT * hf, HT * hf + HT):
                        ins = nc.vector.max(top[:, j, :], logits[:, j, :])
                    t_ch.step(ins)
                    nc.vector.tensor_tensor(gap[:, js], top[:, js, 1], top[:, js, 0], ALU.subtract).then_inc(gap_ready, 1)
                    for j in range(HT * hf, HT * hf + HT):
                        ins = nc.vector.max_index(topi[:, j, :], top[:, j, :], logits[:, j, :])
                    t_ch.step(ins)
                    t_ch.step(nc.vector.tensor_copy(topf[:, js, :], topi[:, js, 0:2]))
                    dve.wait_ge(e2_ready, hf + 1)
                    t_ch.step(nc.vector.tensor_scalar(wa[:, js, 0], e2[:, js], 1.0, None, ALU.add))
                    t_ch.step(nc.vector.reciprocal(w01[:, js, 0], wa[:, js, 0]))
                    t_ch.step(nc.vector.tensor_tensor(w01[:, js, 1], w01[:, js, 0], e2[:, js], ALU.mult))
                    dve.wait_ge(iot_ready, 2)
                    for k, dst in enumerate([wa, wb]):
                        t_ch.step(nc.vector.tensor_tensor(dst[:, js, :], iof[:, :].unsqueeze(1).broadcast_to([P, HT, E]),
                                                        topf[:, js, k:k + 1].broadcast_to([P, HT, E]), ALU.is_equal))
                        t_ch.step(nc.vector.tensor_tensor(dst[:, js, :], dst[:, js, :], w01[:, js, k:k + 1].broadcast_to([P, HT, E]), ALU.mult))
                    nc.vector.tensor_tensor(wts[:, js, :], wa[:, js, :], wb[:, js, :], ALU.add).then_inc(wts_ready, 1)
                    dve.wait_ge(wts_ready, hf + 1)

                def half_begin(f):
                    for j in ln_chunks(f):
                        ins = nc.vector.bn_stats(st[:, j, :], x_res[:, j, :])
                    t_ch.step(ins)
                    for j in ln_chunks(f):
                        ins = nc.vector.bn_aggr(mv[:, j, :], st[:, j, :])
                    ins.then_inc(t_var, 1)

                def half_end(f):
                    dve.wait_ge(t_rstd, ln_at["ln" + f[0][2:], f[1], f[2]] + 1)
                    for j in ln_chunks(f):
                        nc.vector.tensor_scalar(x_res[:, j, :], x_res[:, j, :], mv[:, j, 0:1], rstd[:, j:j + 1], ALU.subtract, ALU.mult)\
                            .then_inc(t_hat, 1)

                def scores(hf):
                    for i in range(HB * hf, HB * hf + HB):
                        t0 = i * (i + 1) // 2
                        s3 = sc[:, t0:t0 + i + 1, :]
                        q = qkv[:, i, :, 0:D].unsqueeze(1).broadcast_to([P, i + 1, CB, D])
                        t_ch.step(nc.vector.tensor_tensor(prod[:, 0:i + 1, :, :], qkv[:, 0:i + 1, :, D:2 * D], q, ALU.mult))
                        t_ch.step(nc.vector.tensor_reduce(s3, prod[:, 0:i + 1, :, :].rearrange("p j c (h d) -> p j (c h) d", d=HD), AX.X, ALU.add))
                        t_ch.step(nc.vector.tensor_reduce(smax[:, i, :], s3.rearrange("p j x -> p x j"), AX.X, ALU.max))
                        ins = nc.vector.tensor_tensor(s3, s3, smax[:, i, :].unsqueeze(1).broadcast_to([P, i + 1, CB * H]), ALU.subtract)
                    ins.then_inc(d_arg, 1)

                def mix(hf):
                    dve.wait_ge(d_exp, hf + 1)
                    i0, i1 = HB * hf, HB * hf + HB
                    for i in range(i0, i1):
                        t0 = i * (i + 1) // 2
                        ins = nc.vector.tensor_reduce(ssum[:, i, :], sc[:, t0:t0 + i + 1, :].rearrange("p j x -> p x j"), AX.X, ALU.add)
                    t_ch.step(ins)
                    ss = ssum[:, i0:i1, :]
                    t_ch.step(nc.vector.tensor_scalar(ss, ss, 1.0, None, ALU.add))
                    t_ch.step(nc.vector.reciprocal(ss, ss))
                    for i in range(i0, i1):
                        t0 = i * (i + 1) // 2
                        for c in range(CB):
                            pb = sc[:, t0:t0 + i + 1, c * H:(c + 1) * H].unsqueeze(3).broadcast_to([P, i + 1, H, HD])
                            ins = nc.vector.tensor_tensor(prod[:, 0:i + 1, c, :].rearrange("p j (h d) -> p j h d", d=HD),
                                                          qkv[:, 0:i + 1, c, 2 * D:3 * D].rearrange("p j (h d) -> p j h d", d=HD), pb, ALU.mult)
                        t_ch.step(ins)
                        t_ch.step(nc.vector.tensor_reduce(att[:, i, :], prod[:, 0:i + 1, :, :].rearrange("p j c d -> p (c d) j"), AX.X, ALU.add))
                    a3 = att[:, i0:i1, :].rearrange("p i (x d) -> p (i x) d", d=HD)
                    t_ch.step(nc.vector.tensor_tensor(a3, a3, ss.rearrange("p i x -> p (i x)").unsqueeze(2).broadcast_to([P, HB * CB * H, HD]),
                                                    ALU.mult))
                    xh = x_res[:, HT * hf:HT * hf + HT, :]
                    t_ch.step(nc.vector.tensor_tensor(xh, att[:, i0:i1, :].rearrange("p i (c d) -> p (i c) d", c=CB), xh, ALU.add))

                def narrow_step(s):
                    if -1 <= s < NGR - 1:
                        g = s + 1
                        b, h = g // NG, G * (g % NG)
                        dve.wait_ge(misc_free, misc_at["QK", b] + 1)
                        if g >= KR:
                            dve.wait_ge(c_ring_done, TU * (g - KR + 1))
                        nc.vector.tensor_scalar(kzn[:, g % KR, 0, :], kTc[:, b % 2, :], hmask[:, h:h + 1], None, ALU.mult)\
                            .then_inc(kz_dve, 1)
                    for u, (heads, c) in enumerate(tiles):
                        if 0 <= s < NGR:
                            n = TU * s + u
                            dve.wait_ge(c_ring_done, n + 1)
                            nc.vector.tensor_reduce(nmax[:, s, stat_of[u]:stat_of[u] + len(heads)],
                                                    ring[:, n % RING, :].rearrange("p (h k) -> p h k", h=len(heads)), AX.X, ALU.min)\
                                .then_inc(c_max, 1)
                        if CT <= s < NGR + CT:
                            g = s - CT
                            if g >= 2 and u == 0:
                                dve.wait_ge(c_o_done, g - 1)
                            n = TU * g + u
                            dve.wait_ge(c_pt_done, n + 1)
                            src = ptb[:, n % 2, :].rearrange("p (h q) -> p h q", q=P)
                            if c == 0:
                                dst = prT[g % 2][:, :, 0, 0:P]
                            else:
                                dst = prT[g % 2][:, heads[0]:heads[0] + 2, :, P:S].rearrange("p h k q -> p (h k) q")
                            nc.vector.tensor_copy(dst, src).then_inc(c_pt_free, 1)
                        if u == 0 and CT + 1 < s <= NGR + CT + 1:
                            g = s - CT - 2
                            b, q = g // NG, g % NG
                            prod4 = obank[:, S:2 * S].rearrange("p (c h v) -> p c h v", c=CB, v=VW)
                            rs = nrs[:, g, :].rearrange("p (c h) -> p c h", c=CB)
                            dve.wait_ge(c_ot_done, g + 1)
                            c_ch.step(nc.vector.reciprocal(rs, prod4[:, :, :, HD]))
                            if b >= 2 and q == 0:
                                dve.wait_ge(misc_done, misc_at["OT", b - 2] + 1)
                            nc.vector.tensor_tensor(oN[:, b % 2, :, G * q * HD:G * (q + 1) * HD].rearrange("p c (h d) -> p c h d", d=HD),
                                                    prod4[:, :, :, 0:HD], rs.unsqueeze(3).broadcast_to([P, CB, G, HD]), ALU.mult)\
                                .then_inc(c_ot_free, 1)
                    for kind, b in c_dve[s]:
                        dve.wait_ge(c_rstd, b + 1)
                        for c in range(CB):
                            ins = nc.vector.tensor_scalar(hat[:, CB * b + c, :], x1[:, b % 2, c, :], lmv2[:, b, c, 0:1], lrs2[:, b, c:c + 1],
                                                          ALU.subtract, ALU.mult)
                        ins.then_inc(c_xhat, 1)
                    for e in c_extras[s]:
                        kind, b = e
                        if kind in ("OUT", "X2", "GATE"):
                            dve.wait_ge(misc_done, misc_at[e] + 1)
                        xb = x_res[:, CB * b:CB * b + CB, :]
                        if kind == "OUT":
                            nc.vector.tensor_tensor(y[:, :, :], misc[:, 0:CB * D].rearrange("p (c d) -> p c d", c=CB),
                                                    rowb("C_bp", CB), ALU.add).then_inc(misc_free, 1)
                            dve.wait_ge(misc_free, misc_at[e] + 1)
                            c_ch.step(nc.vector.tensor_tensor(x1[:, b % 2, :, :], y[:, :, :], xb, ALU.add))
                            nc.vector.tensor_tensor(xb, x1[:, b % 2, :, :], xb, ALU.add)
                            for c in range(CB):
                                ins = nc.vector.bn_stats(st[:, c, :], x1[:, b % 2, c, :])
                            c_ch.step(ins)
                            for c in range(CB):
                                ins = nc.vector.bn_aggr(lmv2[:, b, c, :], st[:, c, :])
                            ins.then_inc(c_var, 1)
                        elif kind == "X2":
                            nc.vector.tensor_scalar(xn_all[:, b * S:(b + 1) * S], misc[:, 0:S], col("C_ln2_g"), col("C_ln2_b"), ALU.mult,
                                                    ALU.add).then_inc(misc_free, 1)
                        elif kind == "GATE":
                            nc.vector.tensor_tensor(logits[:, CB * b:CB * b + CB, :], misc[:, 0:CB * E].rearrange("p (c e) -> p c e", c=CB),
                                                    rowb("M_gb", CB), ALU.add).then_inc(misc_free, 1)

                def tail_step(step):
                    for f in before[step]:
                        kind, hf, i = f
                        xh = x_res[:, HT * hf:HT * hf + HT, :]
                        if f in x_at:
                            if kind == "gate1":
                                dve.wait_ge(gl_ready, HB * hf + i + 1)
                            else:
                                dve.wait_ge(x_done, x_at[f] + 1)
                            bank = xbank(f)
                            tok = bank[:, :].rearrange("p (j d) -> p j d", d=D)
                            if kind == "wT":
                                ins = nc.vector.tensor_copy(wT[:, hf * 512:(hf + 1) * 512], bank[0:E, :])
                            elif kind in ("T_c", "T_d", "T_e"):
                                ins = nc.vector.tensor_copy(xn_all[:, hf * 512:(hf + 1) * 512], bank[:, :])
                            elif kind in ("b2", "gate2"):
                                ins = nc.vector.tensor_tensor(xh, tok, xh, ALU.add)
                            elif kind == "proj":
                                j = HT * hf + i
                                ins = nc.vector.tensor_tensor(qkv[:, j // CB, j % CB, :], bank[:, 0:3 * D], row("D_b"), ALU.add)
                            elif kind == "gate1":
                                g = gl[i][:, :, :].rearrange("p c s -> p (c s)")
                                ins = nc.vector.tensor_tensor(g, g, bank[:, :], ALU.mult)
                            ins.then_inc(x_free, 1)
                            if kind == "gate1":
                                dve.wait_ge(x_free, x_at[f] + 1)
                                dve.sem_inc(h_ready, 1)
                            if kind in ("gate2", "b2", "proj"):
                                dve.wait_ge(x_free, x_at[f] + 1)
                        elif kind == "gate":
                            gate(hf)
                        elif f in ln_at:
                            half_begin(f)
                        elif kind.startswith("le_"):
                            half_end(f)
                        elif kind == "fin":
                            js = slice(HT * hf + 2 * i, HT * hf + 2 * i + 2)
                            dve.wait_ge(last_done, 2 * hf + i + 1)
                            nc.vector.tensor_tensor(hat[:, js, :], ptb[:, i, 0:2 * D].rearrange("p (j d) -> p j d", d=D), rowb("F_s3", 2), ALU.mult)\
                                .then_inc(fin_read, 1)
                            dve.wait_ge(fin_read, 2 * hf + i + 1)
                            t_ch.step(nc.vector.tensor_tensor(x_res[:, js, :], hat[:, js, :], x_res[:, js, :], ALU.add))
                        elif kind == "score":
                            scores(hf)
                        elif kind == "mix":
                            mix(hf)
                    kind, u, i = step
                    if kind == "out":
                        hf = u // E
                        dve.wait_ge(out_done, u + 1)
                        for tc in range(HT):
                            j = HT * hf + tc
                            ins = nc.vector.scalar_tensor_tensor(x_res[:, j, :], ptb[:, u % 2, tc * P:(tc + 1) * P],
                                                                 wts[:, j, u % E:u % E + 1], x_res[:, j, :], ALU.mult, ALU.add)
                        ins.then_inc(out_free, 1)
                        dve.wait_ge(out_free, u + 1)
                    elif kind == "gated":
                        n = t_ring_at["gated", u, i, 1]
                        dve.wait_ge(silu_ready, FC * u + i + 1)
                        dve.wait_ge(t_ring_done, n + 1)
                        a = f_a[:, u, i, :]
                        nc.vector.scalar_tensor_tensor(a, ring[:, n % RING, :], col("F_s2", i), a, ALU.mult, ALU.mult).then_inc(t_ring_free, 2)

                for s in range(STEPS):
                    if TL < s <= NP + TL:
                        g = s - TL - 1
                        if g >= 2:
                            dve.wait_ge(o_done, g - 1)
                        for c in range(CB):
                            dve.wait_ge(pt_done, CB * g + c + 1)
                            nc.vector.tensor_copy(probsT[g % 2][:, :, :, c * P:(c + 1) * P].rearrange("p h k q -> p (h k) q"),
                                                  ptb[:, c, :].rearrange("p (k q) -> p k q", q=P)).then_inc(pt_free, 1)
                    norm, top_ = 2 <= s <= NP + 1, 1 <= s <= NP
                    if norm:
                        g = s - 2
                        bb, q = g // PAIRS, g % PAIRS
                        i = bb % 2
                        dve.wait_ge(ring_free, ring_at["S", g, CB - 1] + 1)
                        if bb >= B:
                            summed = ch.mark(nc.vector.tensor_tensor(sums[:, i, q, :, :], sums[:, i, q, :, :], pn[:, i, q, :, :], ALU.add))
                        else:
                            inverted = ch.mark(nc.vector.reciprocal(rsum[:, i, q, :, :], sums[:, i, q, :, :]))
                    if top_:
                        g1 = s - 1
                        b1, q1 = g1 // PAIRS, g1 % PAIRS
                        i1 = b1 % 2
                        dve.wait_ge(ring_done, ring_at["S", g1, CB - 1] + 1)
                        r = ring_at["S", g1, 0] % RING
                        dst = negmax if b1 < B else mins
                        if r + CB <= RING:
                            ins = nc.vector.tensor_reduce(dst[:, i1, q1, :, :], ring[:, r:r + CB, :].rearrange("p c (h k) -> p c h k", h=2), AX.X, ALU.min)
                        else:
                            for c in range(CB):
                                r = ring_at["S", g1, c] % RING
                                ins = nc.vector.tensor_reduce(dst[:, i1, q1, c, :], ring[:, r, :].rearrange("p (h k) -> p h k", h=2), AX.X, ALU.min)
                        if b1 < B:
                            ins.then_inc(max_ready, 1)
                        else:
                            reduced = ch.mark(ins)
                    if norm and bb >= B:
                        ch.after(summed)
                        inverted = ch.mark(nc.vector.reciprocal(rsum[:, i, q, :, :], sums[:, i, q, :, :]))

                    def normalise(k):
                        if norm:
                            a = probs[g % 4][:, k // 2, k % 2, :]
                            ins = nc.vector.tensor_scalar(a, a, rsum[:, i, q, k // 2, k % 2:k % 2 + 1], None, ALU.mult)
                            if k == 3:
                                ins.then_inc(norm_done, 1)

                    if top_ and b1 >= B:
                        if q1 == 0:
                            dve.wait_ge(rq_ready, b1 - B + 1)
                        m = mins[:, i1, q1, :, :]
                        ch.after(reduced)
                        limited = ch.mark(nc.vector.tensor_tensor(m, m, nulls(b1 - B, q1), ALU.min))
                        if norm:
                            ch.after(inverted)
                        normalise(0)
                        ch.after(limited)
                        scaled = ch.mark(nc.vector.tensor_tensor(negmax[:, i1, q1, :, :], m, prq[:, i1, q1, :, :], ALU.mult))
                        normalise(1)
                        ch.after(scaled)
                        nc.vector.tensor_tensor(pnarg[:, i1, q1, :, :], negmax[:, i1, q1, :, :], snr[:, i1, q1, :, :], ALU.add).then_inc(max_ready, 1)
                    else:
                        if norm:
                            ch.after(inverted)
                        normalise(0)
                        normalise(1)
                    normalise(2)
                    normalise(3)
                    for e in misc_extras[s]:
                        kind, b, r = e
                        if kind == "out":
                            dve.wait_ge(misc_done, misc_at[e] + 1)
                            if b == 0:
                                dve.wait_ge(bo_added, 1)
                            if b < B:
                                nc.vector.tensor_tensor(y[:, r, :], misc[:, 0:D], x_res[:, CB * b + r, :], ALU.add).then_inc(misc_free, 1)
                            else:
                                nc.vector.tensor_copy(y[:, r, :], misc[:, 0:D]).then_inc(misc_free, 1)
                            if r == CB - 1:
                                dve.wait_ge(misc_free, misc_at[e] + 1)
                                ln_begin(y)
                        elif kind in ("X", "CX"):
                            gain, bias = ("B_in_g", "B_in_b") if kind == "X" else ("C_ln1_g", "C_ln1_b")
                            dve.wait_ge(misc_done, misc_at[e] + 1)
                            nc.vector.tensor_scalar(xn_all[:, b * S:(b + 1) * S], misc[:, 0:S], col(gain), col(bias), ALU.mult,
                                                    ALU.add).then_inc(misc_free, 1)
                        elif kind == "C":
                            dve.wait_ge(misc_done, misc_at[e] + 1)
                            nc.vector.tensor_scalar(cn_all[:, b * 512:(b + 1) * 512], misc[:, :], col("B_ctx_g"), col("B_ctx_b"), ALU.mult,
                                                    ALU.add).then_inc(misc_free, 1)
                        elif kind == "NV":
                            dve.wait_ge(misc_done, misc_at[e] + 1)
                            nc.vector.tensor_copy(nvwo[:, :], misc[0:H, 0:D]).then_inc(misc_free, 1)
                    for e in dve_extras[s]:
                        kind, b = e
                        xb = x_res[:, CB * (b % B):CB * (b % B) + CB, :]
                        if kind == "ctx_norm":
                            dve.wait_ge(loadA, 48)
                            ln_stats(ch, lambda i: ctx_tok[:, i, :], NC).then_inc(cstat, 1)
                        elif kind == "null_value":
                            ch.step(nc.vector.memset(nvz[:, :, :], 0.0))
                            flat = nvz[:, :, :].rearrange("p a h -> p (a h)")
                            n = (PAIRS - 1) * (H + 2) + 1
                            nc.vector.tensor_copy(flat[0:A, 0:n:H + 2], col("B_nv", 0, 0, A).broadcast_to([A, PAIRS]))
                            nc.vector.tensor_copy(flat[A:P, 1:1 + n:H + 2], col("B_nv", 0, A, P).broadcast_to([A, PAIRS])).then_inc(consts_ready, 1)
                            nc.vector.tensor_scalar(col("C_bq"), col("C_bq"), -float(HD) ** -0.5, None, ALU.mult)
                            nc.vector.scalar_tensor_tensor(nqk[:, :], col("B_qs"), -1.0, col("B_ks"), ALU.mult, ALU.mult)
                        elif kind == "null_key":
                            ch.step(nc.vector.tensor_tensor(nkr[:, :], row("B_nk"), row("B_nk"), ALU.mult))
                            ch.step(nc.vector.tensor_reduce(nks[:, :], nkr[:, :], AX.X, ALU.add))
                            nc.vector.tensor_scalar(nks[:, :], nks[:, :], NORM_EPS ** 2, None, ALU.max).then_inc(null_ss, 1)
                            dve.wait_ge(null_pow, 1)
                            dve.wait_ge(loadW["B_wq"], 16)
                            ch.step(nc.vector.tensor_scalar(nkr[:, :], row("B_nk"), nks[:, 0:1], -1.0, ALU.mult, ALU.mult))
                            ch.step(nc.vector.tensor_tensor(nkr[:, :], nkr[:, :], row("B_qsr"), ALU.mult))
                            ch.step(nc.vector.tensor_tensor(nkr[:, :], nkr[:, :], row("B_ksr"), ALU.mult))
                            ch.step(nc.vector.tensor_tensor(wtmp, B_wq[:, :].rearrange("p (h a) -> p h a", a=A),
                                                            nkr[:, :].unsqueeze(1).broadcast_to([P, H, A]), ALU.mult))
                            nc.vector.tensor_reduce(wnull[:, :], wtmp, AX.X, ALU.add).then_inc(null_ready, 1)
                        elif kind == "ksum":
                            dve.wait_ge(ring_free, ring_at["K", b, 3] + 1)
                            ch.step(nc.vector.tensor_reduce(kss[:, :], ksq[:, :, :], AX.X, ALU.add))
                            nc.vector.tensor_scalar(kss[:, :], kss[:, :], NORM_EPS ** 2, None, ALU.max).then_inc(ksum_ready, 1)
                        elif kind == "qsum":
                            dve.wait_ge(ssn_ready, b + 1)
                            nc.vector.tensor_scalar(rqt[:, :], ssn[:, b % 2, 0:4 * PAIRS], NORM_EPS ** 2, None, ALU.max).then_inc(qsum_ready, 1)
                        elif kind == "pnt":
                            nc.vector.tensor_tensor(pnt[:, :, :].rearrange("p c (a h) -> p a c h", h=2), pn[:, b % 2, :, :, :],
                                                    rsum[:, b % 2, :, :, :], ALU.mult).then_inc(pnt_ready, 1)
                        elif kind == "norm2":
                            dve.wait_ge(normed, B + B_LNS * b + 1)
                            ln_begin(y)
                        elif kind == "xnorm":
                            dve.wait_ge(normed, b + 1)
                            ln_begin(xb)
                        elif kind == "cnorm":
                            dve.wait_ge(normed, B + B_LNS * b + 2)
                            ln_begin(xb)
                    if s - C_AT >= FIRST:
                        narrow_step(s - C_AT)
                for s in range(STEPS - C_AT, CSTEPS):
                    narrow_step(s)
                    for step in fill.get(s, []):
                        tail_step(step)
                for step in ORDER[FILLED:]:
                    tail_step(step)

            @block.gpsimd
            def _(pool):
                nc.gpsimd.memset(ident[:, :], 0.0).then_inc(cst, 1)
                pool.wait_ge(cst, 1)
                nc.gpsimd.affine_select(out=ident[:, :], in_=ident[:, :], compare_op=ALU.not_equal, fill=1.0,
                                        base=0, pattern=[[-1, P]], channel_multiplier=1).then_inc(cst, 1)
                for k, value in enumerate(CONSTS):
                    nc.gpsimd.memset(const[:, k, :], value).then_inc(cst, 1)
                pool.wait_ge(cst, 2 + len(CONSTS))
                ch = Chain(pool, wide_pool)
                pool.wait_ge(loadA, 48)
                nc.gpsimd.tensor_tensor(x_res[:, :, :], x_res[:, :, :], rowb("A_bo", NC), ALU.add).then_inc(bo_added, 1)
                pool.wait_ge(cstat, 1)
                ch.step(ln_power(ch, NC))
                for i in range(NC):
                    nc.gpsimd.tensor_scalar(hat[:, i, :], ctx_tok[:, i, :], mv[:, i, 0:1], rstd[:, i:i + 1], ALU.subtract, ALU.mult)\
                        .then_inc(chat, 1)
                pool.wait_ge(null_ss, 1)
                nc.gpsimd.tensor_tensor(nks[:, :], nks[:, :], half[:, 0:1], ALU.pow).then_inc(null_pow, 1)
                ch.step(nc.gpsimd.memset(hmask[:, :], 1.0))
                ch.step(nc.gpsimd.affine_select(out=hmask[:, :], in_=hmask[:, :], compare_op=ALU.is_ge, fill=0.0,
                                                base=0, pattern=[[-HD, H]], channel_multiplier=1))
                nc.gpsimd.affine_select(out=hmask[:, :], in_=hmask[:, :], compare_op=ALU.is_ge, fill=0.0,
                                        base=HD - 1, pattern=[[HD, H]], channel_multiplier=-1)
                ch.step(nc.gpsimd.memset(causal[:, :], 0.0))
                nc.gpsimd.affine_select(out=causal[:, :], in_=causal[:, :], compare_op=ALU.is_ge, fill=MASKED,
                                        base=0, pattern=[[-1, P]], channel_multiplier=1)
                nc.gpsimd.tensor_copy(identb[:, :], ident[:, :])
                lns = 0
                c_ch = Chain(pool, c_pool_steps)
                nc.gpsimd.iota(iot[:, :], [[1, E]], 0, 0).then_inc(iot_ready, 1)
                pool.wait_ge(iot_ready, 1)
                nc.gpsimd.tensor_copy(iof[:, :], iot[:, :]).then_inc(iot_ready, 1)
                t_ch = Chain(pool, t_pool)

                def narrow_step(s):
                    if s == FIRST:
                        c_ch.step(nc.gpsimd.memset(vtn[:, :, :, :, HD:], 0.0))
                        nc.gpsimd.memset(vtn[:, :, :, :, HD], 1.0).then_inc(c_ones, 1)
                    if -1 <= s < NGR - 1:
                        g = s + 1
                        b, h = g // NG, G * (g % NG) + 1
                        pool.wait_ge(misc_free, misc_at["QK", b] + 1)
                        if g >= KR:
                            pool.wait_ge(c_ring_done, TU * (g - KR + 1))
                        nc.gpsimd.tensor_tensor(kzn[:, g % KR, 1:3, :], kTc[:, b % 2, :].unsqueeze(1).broadcast_to([P, 2, S]),
                                                hmask[:, h:h + 2].unsqueeze(2).broadcast_to([P, 2, S]), ALU.mult).then_inc(kz_pool, 1)
                    for kind, b in c_extras[s]:
                        if kind == "OUT":
                            pool.wait_ge(c_var, b + 1)
                            c_ch.step(nc.gpsimd.tensor_tensor(lve2[:, b, :], lmv2[:, b, :, 1], const[:, 1, 0:CB], ALU.add))
                            nc.gpsimd.tensor_tensor(lrs2[:, b, :], lve2[:, b, :], half[:, 0:CB], ALU.pow).then_inc(c_rstd, 1)

                def tail_step(step):
                    for f in before[step]:
                        if f in ln_at:
                            j, n = ln_chunks(f)[0], len(ln_chunks(f))
                            pool.wait_ge(t_var, ln_at[f] + 1)
                            t_ch.step(nc.gpsimd.tensor_tensor(veps[:, j:j + n], mv[:, j:j + n, 1], const[:, 1, 0:n], ALU.add))
                            nc.gpsimd.tensor_tensor(rstd[:, j:j + n], veps[:, j:j + n], half[:, 0:n], ALU.pow).then_inc(t_rstd, 1)

                for s in range(STEPS):
                    for kind, b, r in misc_extras[s]:
                        if kind == "out" and r == CB - 1:
                            xb = x_res[:, CB * (b % B):CB * (b % B) + CB, :]
                            if b < B:
                                pool_ln(pool, ch, lns, xb, y).then_inc(normed, 1)
                            else:
                                ch.step(pool_ln(pool, ch, lns, y2, y))
                                ch.step(nc.gpsimd.tensor_tensor(y2[:, :, :], y2[:, :, :], rowb("B_out_g", CB), ALU.mult))
                                ch.step(nc.gpsimd.tensor_tensor(y2[:, :, :], y2[:, :, :], rowb("B_out_b", CB), ALU.add))
                                nc.gpsimd.tensor_tensor(y[:, :, :], y2[:, :, :], xb, ALU.add).then_inc(normed, 1)
                            lns += 1
                    for kind, b in dve_extras[s]:
                        if kind == "ksum":
                            pool.wait_ge(ksum_ready, b + 1)
                            ch.step(nc.gpsimd.tensor_tensor(krn[:, :], kss[:, :], half[:, 0:CB * H], ALU.pow))
                        elif kind == "qsum":
                            def flat(x):
                                return x[:, b % 2, :, :, :].rearrange("p a c h -> p (a c h)")
                            pool.wait_ge(qsum_ready, b + 1)
                            ch.step(nc.gpsimd.tensor_tensor(rqt[:, :], rqt[:, :], half[:, 0:4 * PAIRS], ALU.pow))
                            nc.gpsimd.tensor_tensor(flat(prq), rqt[:, :], const[:, 2, 0:4 * PAIRS], ALU.mult)
                            ch.step(nc.gpsimd.tensor_tensor(flat(nrq), rqt[:, :], const[:, 3, 0:4 * PAIRS], ALU.mult))
                            nc.gpsimd.tensor_tensor(flat(snr), flat(nrq), ssn[:, b % 2, 4 * PAIRS:], ALU.mult).then_inc(rq_ready, 1)
                        if kind in ("xnorm", "cnorm", "norm2"):
                            xb = x_res[:, CB * (b % B):CB * (b % B) + CB, :]
                            if kind == "norm2":
                                pool_ln(pool, ch, lns, xb, y).then_inc(normed, 1)
                            else:
                                pool_ln(pool, ch, lns, xhat, xb).then_inc(xhat_ready if kind == "xnorm" else c_hat_ready, 1)
                            lns += 1
                    for kind, b, r in pool_extras[s]:
                        n = CB * H // 4
                        k3 = ktok[b % 2][:, :, :].rearrange("p c (h a) -> p (c h) a", a=A)[:, n * r:n * r + n, :]
                        nc.gpsimd.tensor_tensor(k3, k3, krn[:, n * r:n * r + n].unsqueeze(2).broadcast_to([P, n, A]), ALU.mult)\
                            .then_inc(khat_ready, 1)
                    if s - C_AT >= FIRST:
                        narrow_step(s - C_AT)
                for s in range(STEPS - C_AT, CSTEPS):
                    narrow_step(s)
                    for step in fill.get(s, []):
                        tail_step(step)
                for step in ORDER[FILLED:]:
                    tail_step(step)


def layout(i):
    import numpy as np

    i = {k: np.asarray(v) for k, v in i.items()}
    a = {}
    a["x"] = i["x"].reshape(B * S, D)
    a["xT"] = i["x"].transpose(0, 2, 1)
    a["ctx"] = i["ctx_1024"].reshape(B * S, D)
    a["ctxT"] = i["ctx_1024"].transpose(0, 2, 1)
    for k in ("q", "k", "v", "o"):
        a["A_w" + k] = i["L0_attn_W" + k]
    a["B_wq"], a["B_wkv"], a["B_wo"] = i["L0_xattn_Wq"], i["L0_xattn_Wkv"], i["L0_xattn_Wo"]
    for k in ("q", "k", "v"):
        a["C_w" + k] = i["L0_ffn_W" + k]
    a["C_wp"] = i["L0_ffn_Wp"]
    a["M_gw"] = i["L0_ffn_gate_W"]
    a["M_w1"], a["M_b2"] = i["L0_ffn_exp_W1"], i["L0_ffn_exp_b2"]
    a["M_b1"] = i["L0_ffn_exp_b1"].reshape(E, FC, P).transpose(0, 2, 1)
    a["M_w2"] = i["L0_ffn_exp_W2"].reshape(E, FC, P, D).transpose(0, 2, 1, 3)
    a["D_w"] = np.concatenate([i[f"L1_attn_W{k}"].T for k in "qkv"], axis=1)
    a["F_w1"], a["F_w2"] = i["L1_ffn_w1_w"].T, i["L1_ffn_w2_w"].T
    for k in ("h1", "h2", "w3"):
        w = i[f"L1_ffn_{k}_w"].T
        a["F_" + k] = w.reshape(FC, P, w.shape[1]).transpose(1, 0, 2)
    two = lambda v: np.concatenate([v, v])
    c = {
        "A_bq": i["L0_attn_bq"].reshape(PAIRS, P).T, "A_bk": i["L0_attn_bk"].reshape(PAIRS, P).T,
        "A_bv": i["L0_attn_bv"].reshape(PAIRS, P).T, "B_qs": two(i["L0_xattn_q_scale"]), "B_ks": two(i["L0_xattn_k_scale"]),
        "B_nv": two(i["L0_xattn_null_kv"][1]),
        "B_in_g": i["L0_xattn_ln_in_g"], "B_in_b": i["L0_xattn_ln_in_b"], "B_ctx_g": i["L0_xattn_ln_ctx_g"],
        "B_ctx_b": i["L0_xattn_ln_ctx_b"], "C_ln1_g": i["L0_ffn_ln1_g"], "C_ln1_b": i["L0_ffn_ln1_b"],
        "C_ln2_g": i["L0_ffn_ln2_g"], "C_ln2_b": i["L0_ffn_ln2_b"], "C_bq": i["L0_ffn_bq"], "C_bk": i["L0_ffn_bk"],
        "C_bv": i["L0_ffn_bv"],
        "F_s1": i["L1_ffn_w1_s"].reshape(FC, P).T, "F_s2": i["L1_ffn_w2_s"].reshape(FC, P).T,
        "F_h1": i["L1_ffn_h1_s"].reshape(FC, P).T, "F_h2": i["L1_ffn_h2_s"].reshape(FC, P).T,
    }
    a["cols"] = np.concatenate([np.reshape(c[n], (P, w)) for n, (_, w) in COLS.items()], axis=1)
    r = {"A_bo": i["L0_attn_bo"], "B_out_g": i["L0_xattn_ln_out_g"], "B_out_b": i["L0_xattn_ln_out_b"],
         "B_nk": i["L0_xattn_null_kv"][0], "B_qsr": i["L0_xattn_q_scale"], "B_ksr": i["L0_xattn_k_scale"], "C_bp": i["L0_ffn_bp"], "M_gb": i["L0_ffn_gate_b"],
         "D_b": np.concatenate([i[f"L1_attn_b{k}"] for k in "qkv"]), "F_s3": i["L1_ffn_w3_s"]}
    a["rows"] = np.concatenate([r[n] for n in ROWS])
    return {k: np.ascontiguousarray(v) for k, v in a.items()}


def kernel(**inputs):
    import numpy as _np
    import concourse.bacc as _bacc
    from concourse import mybir as _mybir
    from concourse.bass_utils import run_bass_kernel_spmd as _run

    nc = _bacc.Bacc("TRN2", target_bir_lowering=False, num_devices=1)
    arrays, t = {}, {}
    for name, a in layout(inputs).items():
        arrays[f"in_{name}_dram"] = a
        t[name] = nc.dram_tensor(f"in_{name}_dram", a.shape, _mybir.dt.from_np(a.dtype), kind="ExternalInput").ap()
    t["out"] = nc.dram_tensor("out_0_dram", (B * S, D), _mybir.dt.float32, kind="ExternalOutput").ap()
    decoder(nc, t)
    r = _run(nc, [arrays], core_ids=[0])
    return _np.asarray(r.results[0]["out_0_dram"]).reshape(B, S, D)
```
